# Optimizing a Trainium2 kernel written in Bass

```python
import numpy as np
import jax
import jax.numpy as jnp

def _softmax(x, axis=-1):
    return jax.nn.softmax(x, axis=axis)

def _gelu(x):
    return jax.nn.gelu(x, approximate=True)

def _silu(x):
    return jax.nn.silu(x)

def _sigmoid(x):
    return jax.nn.sigmoid(x)

def _layernorm(x, axis=-1, eps=1e-05):
    m = jnp.mean(x, axis=axis, keepdims=True)
    v = jnp.var(x, axis=axis, keepdims=True)
    return (x - m) / jnp.sqrt(v + eps)

def _scatter_add(tgt, idx, src, axis=0):
    return tgt.at[idx].add(src)

def _segment_sum(src, seg, n):
    return jax.ops.segment_sum(src, seg, n)
kernel_name = 'mk_macaron_d1_jaxref_r8_1dba58'

def setup_inputs(seed: int=0):
    np.random.seed(seed)
    _w = jnp.asarray

    def _L0_attn_setup():
        import jax, jax.numpy as jnp
        import numpy as np
        B, T, D, H = (4, 256, 128, 16)
        HD = D // H

        def l2_norm(x, eps=1e-12):
            return x / jnp.maximum(jnp.linalg.norm(x, axis=-1, keepdims=True), eps)
        key = jax.random.key(seed)
        ks = jax.random.split(key, 11)
        std = 0.02
        w = lambda k, shape: jax.random.normal(k, shape, jnp.float32) * std
        return dict(x=jax.random.normal(ks[0], (B, T, D), jnp.float32), Wq=w(ks[1], (D, D)), Wk=w(ks[2], (D, D)), Wv=w(ks[3], (D, D)), Wgamma=w(ks[4], (D, H)), Wf1=w(ks[5], (D, HD)), Wf2=w(ks[6], (HD, D)), Wog1=w(ks[7], (D, HD)), Wog2=w(ks[8], (HD, D)), norm_w=jnp.ones((D,), jnp.float32), Wo=w(ks[9], (D, D)))
    _L0_attn_in = _L0_attn_setup()

    def _L0_ffn_setup():
        import jax, jax.numpy as jnp
        import numpy as np
        NUM_EXPERTS = 8
        TOP_K = 2
        CAPACITY_FACTOR = 1.0

        def _dispatch_compute(xf, top_expert, w1, w2, capacity):
            tokens, hs = xf.shape
            tpe = jnp.bincount(top_expert, length=NUM_EXPERTS)
            indices = jnp.argsort(top_expert)
            offsets = jnp.concatenate([jnp.zeros((1,), tpe.dtype), jnp.cumsum(tpe)[:-1]])
            slot = jnp.arange(capacity)
            pos = offsets[:, None] + slot[None, :]
            valid = slot[None, :] < tpe[:, None]
            tok_idx = indices[jnp.minimum(pos, tokens - 1)]
            xe = jnp.where(valid[..., None], xf[tok_idx], 0.0)
            h = jax.nn.gelu(jnp.einsum('ech,ehf->ecf', xe, w1), approximate=True)
            ye = jnp.einsum('ecf,efh->ech', h, w2)
            tok_safe = jnp.where(valid, tok_idx, tokens)
            out = jnp.zeros((tokens + 1, hs), xf.dtype).at[tok_safe.reshape(-1)].add(ye.reshape(-1, hs))
            return out[:tokens]
        key = jax.random.key(seed)
        k1, k2, k3, k4 = jax.random.split(key, 4)
        hs, ffn = (128, 512)
        x = jax.random.normal(k1, (256, 2, hs), dtype=jnp.float32)
        router_w = jax.random.normal(k2, (hs, NUM_EXPERTS), dtype=jnp.float32) * hs ** (-0.5)
        w1 = jax.random.normal(k3, (NUM_EXPERTS, hs, ffn), dtype=jnp.float32) * 0.02
        w2 = jax.random.normal(k4, (NUM_EXPERTS, ffn, hs), dtype=jnp.float32) * 0.02
        bias = jnp.zeros((1, 1, hs), dtype=jnp.float32)
        return {'x': x, 'router_w': router_w, 'w1': w1, 'w2': w2, 'bias': bias}
    _L0_ffn_in = _L0_ffn_setup()
    _d = {'L0_attn_x': _L0_attn_in['x'], 'L0_attn_Wq': _L0_attn_in['Wq'], 'L0_attn_Wk': _L0_attn_in['Wk'], 'L0_attn_Wv': _L0_attn_in['Wv'], 'L0_attn_Wgamma': _L0_attn_in['Wgamma'], 'L0_attn_Wf1': _L0_attn_in['Wf1'], 'L0_attn_Wf2': _L0_attn_in['Wf2'], 'L0_attn_Wog1': _L0_attn_in['Wog1'], 'L0_attn_Wog2': _L0_attn_in['Wog2'], 'L0_attn_norm_w': _L0_attn_in['norm_w'], 'L0_attn_Wo': _L0_attn_in['Wo'], 'L0_ffn_router_w': _L0_ffn_in['router_w'], 'L0_ffn_w1': _L0_ffn_in['w1'], 'L0_ffn_w2': _L0_ffn_in['w2'], 'L0_ffn_bias': _L0_ffn_in['bias']}
    _x0 = _d['L0_attn_x']
    _d['L0_attn_x'] = jax.random.normal(jax.random.fold_in(jax.random.key(seed), 1), (8, 512, 128), dtype=_x0.dtype)
    del _x0
    return _d

def reference(L0_attn_x, L0_attn_Wq, L0_attn_Wk, L0_attn_Wv, L0_attn_Wgamma, L0_attn_Wf1, L0_attn_Wf2, L0_attn_Wog1, L0_attn_Wog2, L0_attn_norm_w, L0_attn_Wo, L0_ffn_router_w, L0_ffn_w1, L0_ffn_w2, L0_ffn_bias):

    def _L0_attn_ref(x, Wq, Wk, Wv, Wgamma, Wf1, Wf2, Wog1, Wog2, norm_w, Wo):
        import jax, jax.numpy as jnp
        import numpy as np
        B, T, D, H = (4, 256, 128, 16)
        HD = D // H

        def l2_norm(x, eps=1e-12):
            return x / jnp.maximum(jnp.linalg.norm(x, axis=-1, keepdims=True), eps)
        b, n, d = x.shape
        q = jax.nn.silu(x @ Wq)
        k = jax.nn.silu(x @ Wk)
        v = x @ Wv
        log_f = jax.nn.log_sigmoid(x @ Wf1 @ Wf2)
        gamma = -jax.nn.sigmoid(x @ Wgamma)
        q = q.reshape(b, n, H, HD)
        k = l2_norm(k.reshape(b, n, H, HD))
        v = v.reshape(b, n, H, HD)
        gk = log_f.reshape(b, n, H, HD)
        a = k * gamma[..., None] * jnp.exp(gk)

        def step(S, inp):
            qt, kt, vt, at, gkt = inp
            S = S * jnp.exp(gkt)[..., None]
            sab = jnp.einsum('bhk,bhkv->bhv', at, S)
            S = S + kt[..., None] * (sab[..., None, :] + vt[..., None, :])
            ot = jnp.einsum('bhk,bhkv->bhv', qt, S)
            return (S, ot)
        seq = tuple((jnp.moveaxis(t, 1, 0) for t in (q, k, v, a, gk)))
        S0 = jnp.zeros((b, H, HD, HD), x.dtype)
        _, o = jax.lax.scan(step, S0, seq)
        o = jnp.moveaxis(o, 0, 1).reshape(b, n, d)
        o = o * jax.nn.sigmoid(x @ Wog1 @ Wog2)
        mu = o.mean(-1, keepdims=True)
        var = ((o - mu) ** 2).mean(-1, keepdims=True)
        o = (o - mu) * jax.lax.rsqrt(var + 1e-05) * norm_w
        return o @ Wo

    def _L0_ffn_ref(x, router_w, w1, w2, bias):
        import jax, jax.numpy as jnp
        import numpy as np
        NUM_EXPERTS = 8
        TOP_K = 2
        CAPACITY_FACTOR = 1.0

        def _dispatch_compute(xf, top_expert, w1, w2, capacity):
            tokens, hs = xf.shape
            tpe = jnp.bincount(top_expert, length=NUM_EXPERTS)
            indices = jnp.argsort(top_expert)
            offsets = jnp.concatenate([jnp.zeros((1,), tpe.dtype), jnp.cumsum(tpe)[:-1]])
            slot = jnp.arange(capacity)
            pos = offsets[:, None] + slot[None, :]
            valid = slot[None, :] < tpe[:, None]
            tok_idx = indices[jnp.minimum(pos, tokens - 1)]
            xe = jnp.where(valid[..., None], xf[tok_idx], 0.0)
            h = jax.nn.gelu(jnp.einsum('ech,ehf->ecf', xe, w1), approximate=True)
            ye = jnp.einsum('ecf,efh->ech', h, w2)
            tok_safe = jnp.where(valid, tok_idx, tokens)
            out = jnp.zeros((tokens + 1, hs), xf.dtype).at[tok_safe.reshape(-1)].add(ye.reshape(-1, hs))
            return out[:tokens]
        sl, bs, hs = x.shape
        tokens = sl * bs
        capacity = int(CAPACITY_FACTOR * tokens / NUM_EXPERTS)
        xf = x.reshape(tokens, hs)
        scores = jax.nn.softmax(xf @ router_w, axis=-1)
        expert_weights, top_experts = jax.lax.top_k(scores, TOP_K)
        out = jnp.zeros_like(xf)
        for k in range(TOP_K):
            y = _dispatch_compute(xf, top_experts[:, k].astype(jnp.int32), w1, w2, capacity)
            out = out + y * expert_weights[:, k][:, None]
        return out.reshape(sl, bs, hs) + bias
    x = L0_attn_x
    x = x + 0.5 * _L0_ffn_ref(_layernorm(x, axis=-1), L0_ffn_router_w, L0_ffn_w1, L0_ffn_w2, L0_ffn_bias)
    x = x + _L0_attn_ref(_layernorm(x, axis=-1), L0_attn_Wq, L0_attn_Wk, L0_attn_Wv, L0_attn_Wgamma, L0_attn_Wf1, L0_attn_Wf2, L0_attn_Wog1, L0_attn_Wog2, L0_attn_norm_w, L0_attn_Wo)
    x = x + 0.5 * _L0_ffn_ref(_layernorm(x, axis=-1), L0_ffn_router_w, L0_ffn_w1, L0_ffn_w2, L0_ffn_bias)
    return x

_drawn_inputs = setup_inputs


def setup_inputs(seed=0):
    import zlib

    import numpy as np

    out = dict(_drawn_inputs(seed))
    spreads = {'L0_attn_norm_w': (1.0, 0.2), 'L0_ffn_bias': (0.0, 0.1)}
    factors = {'L0_attn_Wgamma': 8.0,
     'L0_attn_Wf1': 8.0,
     'L0_attn_Wf2': 8.0,
     'L0_attn_Wog1': 8.0,
     'L0_attn_Wog2': 8.0,
     'L0_ffn_router_w': 2.799}
    for name, (base, spread) in spreads.items():
        noise = np.random.default_rng([zlib.crc32(name.encode()), seed]).standard_normal(out[name].shape)
        drawn = base * np.exp(spread * noise) if base else spread * noise
        out[name] = jnp.asarray(drawn.astype(out[name].dtype))
    for name, factor in factors.items():
        out[name] = (out[name] * factor).astype(out[name].dtype)
    return out
```

```python
from contextlib import ExitStack

import numpy as np
import concourse.bass as bass
from concourse import mybir
from concourse.alu_op_type import AluOpType as ALU

F32 = mybir.dt.float32
BF16 = mybir.dt.bfloat16
U32 = mybir.dt.uint32
ACT = mybir.ActivationFunctionType
AX = mybir.AxisListType.X

P = 128
D = 128
NB = 8
NT = 512
H, HD = 16, 8
T = NB * NT
NTILE = T // P
NG = NTILE // 4
E = 8
FF = 512
NF = FF // P
CAP = T // E
NJ = CAP // P
RANKS = 2
NBLK = E * NJ
NRUN = RANKS * E
EMPTY = 1 << 20

_off = 0
COL = {}
for _name, _n in (("ident", 128), ("headsum", 128), ("tri", 128), ("ones", 128), ("iota", 128),
                  ("tile", 32), ("tieorder", 8), ("expert", 8), ("segment", 512), ("part", 1), ("delta", 8),
                  ("collect", 1024)):
    COL[_name] = (_off, _off + _n)
    _off += _n
NCONST = _off


def constant_table():
    t = np.zeros((P, NCONST), np.float32)

    def put(name, a):
        lo, hi = COL[name]
        t[:, lo:hi] = np.broadcast_to(a, (P, hi - lo))
    p = np.arange(P)
    put("ident", np.eye(P))
    put("headsum", p[:, None] // HD == p[None, :] // HD)
    put("tri", p[:, None] < p[None, :])
    put("ones", 1.0)
    put("iota", p[None, :])
    put("tile", np.arange(32)[None, :])
    put("tieorder", 8.0 - np.arange(8)[None, :])
    put("expert", np.arange(8)[None, :])
    put("segment", (np.arange(512) % 32 != 0)[None, :])
    put("part", p[:, None])
    put("delta", p[:, None] % HD == np.arange(HD)[None, :])
    same = p[:, None] // HD == p[None, :] // HD
    put("collect", np.concatenate([same & (p[None, :] % HD == v) for v in range(HD)], 1))
    return t


class Chain:

    def __init__(self, eng, sem):
        self.eng, self.sem, self.base, self.n = eng, sem, 0, 0

    def begin(self, base):
        self.base, self.n = base, 0

    def __call__(self, ins):
        self.n += 1
        ins.then_inc(self.sem, 1)
        self.eng.wait_ge(self.sem, self.base + self.n)



class Shared:
    pass


def load_phase(nc, g, x_in, consts):
    with ExitStack() as ctx:
        loaded = ctx.enter_context(nc.semaphore("inputs_loaded"))
        zeroed = ctx.enter_context(nc.semaphore("zero_tile_made"))
        cleared = ctx.enter_context(nc.semaphore("expert_rows_cleared"))
        copied = ctx.enter_context(nc.semaphore("bf16_constants_made"))
        block = ctx.enter_context(nc.Block(no_gpsimd_drain=True))

        @block.sync
        def _(sp):
            for q in range(4):
                sp.dma_start(g.x[:, 8 * q:8 * q + 8, :],
                             x_in[8 * q * P:(8 * q + 8) * P, :].rearrange("(n p) d -> p n d", p=P)).then_inc(loaded, 16)
            sp.dma_start(g.const[:, :], consts[:, :]).then_inc(loaded, 16)
            sp.dma_start(g.router[:, :], g.router_in[:, :]).then_inc(loaded, 16)
            sp.dma_start(g.bias[:, :], g.bias_in.rearrange("a b d -> (a b) d").broadcast_to([P, D])).then_inc(loaded, 16)
            sp.wait_ge(zeroed, 1)
            for q in range(8):
                rows = RANKS * T // 8
                sp.dma_start(g.y_dram[q * rows:(q + 1) * rows, :].rearrange("(p n) d -> p (n d)", p=P),
                             g.xe[:, :, :, :].rearrange("p a j d -> p (a j d)")).then_inc(cleared, 16)
            sp.wait_ge(loaded, 7 * 16)
            sp.wait_ge(cleared, 8 * 16)

        @block.vector
        def _(dve):
            nc.vector.memset(g.xe[:, :, :, :], 0.0).then_inc(zeroed, 1)
            dve.wait_ge(loaded, 7 * 16)
            for src, dst in (("tri", g.tri), ("ones", g.ones)):
                nc.vector.tensor_copy(dst[:, :], g.c(src)).then_inc(copied, 1)
            nc.vector.tensor_scalar(g.bias[:, :], g.bias[:, :], 0.5, None, ALU.mult).then_inc(copied, 1)
            dve.wait_ge(copied, 3)


def norm_phase(nc, g, name, route):
    with ExitStack() as ctx:
        def sb(n, shape, dt=F32):
            return ctx.enter_context(nc.sbuf_tensor(f"{name}_{n}", shape, dt))

        def sem(n):
            return ctx.enter_context(nc.semaphore(f"{name}_{n}"))

        stats = sb("stats", [P, NTILE, 6])
        w = sb("stat_work", [P, 8, NTILE])
        mean, dmean, m2, var, root, quot, scale = (w[:, i, :] for i in range(7))
        rows = sb("rows", [P, 2, 4, D])
        cols = sb("cols", [P, 2, 4 * P]) if route else None
        psT = [ctx.enter_context(nc.psum_tensor(f"{name}_psT{u}", [P, 4, P], F32)) for u in range(2)]

        step = sem("vector_step")
        var_ready = sem("variance_ready")
        root_ready = sem("root_ready")
        rows_ready = sem("rows_normalised")
        transposed = sem("rows_transposed")
        cols_ready = sem("columns_copied")
        scored = sem("logits_done")
        stored = [sem(f"rows_stored{u}") for u in range(2)]
        block = ctx.enter_context(nc.Block(no_gpsimd_drain=True))

        @block.vector
        def _(dve):
            link = Chain(dve, step)
            with dve.Fori(0, NG) as i:
                for j in range(4):
                    ins = nc.vector.bn_stats(stats[:, bass.ds(i * 4 + j, 1), :], g.x[:, bass.ds(i * 4 + j, 1), :])
                ins.then_inc(step, 1)
            dve.wait_ge(step, NG)
            link.begin(NG)
            rsqrt_of_stats(nc, dve, link, stats, w, var_ready, root_ready)

            def normalise(i, u, first):
                if not first:
                    dve.wait_ge(transposed, 2 * i + u - 1)
                    if route:
                        dve.wait_ge(stored[u], 16 * i)
                for j in range(4):
                    t = 8 * i + 4 * u + j
                    ins = nc.vector.tensor_scalar(rows[:, u, j, :], g.x[:, bass.ds(t, 1), :],
                                                  mean[:, bass.ds(t, 1)], scale[:, bass.ds(t, 1)],
                                                  ALU.subtract, ALU.mult)
                ins.then_inc(rows_ready, 1)
            for u in range(2):
                normalise(0, u, True)
            with dve.Fori(1, NG // 2) as i:
                for u in range(2):
                    normalise(i, u, False)

        @block.tensor
        def _(pe):
            def transposes(i, u, first):
                pe.wait_ge(rows_ready, 2 * i + u + 1)
                if not first:
                    pe.wait_ge(cols_ready, 2 * i + u - 1)
                for j in range(4):
                    ins = nc.tensor.transpose(psT[u][:, j, :], rows[:, u, j, :], g.c("ident"))
                ins.then_inc(transposed, 1)

            def logits(i, u):
                pe.wait_ge(cols_ready, 2 * i + u + 1)
                for j in range(4):
                    ins = nc.tensor.matmul(g.logits[:, bass.ds(8 * i + 4 * u + j, 1), :],
                                           cols[:, u, j * P:(j + 1) * P], g.router[:, :], start=True, stop=True)
                ins.then_inc(scored, 1)

            def body(i, first):
                transposes(i, 0, first)
                transposes(i, 1, first)
                if route:
                    logits(i, 0)
                    logits(i, 1)
            body(0, True)
            with pe.Fori(1, NG // 2) as i:
                body(i, False)

        @block.scalar
        def _(act):
            act.wait_ge(var_ready, 1)
            nc.scalar.activation(root, var, ACT.Sqrt).then_inc(root_ready, 1)

            def copies(i, u, first):
                act.wait_ge(transposed, 2 * i + u + 1)
                if route:
                    if not first:
                        act.wait_ge(scored, 2 * i + u - 1)
                    dst = cols[:, u, :]
                else:
                    dst = g.xnT[:, bass.ds(i * 2 + u, 1), :]
                nc.scalar.activation(dst, psT[u][:, :, :].rearrange("p j q -> p (j q)"), ACT.Copy).then_inc(cols_ready, 1)
            for u in range(2):
                copies(0, u, True)
            with act.Fori(1, NG // 2) as i:
                for u in range(2):
                    copies(i, u, False)

        if route:
            @block.sync
            def _(sp):
                with sp.Fori(0, NG // 2) as i:
                    for u in range(2):
                        sp.wait_ge(rows_ready, 2 * i + u + 1)
                        sp.dma_start(g.xn_dram[bass.ds((2 * i + u) * 4, 4), :, :].rearrange("n p d -> p n d"),
                                     rows[:, u, :, :]).then_inc(stored[u], 16)
                for u in range(2):
                    sp.wait_ge(stored[u], 16 * (NG // 2))


def route_phase(nc, g, name):
    with ExitStack() as ctx:
        def sb(n, shape, dt=F32):
            return ctx.enter_context(nc.sbuf_tensor(f"{name}_{n}", shape, dt))

        def ps(n, shape):
            return ctx.enter_context(nc.psum_tensor(f"{name}_{n}", shape, F32))

        def sem(n):
            return ctx.enter_context(nc.semaphore(f"{name}_{n}"))

        scores = sb("scores", [P, NTILE, E])
        work = sb("work", [P, NTILE, E])
        row = sb("row", [P, NTILE])
        best = sb("best", [P, RANKS, NTILE])
        choice = sb("choice", [P, RANKS, NTILE, E])
        choice_bf = sb("choice_bf", [P, RANKS, NTILE, E], BF16)
        before = sb("before", [P, RANKS, E, NTILE])
        place = sb("place", [P, RANKS, NTILE, E])
        pos = sb("pos", [P, RANKS, NTILE])
        hi = sb("hi", [P, RANKS, NTILE])
        lo = sb("lo", [P, RANKS, NTILE])
        low = sb("low_onehot", [P, RANKS, NTILE, P], BF16)
        high = sb("high_onehot", [P, RANKS, NTILE, 3, NBLK], BF16)
        found = sb("found", [P, 3, NBLK])
        ps_rank = ps("ps_rank", [P, RANKS, NTILE, E])
        ps_total = ps("ps_total", [P, RANKS, NTILE, E])
        ps_found = [ps(f"ps_found{k}", [P, 3 * NBLK]) for k in range(RANKS)]

        step = sem("vector_step")
        shifted = sem("logits_shifted")
        raised = sem("exponentials_ready")
        chosen = sem("choices_ready")
        counted = sem("counts_ready")
        onehot = sem("onehots_ready")
        listed = sem("slot_tokens_ready")
        block = ctx.enter_context(nc.Block(no_gpsimd_drain=True))

        def over_experts(a):
            return a.broadcast_to([P, NTILE, E]) if a.shape[1] == NTILE else a

        @block.vector
        def _(dve):
            V = nc.vector
            link = Chain(dve, step)
            each = [P, NTILE, E]

            def wide(a):
                return a.rearrange("p (t o) -> p t o", o=1).broadcast_to(each)

            def ramp(n):
                return g.c(n).rearrange("p (o e) -> p o e", o=1).broadcast_to(each)
            link(V.tensor_reduce(row[:, :], g.logits[:, :, :], AX, ALU.max))
            V.tensor_tensor(scores[:, :, :], g.logits[:, :, :], wide(row[:, :]), ALU.subtract).then_inc(shifted, 1)
            dve.wait_ge(raised, 1)
            link(V.tensor_reduce(row[:, :], work[:, :, :], AX, ALU.add))
            link(V.reciprocal(row[:, :], row[:, :]))
            link(V.tensor_tensor(scores[:, :, :], work[:, :, :], wide(row[:, :]), ALU.mult))
            for k in range(RANKS):
                link(V.tensor_reduce(best[:, k, :], scores[:, :, :], AX, ALU.max))
                link(V.tensor_tensor(work[:, :, :], scores[:, :, :], wide(best[:, k, :]), ALU.is_equal))
                link(V.tensor_tensor(work[:, :, :], work[:, :, :], ramp("tieorder"), ALU.mult))
                link(V.tensor_reduce(row[:, :], work[:, :, :], AX, ALU.max))
                link(V.tensor_tensor(choice[:, k], work[:, :, :], wide(row[:, :]), ALU.is_equal))
                if k == 0:
                    link(V.scalar_tensor_tensor(scores[:, :, :], choice[:, k], -4.0, scores[:, :, :], ALU.mult, ALU.add))
            V.tensor_copy(choice_bf[:, :, :, :], choice[:, :, :, :]).then_inc(chosen, 1)
            V.memset(before[:, :, :, 0:1], 0.0)
            dve.wait_ge(counted, 1)
            for k in range(RANKS):
                ins = V.tensor_copy(before[:, k, :, 1:NTILE], ps_total[:, k, 0:NTILE - 1, :].rearrange("p t e -> p e t"))
            link(ins)
            flat = before[:, :, :, :].rearrange("p k e t -> p (k e t)")
            link(V.tensor_tensor_scan(flat, g.c("segment"), flat, 0.0, ALU.mult, ALU.add))
            for k in range(RANKS):
                ins = V.tensor_tensor(place[:, k], ps_rank[:, k], before[:, k].rearrange("p e t -> p t e"), ALU.add)
            link(ins)
            link(V.tensor_tensor(place[:, :, :, :], place[:, :, :, :], choice[:, :, :, :], ALU.mult))
            link(V.tensor_reduce(pos[:, :, :], place[:, :, :, :], AX, ALU.add))
            for k in range(RANKS):
                ins = V.tensor_tensor(place[:, k], choice[:, k], ramp("expert"), ALU.mult)
            link(ins)
            link(V.tensor_reduce(hi[:, :, :], place[:, :, :, :], AX, ALU.add))
            link(V.tensor_scalar(lo[:, :, :], pos[:, :, :], float(CAP), 0.5, ALU.is_lt, ALU.mult))
            link(V.tensor_tensor(g.weight[:, :, :], best[:, :, :], lo[:, :, :], ALU.mult))
            link(V.tensor_scalar(lo[:, :, :], pos[:, :, :], float(P), None, ALU.is_ge))
            for m in range(2, NJ):
                link(V.scalar_tensor_tensor(lo[:, :, :], pos[:, :, :], float(m * P), lo[:, :, :], ALU.is_ge, ALU.add))
            link(V.scalar_tensor_tensor(hi[:, :, :], hi[:, :, :], float(NJ), lo[:, :, :], ALU.mult, ALU.add))
            link(V.scalar_tensor_tensor(lo[:, :, :], lo[:, :, :], -float(P), pos[:, :, :], ALU.mult, ALU.add))
            for k in range(RANKS):
                shape = [P, NTILE, P]
                V.tensor_tensor(low[:, k], g.c("iota").rearrange("p (o q) -> p o q", o=1).broadcast_to(shape),
                                lo[:, k].rearrange("p (t o) -> p t o", o=1).broadcast_to(shape), ALU.is_equal)
                shape = [P, NTILE, NBLK]
                link(V.tensor_tensor(high[:, k, :, 0, :],
                                     g.c("tile").rearrange("p (o q) -> p o q", o=1).broadcast_to(shape),
                                     hi[:, k].rearrange("p (t o) -> p t o", o=1).broadcast_to(shape), ALU.is_equal))
                V.tensor_tensor(high[:, k, :, 1, :], high[:, k, :, 0, :],
                                g.c("tile").rearrange("p (t o) -> p t o", o=1).broadcast_to(shape), ALU.mult)
                V.tensor_scalar(high[:, k, :, 2, :], high[:, k, :, 0, :], g.c("part"), None, ALU.mult).then_inc(onehot, 1)
            for k in range(RANKS):
                dve.wait_ge(listed, k + 1)
                link(V.tensor_copy(found[:, :, :].rearrange("p c h -> p (c h)"), ps_found[k][:, :]))
                link(V.scalar_tensor_tensor(found[:, 1], found[:, 1], float(P), found[:, 2], ALU.mult, ALU.add))
                link(V.scalar_tensor_tensor(found[:, 0], found[:, 0], -float(EMPTY), found[:, 1], ALU.mult, ALU.add))
                V.tensor_scalar(g.take[:, k * NBLK:(k + 1) * NBLK], found[:, 0], float(EMPTY), None, ALU.add)
                link(V.tensor_scalar(g.put[:, k * NBLK:(k + 1) * NBLK], found[:, 0], float(EMPTY + k * T), None, ALU.add))

        @block.scalar
        def _(act):
            act.wait_ge(shifted, 1)
            nc.scalar.activation(work[:, :, :], scores[:, :, :], ACT.Exp).then_inc(raised, 1)

        @block.tensor
        def _(pe):
            pe.wait_ge(chosen, 1)
            c = choice_bf[:, :, :, :].rearrange("p k t e -> p (k t e)")
            nc.tensor.matmul(ps_rank[:, :, :, :].rearrange("p k t e -> p (k t e)"), g.tri[:, :], c, start=True, stop=True)
            nc.tensor.matmul(ps_total[:, :, :, :].rearrange("p k t e -> p (k t e)"), g.ones[:, :], c,
                             start=True, stop=True).then_inc(counted, 1)
            for k in range(RANKS):
                pe.wait_ge(onehot, k + 1)

                def add(t, start=False, stop=False):
                    return nc.tensor.matmul(ps_found[k][:, :], low[:, k, bass.ds(t, 1), :],
                                            high[:, k, bass.ds(t, 1), :, :].rearrange("p o c h -> p (o c h)"),
                                            start=start, stop=stop)
                add(0, start=True)
                with pe.Fori(0, 6) as i:
                    for j in range(5):
                        add(5 * i + j + 1)
                add(NTILE - 1, stop=True).then_inc(listed, 1)


def expert_phase(nc, g, name, w1, w2):
    with ExitStack() as ctx:
        def sb(n, shape, dt=F32):
            return ctx.enter_context(nc.sbuf_tensor(f"{name}_{n}", shape, dt))

        def ps(n, shape):
            return ctx.enter_context(nc.psum_tensor(f"{name}_{n}", shape, F32))

        def sem(n):
            return ctx.enter_context(nc.semaphore(f"{name}_{n}"))

        w1s = sb("w1", [P, 2, FF])
        w2s = sb("w2", [P, 2, NF, D])
        xT = sb("xT", [P, 2, CAP])
        hT = sb("hT", [P, 2, NF, CAP])
        yT = sb("yT", [P, CAP])
        y = sb("y", [P, 2, NJ, D])
        take = sb("take_now", [P, 2, NJ], U32)
        put = sb("put_now", [P, 2, NJ], U32)
        ps_in = ps("ps_in", [P, CAP])
        ps_h = [ps(f"ps_h{f}", [P, CAP]) for f in range(NF)]
        ps_yT = ps("ps_yT", [P, CAP])
        ps_y = ps("ps_y", [P, NJ, D])

        w_loaded = [sem(f"weights_loaded{u}") for u in range(2)]
        gathered = [sem(f"rows_gathered{u}") for u in range(2)]
        scattered = [sem(f"rows_scattered{u}") for u in range(2)]
        indexed = sem("indices_ready")
        in_done = sem("rows_transposed")
        xT_ready = sem("xT_ready")
        up_done = sem("up_done")
        h_ready = sem("h_ready")
        down_done = sem("down_done")
        yT_ready = sem("yT_ready")
        out_done = sem("y_transposed")
        y_ready = sem("y_ready")
        passed = sem("waits_passed")
        block = ctx.enter_context(nc.Block())

        def stages(eng, emit):
            for i in range(-2, 3):
                emit(i, i % 2, 0, static=i)
            with eng.Fori(0, 5) as m:
                for u in range(2):
                    emit(2 * m + 3 + u, (1 + u) % 2, m, static=None)
            for i in range(13, NRUN + 1):
                emit(i, i % 2, 0, static=i)

        def runs(static, shift):
            return static is None or 0 <= static + shift < NRUN


        @block.sync
        def _(sp):
            def load(r, u, first):
                e = r % E if isinstance(r, int) else r & (E - 1)
                if not first:
                    sp.wait_ge(down_done, r - 1)
                    sp.sem_inc(passed, 1)
                sp.dma_start(w1s[:, u, :], w1[bass.ds(e, 1), :, :].rearrange("o c f -> c (o f)")).then_inc(w_loaded[u], 16)
                sp.dma_start(w2s[:, u, :, :], w2[bass.ds(e, 1), :, :].rearrange("o (b f) c -> f (o b) c", b=NF)).then_inc(w_loaded[u], 16)
            for r in (0, 1):
                load(r, r, True)
            with sp.Fori(1, NRUN // 2) as m:
                for u in range(2):
                    load(2 * m + u, u, False)

        @block.gpsimd
        def _(pool):
            def gather(r, u, static):
                if static is None or static + 3 >= 2:
                    pool.wait_ge(in_done, r - 1)
                nc.gpsimd.tensor_copy(take[:, u, :], g.take[:, bass.ds(r * NJ, NJ)]).then_inc(indexed, 1)
                pool.wait_ge(indexed, take_count(r, static))
                pool.sem_inc(passed, 1)
                for j in range(NJ):
                    nc.gpsimd.indirect_dma_start(out=g.xe[:, u, j, :], out_offset=None, in_=g.xn_rows,
                                                 in_offset=bass.IndirectOffsetOnAxis(ap=take[:, u, j:j + 1], axis=0),
                                                 bounds_check=T - 1, oob_is_err=False).then_inc(gathered[u], 16)

            def take_count(r, static):
                return r + 1 + (max(r - 4, 0) if isinstance(r, int) else r - 4)

            def scatter(r, u, static):
                if static is None or static - 1 >= 2:
                    pool.wait_ge(scattered[u], (r - u) // 2 * NJ * 16 if isinstance(r, int) else (r - u) * (NJ * 8))
                nc.gpsimd.tensor_copy(put[:, u, :], g.put[:, bass.ds(r * NJ, NJ)]).then_inc(indexed, 1)
                pool.wait_ge(indexed, r + 1 + (min(r + 5, NRUN) if isinstance(r, int) else r + 5))
                pool.wait_ge(y_ready, r + 1)
                pool.sem_inc(passed, 1)
                for j in range(NJ):
                    nc.gpsimd.indirect_dma_start(out=g.y_dram, out_offset=bass.IndirectOffsetOnAxis(ap=put[:, u, j:j + 1], axis=0),
                                                 in_=y[:, u, j, :], in_offset=None,
                                                 bounds_check=RANKS * T - 1, oob_is_err=False).then_inc(scattered[u], 16)

            def emit(i, u, m, static):
                if runs(static, 3):
                    gather(i + 3, (u + 3) % 2, static)
                if runs(static, -1):
                    scatter(i - 1, (u + 1) % 2, static)
            emit(-3, 1, 0, static=-3)
            stages(pool, emit)
            for u in range(2):
                pool.wait_ge(scattered[u], NRUN // 2 * NJ * 16)

        @block.tensor
        def _(pe):
            def transpose_in(r, u, static):
                pe.wait_ge(gathered[u], (r // 2 + 1) * NJ * 16 if isinstance(r, int) else (r + (2 - u)) * (NJ * 8))
                if static is None or static + 2 >= 1:
                    pe.wait_ge(xT_ready, r)
                for j in range(NJ):
                    ins = nc.tensor.transpose(ps_in[:, j * P:(j + 1) * P], g.xe[:, u, j, :], g.c("ident"))
                ins.then_inc(in_done, 1)

            def up(r, u, static):
                pe.wait_ge(w_loaded[u], (r // 2 + 1) * 32 if isinstance(r, int) else (r + (2 - u)) * 16)
                pe.wait_ge(xT_ready, r + 1)
                for f in range(NF):
                    if static is None or static + 1 >= 1:
                        pe.wait_ge(h_ready, NF * (r - 1) + f + 1)
                    nc.tensor.matmul(ps_h[f][:, :], w1s[:, u, f * P:(f + 1) * P], xT[:, u, :],
                                     start=True, stop=True).then_inc(up_done, 1)

            def transpose_out(r, u, static):
                pe.wait_ge(yT_ready, r + 1)
                if static is None or static - 1 >= 1:
                    pe.wait_ge(y_ready, r)
                for j in range(NJ):
                    ins = nc.tensor.transpose(ps_y[:, j, :], yT[:, j * P:(j + 1) * P], g.c("ident"))
                ins.then_inc(out_done, 1)

            def down(r, u, static):
                if static is None or static >= 1:
                    pe.wait_ge(yT_ready, r)
                for f in range(NF):
                    pe.wait_ge(h_ready, NF * r + f + 1)
                    ins = nc.tensor.matmul(ps_yT[:, :], w2s[:, u, f, :], hT[:, u, f, :], start=(f == 0), stop=(f == NF - 1))
                ins.then_inc(down_done, 1)

            def emit(i, u, m, static):
                if runs(static, 2):
                    transpose_in(i + 2, u, static)
                if runs(static, 1):
                    up(i + 1, (u + 1) % 2, static)
                if runs(static, -1):
                    transpose_out(i - 1, (u + 1) % 2, static)
                if runs(static, 0):
                    down(i, u, static)
            stages(pe, emit)

        @block.scalar
        def _(act):
            def emit(i, u, m, static):
                if not runs(static, 1):
                    return
                r, u = i + 1, (u + 1) % 2
                for f in range(NF):
                    act.wait_ge(up_done, NF * r + f + 1)
                    if f == 0 and (static is None or static + 1 >= 2):
                        act.wait_ge(down_done, r - 1)
                    nc.scalar.activation(hT[:, u, f, :], ps_h[f][:, :], ACT.Gelu_apprx_tanh).then_inc(h_ready, 1)
            stages(act, emit)

        @block.vector
        def _(dve):
            def emit(i, u, m, static):
                if runs(static, 2):
                    r = i + 2
                    dve.wait_ge(in_done, r + 1)
                    if static is None or static + 2 >= 2:
                        dve.wait_ge(up_done, NF * (r - 1))
                    nc.vector.tensor_copy(xT[:, u, :], ps_in[:, :]).then_inc(xT_ready, 1)
                if runs(static, -1):
                    r = i - 1
                    dve.wait_ge(out_done, r + 1)
                    if static is None or static - 1 >= 2:
                        dve.wait_ge(scattered[(u + 1) % 2], (r // 2) * NJ * 16 if isinstance(r, int)
                                    else (r - (u + 1) % 2) * (NJ * 8))
                    nc.vector.tensor_copy(y[:, (u + 1) % 2, :, :], ps_y[:, :, :]).then_inc(y_ready, 1)
                if runs(static, 0):
                    dve.wait_ge(down_done, i + 1)
                    if static is None or static >= 1:
                        dve.wait_ge(out_done, i)
                    nc.vector.tensor_copy(yT[:, :], ps_yT[:, :]).then_inc(yT_ready, 1)
            stages(dve, emit)


def combine_phase(nc, g, name, out=None):
    with ExitStack() as ctx:
        rows = ctx.enter_context(nc.sbuf_tensor(f"{name}_rows", [P, 2, RANKS, 4, D], F32))

        def sem(n):
            return ctx.enter_context(nc.semaphore(f"{name}_{n}"))
        loaded = [sem(f"rows_loaded{u}") for u in range(2)]
        biased = sem("bias_added")
        first = sem("first_rank_added")
        summed = sem("group_summed")
        stored = sem("group_stored")
        block = ctx.enter_context(nc.Block(no_gpsimd_drain=True))
        y_tiles = g.y_dram.rearrange("(k n p) d -> k n p d", k=RANKS, p=P)

        @block.sync
        def _(sp):
            def load(i, u, start):
                if not start:
                    sp.wait_ge(summed, 2 * i + u - 1)
                for k in range(RANKS):
                    sp.dma_start(rows[:, u, k, :, :],
                                 y_tiles[k, bass.ds((2 * i + u) * 4, 4), :, :].rearrange("n p d -> p n d")).then_inc(loaded[u], 16)
            for u in range(2):
                load(0, u, True)
            with sp.Fori(1, NG // 2) as i:
                for u in range(2):
                    load(i, u, False)

        @block.vector
        def _(dve):
            with dve.Fori(0, NG // 2) as i:
                for u in range(2):
                    n = 2 * i + u
                    xg = g.x[:, bass.ds(4 * n, 4), :]
                    nc.vector.tensor_tensor(xg, xg, g.bias[:, :].rearrange("p (o d) -> p o d", o=1).broadcast_to([P, 4, D]),
                                            ALU.add).then_inc(biased, 1)
                    dve.wait_ge(loaded[u], 32 * i + 32)
                    for k in range(RANKS):
                        dve.wait_ge(biased if k == 0 else first, n + 1)
                        for j in range(4):
                            xt = g.x[:, bass.ds(4 * n + j, 1), :]
                            ins = nc.vector.scalar_tensor_tensor(xt, rows[:, u, k, j:j + 1, :], g.weight[:, k, bass.ds(4 * n + j, 1)],
                                                                 xt, ALU.mult, ALU.add)
                        ins.then_inc(first if k == 0 else summed, 1)
            dve.wait_ge(summed, NG)

        if out is not None:
            @block.scalar
            def _(act):
                with act.Fori(0, NG) as i:
                    act.wait_ge(summed, i + 1)
                    act.dma_start(out[bass.ds(4 * i, 4), :, :].rearrange("n p d -> p n d"), g.x[:, bass.ds(4 * i, 4), :]).then_inc(stored, 16)
                act.wait_ge(stored, 16 * NG)


def ffn(nc, g, name, w1, w2, out=None):
    with ExitStack() as ctx:
        g.logits = ctx.enter_context(nc.psum_tensor(f"{name}_logits", [P, NTILE, E], F32))
        norm_phase(nc, g, f"{name}_norm", True)
        route_phase(nc, g, f"{name}_route")
    expert_phase(nc, g, f"{name}_experts", w1, w2)
    combine_phase(nc, g, f"{name}_combine", out)


C = 4
BT = 64
NBK = NT // BT
NCH = BT // C
GR = NB * NCH
PASSES = 12


def attention_core(nc, g, W):
    with ExitStack() as ctx:
        def sb(n, shape, dt=F32):
            return ctx.enter_context(nc.sbuf_tensor(f"att_{n}", shape, dt))

        def ps(n, shape):
            return ctx.enter_context(nc.psum_tensor(f"att_{n}", shape, F32))

        def sem(n):
            return ctx.enter_context(nc.semaphore(f"att_{n}"))

        blk = [P, GR, C]
        XY = sb("XY", [P, 2, 2, GR, C])
        ZO = sb("ZO", [P, 2, 2, GR, C])
        Xm = sb("X_masked", [P, 2, HD, NB * BT])
        Kbar = sb("K_bar", [P, 2, GR, C])
        decay = sb("decay", [P, 2, GR, C])
        gate = sb("out_gate", [P, 2, GR, C])
        hist = sb("states", [P, 2, NCH, HD, NB])
        z16 = sb("low_rank", [16, NB * BT])
        sk, kraw, k2, kinv, k, f, sg, sq, q, a = (sb(n, blk) for n in (
            "sig_k", "k_raw", "k_square", "k_inverse_norm", "k", "forget", "sig_gamma", "sig_q", "q", "a"))
        kd = [k] + [sb(f"k_decayed{d}", [P, GR, C - d]) for d in range(1, C)]
        pa = [None] + [sb(f"a_k{d}", [P, GR, C - d]) for d in range(1, C)]
        pb = [sb(f"q_k{d}", [P, GR, C - d]) for d in range(C)]
        A = sb("A", [P, GR, C * C])
        B = sb("B", [P, GR, C * C])
        tmp = sb("solve_term", [P, 2, GR, C])
        tmp2 = sb("output_term", [P, 2, GR, C])
        Es = sb("Y_S", [P, 2, HD, NB, C])
        R = sb("K_u", [P, HD, NB, C + 1])
        E2 = sb("Z_S", [P, 2, HD, NB, 4 * C])
        pp = [ps(f"ps_pass{n}", [P, NB * BT]) for n in range(4)]
        pc = [ps(f"ps_u{n}", [P, HD, NB, 2 * C]) for n in range(2)]
        po = ps("ps_o", [P, NB, BT])

        projected = sem("passes_done")
        act_read = sem("passes_read_by_scalar")
        dve_read = sem("passes_read_by_vector")
        sig_done = sem("sigmoids_for_products")
        A_ready = sem("A_ready")
        k2_ready = sem("k_square_ready")
        k_ready = sem("k_and_a_ready")
        pool_step = sem("pool_step")
        pa_ready = sem("a_k_products_ready")
        pb_ready = sem("q_k_products_ready")
        Y_ready = sem("Y_start_ready")
        solved = sem("X_Y_solved")
        masked = sem("X_masked_ready")
        ZO_ready = sem("Z_O_ready")
        pre_step = sem("vector_prepare_step")
        E_ready = sem("Y_S_ready")
        u_ready = sem("u_ready")
        R_ready = sem("K_u_ready")
        state = sem("states_ready")
        E2_ready = sem("Z_S_ready")
        o_done = sem("o_collected")
        o_read = sem("o_read")
        o_ready = sem("o_gated")
        spread = sem("X_in_bank")
        zero = sem("state_zeroed")
        passed = sem("waits_passed")
        block = ctx.enter_context(nc.Block(no_gpsimd_drain=True))

        def cols(i):
            return g.xnT[:, :, :].rearrange("p b t -> p b t")[:, :, bass.ds(BT * i, BT)]

        def flat(t):
            return t.rearrange("p a b -> p (a b)")

        def blocks(eng, emit):
            emit(0, 0, True, True)
            with eng.Fori(0, 3) as m:
                emit(2 * m + 1, 1, True, False)
                emit(2 * m + 2, 0, True, False)
            emit(NBK - 1, 1, False, False)

        @block.tensor
        def _(pe):
            def mm(out, w, x, start=True):
                return nc.tensor.matmul(out, w, x, start=start, stop=True, skip_group_check=not start)

            def bank_free(i, n, first):
                by_act = {0: 7, 1: 8, 2: 9, 3: 10, 4: 1, 6: 2, 7: 3, 9: 4, 10: 5, 11: 6}
                if n < 4:
                    if not first:
                        pe.wait_ge(act_read, 10 * (i - 1) + by_act[n])
                elif n in by_act:
                    pe.wait_ge(act_read, 10 * i + by_act[n])
                else:
                    pe.wait_ge(dve_read, 2 * i + {5: 1, 8: 2}[n])

            def project(i, n, first):
                bank_free(i, n, first)
                bank = pp[n % 4]
                if n == 2 or n == 5:
                    pe.wait_ge(act_read, 10 * i + 1)
                if n in (0, 1, 3, 4, 6):
                    w = {0: W.low, 1: W.k, 3: W.gamma, 4: W.q, 6: W.v}[n]
                    m = 16 if n == 0 else P
                    ins = mm(bank[0:m, :].rearrange("p (b t) -> p b t", b=NB), w, cols(i))
                elif n in (2, 5):
                    ins = mm(bank[:, :], W.f2 if n == 2 else W.og2, z16[:, :])
                elif n == 7:
                    pe.wait_ge(k2_ready, i + 1)
                    ins = mm(bank[:, :], g.c("headsum"), flat(k2[:, :, :]))
                elif n == 8:
                    pe.wait_ge(pa_ready, i + 1)
                    mm(bank[:, 0:3 * GR], g.c("headsum"), flat(pa[1][:, :, :]))
                    ins = mm(bank[:, 3 * GR:4 * GR], g.c("headsum"), flat(pa[3][:, :, :]))
                elif n == 9:
                    mm(bank[:, 0:2 * GR], g.c("headsum"), flat(pa[2][:, :, :]))
                    pe.wait_ge(pb_ready, i + 1)
                    ins = mm(bank[:, 2 * GR:4 * GR], g.c("headsum"), flat(pb[2][:, :, :]))
                elif n == 10:
                    ins = mm(bank[:, :], g.c("headsum"), flat(pb[0][:, :, :]))
                else:
                    mm(bank[:, 0:3 * GR], g.c("headsum"), flat(pb[1][:, :, :]))
                    ins = mm(bank[:, 3 * GR:4 * GR], g.c("headsum"), flat(pb[3][:, :, :]))
                ins.then_inc(projected, 1)

            def put_X(i, u, n, first):
                if not (first and n < 2):
                    pe.wait_ge(R_ready, NCH * i + 2 * n - 2)
                if n == 0:
                    pe.wait_ge(masked, i + 1)
                x = Xm[:, u, :, :].rearrange("p v (b t) -> p (v b) t", b=NB)[:, :, 2 * C * n:2 * C * (n + 1)]
                mm(pc[n % 2][:, :, :, :].rearrange("p v b t -> p (v b) t"), g.c("headsum"), x).then_inc(spread, 1)

            def add_YS(i, c):
                pe.wait_ge(E_ready, NCH * i + c + 1)
                h = c % 2
                out = pc[(c // 2) % 2][:, :, :, C * h:C * h + C].rearrange("p v b t -> p (v b) t")
                mm(out, g.c("headsum"), Es[:, c % 2].rearrange("p v b t -> p (v b) t"), start=False).then_inc(u_ready, 1)

            def collect(i, s, first):
                pe.wait_ge(E2_ready, 4 * i + s + 1)
                if s == 0 and not first:
                    pe.wait_ge(o_read, i)
                for v in range(HD):
                    lo = COL["collect"][0] + v * P
                    ins = mm(po[:, :, 4 * C * s:4 * C * (s + 1)], g.const[:, lo:lo + P], E2[:, s % 2, v], start=(v == 0))
                ins.then_inc(o_done, 1)

            def emit(i, u, prep, first):
                put_X(i, u, 0, first)
                for c in range(NCH):
                    add_YS(i, c)
                    if c == 2 and not first:
                        collect(i - 1, 3, False)
                    if c % 2 == 0 and c < NCH - 2:
                        put_X(i, u, c // 2 + 1, first)
                    if prep:
                        for n, at in enumerate((0, 1, 3, 4, 5, 6, 7, 8, 11, 12, 13, 14)):
                            if c == at:
                                project(i + 1, n, False)
                    if c in (7, 11, 15):
                        collect(i, (c - 7) // 4, first)
            for n in range(PASSES):
                project(0, n, True)
            blocks(pe, emit)
            collect(NBK - 1, 3, False)

        @block.scalar
        def _(act):
            def sig(out, n, i, inc):
                act.wait_ge(projected, PASSES * i + n + 1)
                return nc.scalar.activation(out, pp[n % 4][:, :], ACT.Sigmoid).then_inc(inc, 1)

            def prepare(i, u, first):
                act.wait_ge(projected, PASSES * i + 1)
                nc.scalar.activation(z16[:, :], pp[0][0:16, :], ACT.Copy).then_inc(act_read, 1)
                if not first:
                    act.wait_ge(dve_read, 2 * i - 1)
                sig(flat(sk[:, :, :]), 1, i, sig_done)
                if not first:
                    act.wait_ge(pb_ready, i)
                sig(flat(f[:, :, :]), 2, i, act_read)
                if not first:
                    act.wait_ge(k_ready, i)
                sig(flat(sg[:, :, :]), 3, i, act_read)
                if not first:
                    act.wait_ge(dve_read, 2 * i)
                sig(flat(sq[:, :, :]), 4, i, sig_done)
                if not (first or prologue[0]):
                    act.wait_ge(o_ready, i - 1)
                sig(flat(gate[:, u]), 5, i, act_read)
                act.wait_ge(projected, PASSES * i + 7)
                if not (first or prologue[0]):
                    act.wait_ge(ZO_ready, i - 1)
                nc.scalar.activation(flat(XY[:, u, 1]), pp[2][:, :], ACT.Copy).then_inc(act_read, 1)
                act.wait_ge(projected, PASSES * i + 8)
                if not first:
                    act.wait_ge(k_ready, i)
                nc.scalar.activation(flat(kinv[:, :, :]), pp[3][:, :], ACT.Sqrt).then_inc(act_read, 1)

                def spread_out(dst, bank, lo, d):
                    n = C - d
                    src = bank[:, lo:lo + n * GR].rearrange("p (g t) -> p g t", g=GR)
                    last = d + (n - 1) * (C + 1) + 1
                    return nc.scalar.activation(dst[:, :, d:last:C + 1], src, ACT.Copy)
                act.wait_ge(projected, PASSES * i + 9)
                if not first:
                    act.wait_ge(solved, i)
                spread_out(A, pp[0], 0, 1)
                spread_out(A, pp[0], 3 * GR, 3).then_inc(act_read, 1)
                act.wait_ge(projected, PASSES * i + 10)
                spread_out(A, pp[1], 0, 2).then_inc(A_ready, 1)
                if not first:
                    act.wait_ge(ZO_ready, i)
                spread_out(B, pp[1], 2 * GR, 2).then_inc(act_read, 1)
                act.wait_ge(projected, PASSES * i + 11)
                spread_out(B, pp[2], 0, 0).then_inc(act_read, 1)
                act.wait_ge(projected, PASSES * i + 12)
                spread_out(B, pp[3], 0, 1)
                spread_out(B, pp[3], 3 * GR, 3).then_inc(act_read, 1)
                act.wait_ge(solved, i + 1)
                if not (first or prologue[0]):
                    act.wait_ge(spread, (i - 1) * (NCH // 2))
                for v in range(HD):
                    ins = nc.scalar.activation(Xm[:, u, v, :], flat(XY[:, u, 1]), ACT.Copy, scale=g.c("delta")[:, v:v + 1])
                ins.then_inc(masked, 1)

            prologue = [True]

            def emit(i, u, prep, first):
                prologue[0] = first
                if prep:
                    prepare(i + 1, 1 - u, False)
            prepare(0, 0, True)
            blocks(act, emit)

        @block.gpsimd
        def _(pool):
            G = nc.gpsimd
            link = Chain(pool, pool_step)
            POOL_LINKS = 16

            def prepare1(i, u, first):
                link.begin(POOL_LINKS * i)
                pool.wait_ge(dve_read, 2 * i + 1)
                if not first:
                    pool.wait_ge(act_read, 10 * i - 4)
                G.tensor_tensor(k2[:, :, :], kraw[:, :, :], kraw[:, :, :], ALU.mult).then_inc(k2_ready, 1)
                pool.wait_ge(act_read, 10 * i + 2)
                if not (first or prologue[0]):
                    pool.wait_ge(state, NCH * (i - 1))
                pool.sem_inc(passed, 1)
                link(G.tensor_copy(decay[:, u, :, 0:1], f[:, :, 0:1]))
                for t in range(1, C):
                    link(G.tensor_tensor(decay[:, u, :, t:t + 1], decay[:, u, :, t - 1:t], f[:, :, t:t + 1], ALU.mult))

            def prepare2(i, u, first):
                pool.wait_ge(k_ready, i + 1)
                link(G.tensor_tensor(a[:, :, :], a[:, :, :], f[:, :, :], ALU.mult))
                if not first:
                    pool.wait_ge(projected, PASSES * i)
                for d in range(1, C):
                    link(G.tensor_tensor(kd[d][:, :, :], kd[d - 1][:, :, 0:C - d], f[:, :, d:C], ALU.mult))
                for d in range(1, C):
                    ins = G.tensor_tensor(pa[d][:, :, :], a[:, :, d:C], kd[d][:, :, :], ALU.mult)
                ins.then_inc(pa_ready, 1)
                G.tensor_tensor(XY[:, u, 0], a[:, :, :], decay[:, u], ALU.mult).then_inc(Y_ready, 1)
                for s in range(C):
                    G.tensor_copy(Kbar[:, u, :, s:s + 1], kd[C - 1 - s][:, :, s:s + 1])
                pool.wait_ge(dve_read, 2 * i + 2)
                for d in range(C):
                    ins = G.tensor_tensor(pb[d][:, :, :], q[:, :, d:C], kd[d][:, :, :], ALU.mult)
                ins.then_inc(pb_ready, 1)

            def prepare3(i, u, first):
                pool.wait_ge(solved, i + 1)
                pool.wait_ge(act_read, 10 * i + 10)
                if not (first or prologue[0]):
                    pool.wait_ge(o_read, i - 1)
                link(G.tensor_tensor(q[:, :, :], q[:, :, :], decay[:, u], ALU.mult))
                for s in range(C):
                    n = C - s
                    b4 = B[:, :, :].rearrange("p g (s t) -> p g s t", s=C)[:, :, s, s:C]
                    for h in range(2):
                        x = XY[:, u, h, :, s:s + 1].broadcast_to([P, GR, n])
                        ins = G.tensor_tensor((ZO[:, u, h] if s == 0 else tmp2[:, h, :, 0:n]), x, b4, ALU.mult)
                    link(ins)
                    if s:
                        ins = G.tensor_tensor(ZO[:, u, :, :, s:C], ZO[:, u, :, :, s:C], tmp2[:, :, :, 0:n], ALU.add)
                        if s < C - 1:
                            link(ins)
                link(ins)
                G.tensor_tensor(ZO[:, u, 0], ZO[:, u, 0], q[:, :, :], ALU.add).then_inc(ZO_ready, 1)

            def z_state(i, u, s, first):
                if s == 0:
                    pool.wait_ge(ZO_ready, i + 1)
                if not (first and s < 2):
                    pool.wait_ge(o_done, 4 * i + s - 1)
                for c in range(4 * s, 4 * s + 4):
                    if not (first and c == 0):
                        pool.wait_ge(state, NCH * i + c)
                    z = ZO[:, u, 0].rearrange("p (b n) t -> p b n t", b=NB)[:, :, c, :]
                    z = z.rearrange("p (o b) t -> p o b t", o=1).broadcast_to([P, HD, NB, C])
                    st = hist[:, u, c].rearrange("p v (b o) -> p v b o", o=1).broadcast_to([P, HD, NB, C])
                    ins = G.tensor_tensor(E2[:, s % 2, :, :, C * (c % 4):C * (c % 4 + 1)], z, st, ALU.mult)
                ins.then_inc(E2_ready, 1)

            prologue = [True]

            def emit(i, u, prep, first):
                prologue[0] = first
                if prep:
                    prepare1(i + 1, 1 - u, False)
                z_state(i, u, 0, first)
                z_state(i, u, 1, first)
                if prep:
                    prepare2(i + 1, 1 - u, False)
                z_state(i, u, 2, first)
                z_state(i, u, 3, first)
                if prep:
                    prepare3(i + 1, 1 - u, False)
            pool.wait_ge(zero, 1)
            prepare1(0, 0, True)
            prepare2(0, 0, True)
            prepare3(0, 0, True)
            blocks(pool, emit)

        @block.vector
        def _(dve):
            V = nc.vector
            link = Chain(dve, pre_step)
            VEC_LINKS = 8

            def k_product(i, first):
                dve.wait_ge(sig_done, 2 * i + 1)
                if not first:
                    dve.wait_ge(k2_ready, i)
                    dve.wait_ge(k_ready, i)
                V.tensor_tensor(kraw[:, :, :], as3(pp[1]), sk[:, :, :], ALU.mult).then_inc(dve_read, 1)

            def as3(bank):
                return bank[:, :].rearrange("p (g t) -> p g t", t=C)

            def q_product(i, first):
                dve.wait_ge(sig_done, 2 * i + 2)
                if not first:
                    dve.wait_ge(ZO_ready, i)
                V.tensor_tensor(q[:, :, :], as3(pp[0]), sq[:, :, :], ALU.mult).then_inc(dve_read, 1)

            def k_norm(i, first):
                link.begin(VEC_LINKS * i)
                dve.wait_ge(act_read, 10 * i + 6)
                if not first:
                    dve.wait_ge(pb_ready, i)
                link(V.tensor_scalar(kinv[:, :, :], kinv[:, :, :], 1e-12, None, ALU.max))
                link(V.reciprocal(kinv[:, :, :], kinv[:, :, :]))
                link(V.tensor_tensor(k[:, :, :], kraw[:, :, :], kinv[:, :, :], ALU.mult))
                V.scalar_tensor_tensor(a[:, :, :], k[:, :, :], -1.0, sg[:, :, :], ALU.mult, ALU.mult).then_inc(k_ready, 1)

            def solve(i, u):
                dve.wait_ge(A_ready, i + 1)
                dve.wait_ge(Y_ready, i + 1)
                for s in range(C - 1):
                    n = C - 1 - s
                    a4 = A[:, :, :].rearrange("p g (s t) -> p g s t", s=C)[:, :, s, s + 1:C]
                    for h in range(2):
                        x = XY[:, u, h, :, s:s + 1].broadcast_to([P, GR, n])
                        ins = V.tensor_tensor(tmp[:, h, :, 0:n], x, a4, ALU.mult)
                    link(ins)
                    ins = V.tensor_tensor(XY[:, u, :, :, s + 1:C], XY[:, u, :, :, s + 1:C], tmp[:, :, :, 0:n], ALU.add)
                    if s < C - 2:
                        link(ins)
                ins.then_inc(solved, 1)

            def chunk(i, u, c, first):
                if c == 0:
                    dve.wait_ge(solved, i + 1)
                each = [P, HD, NB, C]
                S = hist[:, u, c]
                S4 = S.rearrange("p v (b o) -> p v b o", o=1)

                def part(t):
                    t = t.rearrange("p (b n) t -> p b n t", b=NB)[:, :, c, :]
                    return t.rearrange("p (o b) t -> p o b t", o=1)
                if not (first and c == 0):
                    dve.wait_ge(state, NCH * i + c)
                V.tensor_tensor(Es[:, c % 2], part(XY[:, u, 0]).broadcast_to(each), S4.broadcast_to(each), ALU.mult).then_inc(E_ready, 1)
                V.tensor_tensor(R[:, :, :, C:C + 1], part(decay[:, u])[:, :, :, C - 1:C].broadcast_to([P, HD, NB, 1]), S4, ALU.mult)
                dve.wait_ge(u_ready, NCH * i + c + 1)
                V.tensor_tensor(R[:, :, :, 0:C], pc[(c // 2) % 2][:, :, :, C * (c % 2):C * (c % 2) + C],
                                part(Kbar[:, u]).broadcast_to(each), ALU.mult).then_inc(R_ready, 1)
                dve.wait_ge(R_ready, NCH * i + c + 1)
                if c < NCH - 1:
                    dst = hist[:, u, c + 1]
                else:
                    dst = hist[:, 1 - u, 0]
                    if not first:
                        dve.wait_ge(E2_ready, 4 * i)
                V.tensor_reduce(dst, R[:, :, :, :], AX, ALU.add).then_inc(state, 1)

            def finish(i, u):
                dve.wait_ge(o_done, 4 * i + 4)
                out = g.oT[:, :, bass.ds(BT * i, BT)]
                V.tensor_tensor(out, po[:, :, :], ZO[:, u, 1].rearrange("p (b n) t -> p b (n t)", b=NB), ALU.add).then_inc(o_read, 1)
                dve.wait_ge(o_read, i + 1)
                V.tensor_tensor(out, out, gate[:, u].rearrange("p (b n) t -> p b (n t)", b=NB), ALU.mult).then_inc(o_ready, 1)

            def emit(i, u, prep, first):
                for c in range(NCH):
                    chunk(i, u, c, first)
                    if c == 5 and not first:
                        finish(i - 1, 1 - u)
                    if prep:
                        if c == 4:
                            k_product(i + 1, False)
                        if c == 6:
                            q_product(i + 1, False)
                        if c == 9:
                            k_norm(i + 1, False)
                        if c == 14:
                            solve(i + 1, 1 - u)

            V.memset(hist[:, 0, 0], 0.0).then_inc(zero, 1)
            dve.wait_ge(zero, 1)
            k_product(0, True)
            q_product(0, True)
            k_norm(0, True)
            solve(0, 0)
            blocks(dve, emit)
            finish(NBK - 1, 1)
            dve.wait_ge(o_ready, NBK)


def rsqrt_of_stats(nc, dve, link, stats, w, var_ready, root_ready):
    V = nc.vector
    mean, dmean, m2, var, root, quot, scale = (w[:, i, :] for i in range(7))
    a = [stats[:, :, k] for k in range(6)]
    V.tensor_tensor(mean, a[1], a[4], ALU.add)
    V.tensor_tensor(dmean, a[1], a[4], ALU.subtract)
    link(V.tensor_tensor(m2, a[2], a[5], ALU.add))
    link(V.tensor_tensor(dmean, dmean, dmean, ALU.mult))
    link(V.tensor_scalar(dmean, dmean, 0.25, 1e-5, ALU.mult, ALU.add))
    V.tensor_scalar(mean, mean, 0.5, None, ALU.mult)
    V.scalar_tensor_tensor(var, m2, 1.0 / D, dmean, ALU.mult, ALU.add).then_inc(var_ready, 1)
    dve.wait_ge(root_ready, 1)
    link(V.reciprocal(quot, root))
    link(V.tensor_tensor(quot, quot, var, ALU.mult))
    link(V.tensor_tensor(root, root, quot, ALU.add))
    link(V.reciprocal(scale, root))
    link(V.tensor_scalar(scale, scale, 2.0, None, ALU.mult))


def attention_weights(nc, g, W, Wq, Wk, Wv, Wgamma, Wf1, Wf2, Wog1, Wog2, norm_w, Wo):
    with ExitStack() as ctx:
        ps_mean = ctx.enter_context(nc.psum_tensor("ps_column_sums", [P, D], F32))
        cleared = ctx.enter_context(nc.semaphore("padding_zeroed"))
        loaded = ctx.enter_context(nc.semaphore("weights_loaded"))
        padded = ctx.enter_context(nc.semaphore("padded_weights_loaded"))
        weighted = ctx.enter_context(nc.semaphore("norm_weighted"))
        summed = ctx.enter_context(nc.semaphore("columns_summed"))
        made = ctx.enter_context(nc.semaphore("attention_weights_made"))
        gsmall = ctx.enter_context(nc.sbuf_tensor("gamma_small", [P, H], F32))
        nw = ctx.enter_context(nc.sbuf_tensor("norm_weight", [P, 1], F32))
        wo = ctx.enter_context(nc.sbuf_tensor("Wo_weighted", [P, D], F32))
        block = ctx.enter_context(nc.Block(no_gpsimd_drain=True))

        @block.sync
        def _(sp):
            for dst, src in ((W.q, Wq), (W.k, Wk), (W.v, Wv), (gsmall[:, :], Wgamma), (W.low[:, 0:HD], Wf1),
                             (W.low[:, HD:2 * HD], Wog1), (wo[:, :], Wo), (nw[:, :], norm_w.rearrange("(p o) -> p o", o=1))):
                sp.dma_start(dst, src[:, :]).then_inc(loaded, 16)
            sp.wait_ge(cleared, 2)
            sp.dma_start(W.f2[0:HD, :], Wf2[:, :]).then_inc(padded, 16)
            sp.dma_start(W.og2[HD:2 * HD, :], Wog2[:, :]).then_inc(padded, 16)
            sp.wait_ge(padded, 32)

        @block.vector
        def _(dve):
            V = nc.vector
            V.memset(W.f2, 0.0).then_inc(cleared, 1)
            V.memset(W.og2, 0.0).then_inc(cleared, 1)
            dve.wait_ge(loaded, 8 * 16)
            V.tensor_copy(W.gamma.rearrange("p (h c) -> p h c", h=H),
                          gsmall[:, :].rearrange("p (h o) -> p h o", o=1).broadcast_to([P, H, HD])).then_inc(made, 1)
            V.tensor_scalar(wo[:, :], wo[:, :], nw[:, :], None, ALU.mult).then_inc(weighted, 1)
            V.tensor_copy(W.out[:, D:2 * D], g.c("ident")).then_inc(made, 1)
            dve.wait_ge(weighted, 1)
            dve.wait_ge(summed, 1)
            V.scalar_tensor_tensor(W.out[:, 0:D], ps_mean[:, :], -1.0 / D, wo[:, :], ALU.mult, ALU.add).then_inc(made, 1)
            dve.wait_ge(made, 3)

        @block.tensor
        def _(pe):
            pe.wait_ge(weighted, 1)
            nc.tensor.matmul(ps_mean[:, :], g.c("ones"), wo[:, :], start=True, stop=True).then_inc(summed, 1)


def attention_output(nc, g, W, out=None):
    with ExitStack() as ctx:
        def sb(n, shape, dt=F32):
            return ctx.enter_context(nc.sbuf_tensor(f"attout_{n}", shape, dt))

        def sem(n):
            return ctx.enter_context(nc.semaphore(f"attout_{n}"))
        stage = sb("stage", [P, 2, 4 * P])
        proj = sb("projected", [P, NTILE, D])
        stats = sb("stats", [P, NTILE, 6])
        w = sb("stat_work", [P, 8, NTILE])
        ps = [ctx.enter_context(nc.psum_tensor(f"attout_ps{n}", [P, 4, 2 * D], F32)) for n in range(2)]
        staged = sem("staged")
        multiplied = sem("projected")
        kept = sem("projection_kept")
        measured = sem("statistics_taken")
        step = sem("vector_step")
        var_ready = sem("variance_ready")
        root_ready = sem("root_ready")
        summed = sem("group_summed")
        stored = sem("group_stored")
        block = ctx.enter_context(nc.Block(no_gpsimd_drain=True))

        def pairs(eng, emit):
            for u in range(2):
                emit(0, u, True)
            with eng.Fori(1, NG // 2) as i:
                for u in range(2):
                    emit(i, u, False)

        @block.scalar
        def _(act):
            def emit(i, u, first):
                if not first:
                    act.wait_ge(multiplied, 2 * i + u - 1)
                nc.scalar.activation(stage[:, u, :], g.oT[:, bass.ds(2 * i + u, 1), :], ACT.Copy).then_inc(staged, 1)
                act.wait_ge(measured, 2 * i + u + 1)
                nc.scalar.activation(proj[:, bass.ds(8 * i + 4 * u, 4), :], ps[u][:, :, 0:D], ACT.Copy).then_inc(kept, 1)
            pairs(act, emit)
            act.wait_ge(var_ready, 1)
            nc.scalar.activation(w[:, 4, :], w[:, 3, :], ACT.Sqrt).then_inc(root_ready, 1)

        @block.tensor
        def _(pe):
            def emit(i, u, first):
                pe.wait_ge(staged, 2 * i + u + 1)
                if not first:
                    pe.wait_ge(kept, 2 * i + u - 1)
                for j in range(4):
                    ins = nc.tensor.matmul(ps[u][:, j, :], stage[:, u, j * P:(j + 1) * P], W.out, start=True, stop=True)
                ins.then_inc(multiplied, 1)
            pairs(pe, emit)

        @block.vector
        def _(dve):
            link = Chain(dve, step)

            def emit(i, u, first):
                dve.wait_ge(multiplied, 2 * i + u + 1)
                for j in range(4):
                    ins = nc.vector.bn_stats(stats[:, bass.ds(8 * i + 4 * u + j, 1), :], ps[u][:, j:j + 1, D:2 * D])
                ins.then_inc(measured, 1)
            pairs(dve, emit)
            dve.wait_ge(measured, NG)
            rsqrt_of_stats(nc, dve, link, stats, w, var_ready, root_ready)
            dve.wait_ge(kept, NG)
            with dve.Fori(0, NG) as i:
                for j in range(4):
                    t = 4 * i + j
                    xt = g.x[:, bass.ds(t, 1), :]
                    ins = nc.vector.scalar_tensor_tensor(xt, proj[:, bass.ds(t, 1), :], w[:, 6, bass.ds(t, 1)], xt, ALU.mult, ALU.add)
                ins.then_inc(summed, 1)
            dve.wait_ge(summed, NG)

        if out is not None:
            @block.sync
            def _(sp):
                with sp.Fori(0, NG) as i:
                    sp.wait_ge(summed, i + 1)
                    sp.dma_start(out[bass.ds(4 * i, 4), :, :].rearrange("n p d -> p n d"), g.x[:, bass.ds(4 * i, 4), :]).then_inc(stored, 16)
                sp.wait_ge(stored, 16 * NG)


def attention(nc, g, Wq, Wk, Wv, Wgamma, Wf1, Wf2, Wog1, Wog2, norm_w, Wo, out=None):
    W = Shared()
    with ExitStack() as ctx:
        def sb(n, shape):
            return ctx.enter_context(nc.sbuf_tensor(f"weight_{n}", shape, F32))
        W.out = sb("out", [P, 2 * D])[:, :]
        g.oT = sb("oT", [P, NB, NT])
        with ExitStack() as inner:
            def sbi(n, shape):
                return inner.enter_context(nc.sbuf_tensor(f"weight_{n}", shape, F32))[:, :]
            W.q, W.k, W.v, W.gamma = (sbi(n, [P, D]) for n in ("q", "k", "v", "gamma"))
            W.low = sbi("low", [P, 2 * HD])
            W.f2, W.og2 = sbi("f2", [2 * HD, D]), sbi("og2", [2 * HD, D])
            g.xnT = inner.enter_context(nc.sbuf_tensor("attention_xnT", [P, NB, NT], F32))
            attention_weights(nc, g, W, Wq, Wk, Wv, Wgamma, Wf1, Wf2, Wog1, Wog2, norm_w, Wo)
            norm_phase(nc, g, "att_norm", False)
            attention_core(nc, g, W)
        attention_output(nc, g, W, out)


def macaron_kernel(nc, x, Wq, Wk, Wv, Wgamma, Wf1, Wf2, Wog1, Wog2, norm_w, Wo, router_w, w1, w2, bias, consts, out):
    g = Shared()
    with ExitStack() as ctx:
        def sb(n, shape, dt=F32):
            return ctx.enter_context(nc.sbuf_tensor(n, shape, dt))
        g.x = sb("x_tokens", [P, NTILE, D])
        g.const = sb("constants", [P, NCONST])
        g.c = lambda n: g.const[:, COL[n][0]:COL[n][1]]
        g.tri = sb("tri_bf", [P, P], BF16)
        g.ones = sb("ones_bf", [P, P], BF16)
        g.router = sb("router", [P, E])
        g.bias = sb("half_bias", [P, D])
        g.weight = sb("rank_weight", [P, RANKS, NTILE])
        g.take = sb("take_rows", [P, RANKS * NBLK], U32)
        g.put = sb("put_rows", [P, RANKS * NBLK], U32)
        g.xe = sb("expert_rows", [P, 2, NJ, D])
        g.router_in, g.bias_in = router_w, bias
        xn = nc.dram_tensor("normalised_rows", [NTILE, P, D], F32, kind="Internal").ap()
        g.xn_dram = xn
        g.xn_rows = xn.rearrange("n p d -> (n p) d")
        g.y_dram = nc.dram_tensor("expert_outputs", [RANKS * T, D], F32, kind="Internal").ap()
        out_tiles = out.rearrange("b (n p) d -> (b n) p d", p=P)

        load_phase(nc, g, x.rearrange("b t d -> (b t) d"), consts)
        ffn(nc, g, "first", w1, w2)
        attention(nc, g, Wq, Wk, Wv, Wgamma, Wf1, Wf2, Wog1, Wog2, norm_w, Wo)
        ffn(nc, g, "second", w1, w2, out_tiles)


_INS = ["L0_attn_x", "L0_attn_Wq", "L0_attn_Wk", "L0_attn_Wv", "L0_attn_Wgamma", "L0_attn_Wf1", "L0_attn_Wf2",
        "L0_attn_Wog1", "L0_attn_Wog2", "L0_attn_norm_w", "L0_attn_Wo", "L0_ffn_router_w", "L0_ffn_w1", "L0_ffn_w2",
        "L0_ffn_bias"]


def kernel(**inputs):
    import concourse.bacc as _bacc
    from concourse.bass_utils import run_bass_kernel_spmd as _run

    nc = _bacc.Bacc("TRN2", target_bir_lowering=False, num_devices=1)
    arrays, args = {}, []
    for name in _INS:
        a = np.ascontiguousarray(inputs[name])
        arrays[f"in_{name}"] = a
        args.append(nc.dram_tensor(f"in_{name}", a.shape, mybir.dt.from_np(a.dtype), kind="ExternalInput").ap())
    arrays["in_constants"] = constant_table()
    args.append(nc.dram_tensor("in_constants", (P, NCONST), F32, kind="ExternalInput").ap())
    args.append(nc.dram_tensor("out_tokens", (NB, NT, D), F32, kind="ExternalOutput").ap())
    macaron_kernel(nc, *args)
    r = _run(nc, [arrays], core_ids=[0])
    return r.results[0]["out_tokens"]
```

```python
from contextlib import ExitStack

import numpy as np
import concourse.bass as bass
from concourse import mybir
from concourse.alu_op_type import AluOpType as ALU

F32 = mybir.dt.float32
BF16 = mybir.dt.bfloat16
U32 = mybir.dt.uint32
ACT = mybir.ActivationFunctionType
AX = mybir.AxisListType.X

P = 128
D = 128
NB = 8
NT = 512
H, HD = 16, 8
T = NB * NT
NTILE = T // P
NG = NTILE // 4
E = 8
FF = 512
NF = FF // P
CAP = T // E
NJ = CAP // P
RANKS = 2
NBLK = E * NJ
NRUN = RANKS * E
EMPTY = 1 << 20

_off = 0
COL = {}
for _name, _n in (("ident", 128), ("headsum", 128), ("tri", 128), ("ones", 128), ("iota", 128),
                  ("tile", 32), ("tieorder", 8), ("expert", 8), ("segment", 512), ("part", 1), ("delta", 8),
                  ("collect", 1024)):
    COL[_name] = (_off, _off + _n)
    _off += _n
NCONST = _off


def constant_table():
    t = np.zeros((P, NCONST), np.float32)

    def put(name, a):
        lo, hi = COL[name]
        t[:, lo:hi] = np.broadcast_to(a, (P, hi - lo))
    p = np.arange(P)
    put("ident", np.eye(P))
    put("headsum", p[:, None] // HD == p[None, :] // HD)
    put("tri", p[:, None] < p[None, :])
    put("ones", 1.0)
    put("iota", p[None, :])
    put("tile", np.arange(32)[None, :])
    put("tieorder", 8.0 - np.arange(8)[None, :])
    put("expert", np.arange(8)[None, :])
    put("segment", (np.arange(512) % 32 != 0)[None, :])
    put("part", p[:, None])
    put("delta", p[:, None] % HD == np.arange(HD)[None, :])
    same = p[:, None] // HD == p[None, :] // HD
    put("collect", np.concatenate([same & (p[None, :] % HD == v) for v in range(HD)], 1))
    return t


class Chain:

    def __init__(self, eng, sem):
        self.eng, self.sem, self.base, self.n = eng, sem, 0, 0

    def begin(self, base):
        self.base, self.n = base, 0

    def __call__(self, ins):
        self.n += 1
        ins.then_inc(self.sem, 1)
        self.eng.wait_ge(self.sem, self.base + self.n)



class Shared:
    pass


def load_inputs(nc, g, sp, x_in, consts):
    q = NTILE // 4
    for n in range(4):
        sp.dma_start(g.x[:, q * n:q * (n + 1), :],
                     x_in[q * n * P:q * (n + 1) * P, :].rearrange("(n p) d -> p n d", p=P)).then_inc(g.x_loaded[n], 16)
    for dst, src in ((g.const[:, :], consts[:, :]), (g.router[:, :], g.router_in[:, :]),
                     (g.bias[:, :], g.bias_in.rearrange("a b d -> (a b) d").broadcast_to([P, D]))):
        sp.dma_start(dst, src).then_inc(g.consts_loaded, 16)


def clear_expert_rows(g, act):
    act.wait_ge(g.zeroed, 1)
    rows = RANKS * T // 8
    for q in range(8):
        act.dma_start(g.y_dram[q * rows:(q + 1) * rows, :].rearrange("(p n) d -> p (n d)", p=P),
                      g.xe[:, 0:2, :, :].rearrange("p a j d -> p (a j d)")).then_inc(g.cleared, 16)


def norm_phase(nc, g, name, route, load=None):
    with ExitStack() as ctx:
        def sb(n, shape, dt=F32):
            return ctx.enter_context(nc.sbuf_tensor(f"{name}_{n}", shape, dt))

        def sem(n):
            return ctx.enter_context(nc.semaphore(f"{name}_{n}"))

        stats = sb("stats", [P, NTILE, 6])
        w = sb("stat_work", [P, 8, NTILE])
        mean, dmean, m2, var, root, quot, scale = (w[:, i, :] for i in range(7))
        rows = sb("rows", [P, 4, 4, D])
        cols = sb("cols", [P, 2, 4 * P]) if route else None
        psT = [ctx.enter_context(nc.psum_tensor(f"{name}_psT{u}", [P, 4, P], F32)) for u in range(2)]

        step = sem("vector_step")
        var_ready = sem("variance_ready")
        root_ready = sem("root_ready")
        rows_ready = sem("rows_normalised")
        transposed = sem("rows_transposed")
        cols_ready = sem("columns_copied")
        scored = sem("logits_done") if route else None
        stored = [sem(f"rows_stored{u}") for u in range(4)] if route else None
        block = ctx.enter_context(nc.Block(no_gpsimd_drain=True))

        @block.vector
        def _(dve):
            link = Chain(dve, step)
            for q in range(4):
                if load is not None:
                    dve.wait_ge(g.x_loaded[q], 16)
                with dve.Fori(2 * q, 2 * q + 2) as i:
                    for j in range(4):
                        ins = nc.vector.bn_stats(stats[:, bass.ds(i * 4 + j, 1), :], g.x[:, bass.ds(i * 4 + j, 1), :])
                    ins.then_inc(step, 1)
            if load is not None:
                dve.wait_ge(g.consts_loaded, 3 * 16)
                for src, dst in (("tri", g.tri), ("ones", g.ones)):
                    nc.vector.tensor_copy(dst[:, :], g.c(src)).then_inc(g.copied, 1)
                nc.vector.tensor_scalar(g.bias[:, :], g.bias[:, :], 0.5, None, ALU.mult).then_inc(g.copied, 1)
                dve.wait_ge(g.copied, 3)
            dve.wait_ge(step, NG)
            link.begin(NG)
            rsqrt_of_stats(nc, dve, link, stats, w, var_ready, root_ready)

            def normalise(i, u, first):
                if not first:
                    dve.wait_ge(transposed, 4 * i + u - 3)
                    if route:
                        dve.wait_ge(stored[u], 16 * i)
                for j in range(4):
                    t = 16 * i + 4 * u + j
                    ins = nc.vector.tensor_scalar(rows[:, u, j, :], g.x[:, bass.ds(t, 1), :],
                                                  mean[:, bass.ds(t, 1)], scale[:, bass.ds(t, 1)],
                                                  ALU.subtract, ALU.mult)
                ins.then_inc(rows_ready, 1)
            for i in range(NG // 4):
                for u in range(4):
                    normalise(i, u, i == 0)

        @block.tensor
        def _(pe):
            def transposes(n):
                pe.wait_ge(rows_ready, n + 1)
                if n >= 2:
                    pe.wait_ge(cols_ready, n - 1)
                for j in range(4):
                    ins = nc.tensor.transpose(psT[n % 2][:, j, :], rows[:, n % 4, j, :], g.c("ident"))
                ins.then_inc(transposed, 1)

            def logits(n):
                pe.wait_ge(cols_ready, n + 1)
                for j in range(4):
                    ins = nc.tensor.matmul(g.logits[:, 4 * n + j, :],
                                           cols[:, n % 2, j * P:(j + 1) * P], g.router[:, :], start=True, stop=True)
                ins.then_inc(scored, 1)

            if load is not None:
                pe.wait_ge(g.consts_loaded, 3 * 16)
            for n in range(NG):
                transposes(n)
                if route and n >= 1:
                    logits(n - 1)
            if route:
                logits(NG - 1)

        if route:
            @block.gpsimd
            def _(pool):
                nc.gpsimd.memset(g.xe[:, :, :, :], 0.0).then_inc(g.zeroed, 1)

        @block.scalar
        def _(act):
            if load is not None:
                clear_expert_rows(g, act)
            act.wait_ge(var_ready, 1)
            nc.scalar.activation(root, var, ACT.Sqrt).then_inc(root_ready, 1)

            def copies(i, u, first):
                act.wait_ge(transposed, 2 * i + u + 1)
                if route:
                    if not first:
                        act.wait_ge(scored, 2 * i + u - 1)
                    dst = cols[:, u, :]
                else:
                    dst = g.xnT[:, bass.ds(i * 2 + u, 1), :]
                nc.scalar.activation(dst, psT[u][:, :, :].rearrange("p j q -> p (j q)"), ACT.Copy).then_inc(cols_ready, 1)
            for u in range(2):
                copies(0, u, True)
            with act.Fori(1, NG // 2) as i:
                for u in range(2):
                    copies(i, u, False)

        if route:
            @block.sync
            def _(sp):
                if load is not None:
                    load_inputs(nc, g, sp, *load)
                with sp.Fori(0, NG // 4) as i:
                    for u in range(4):
                        sp.wait_ge(rows_ready, 4 * i + u + 1)
                        sp.dma_start(g.xn_dram[bass.ds((4 * i + u) * 4, 4), :, :].rearrange("n p d -> p n d"),
                                     rows[:, u, :, :]).then_inc(stored[u], 16)
                for u in range(4):
                    sp.wait_ge(stored[u], 16 * (NG // 4))


class SlotList:
    CHUNKS = 4

    def __init__(self, nc, ctx, name):
        def sb(n, shape, dt=F32):
            return ctx.enter_context(nc.sbuf_tensor(f"{name}_{n}", shape, dt))
        self.hi = sb("hi", [P, RANKS, NTILE])
        self.lo = sb("lo", [P, RANKS, NTILE])
        self.low = sb("low_onehot", [P, RANKS, NTILE, P], BF16)
        self.high = sb("high_onehot", [P, RANKS, NTILE, 3, NBLK], BF16)
        self.found = sb("found", [P, RANKS, 3, NBLK])
        self.block_known = ctx.enter_context(nc.semaphore(f"{name}_block_onehots"))
        self.place_known = ctx.enter_context(nc.semaphore(f"{name}_place_onehots"))
        self.rows_scaled = ctx.enter_context(nc.semaphore(f"{name}_row_numbers"))
        self.listed = ctx.enter_context(nc.semaphore(f"{name}_slot_tokens"))
        self.step = ctx.enter_context(nc.semaphore(f"{name}_step"))
        self.indices_known = ctx.enter_context(nc.semaphore(f"{name}_indices"))

    def onehots(self, nc, g, dve, k):
        shape = [P, NTILE, NBLK]
        nc.vector.tensor_tensor(self.high[:, k, :, 0, :], g.c("tile").rearrange("p (o q) -> p o q", o=1).broadcast_to(shape),
                                self.hi[:, k].rearrange("p (t o) -> p t o", o=1).broadcast_to(shape),
                                ALU.is_equal).then_inc(self.block_known, 1)
        dve.wait_ge(self.block_known, k + 1)
        nc.vector.tensor_tensor(self.high[:, k, :, 1, :], self.high[:, k, :, 0, :],
                                g.c("tile").rearrange("p (t o) -> p t o", o=1).broadcast_to(shape), ALU.mult)
        n = NTILE // self.CHUNKS
        shape = [P, n, P]
        for c in range(self.CHUNKS):
            nc.vector.tensor_tensor(self.low[:, k, n * c:n * (c + 1)], g.c("iota").rearrange("p (o q) -> p o q", o=1).broadcast_to(shape),
                                    self.lo[:, k, n * c:n * (c + 1)].rearrange("p (t o) -> p t o", o=1).broadcast_to(shape),
                                    ALU.is_equal).then_inc(self.place_known, 1)

    def row_numbers(self, nc, g, act, k):
        act.wait_ge(self.block_known, k + 1)
        nc.scalar.activation(self.high[:, k, :, 2, :], self.high[:, k, :, 0, :], ACT.Copy, scale=g.c("part")).then_inc(self.rows_scaled, 1)

    def products(self, nc, pe, k, bank):
        pe.wait_ge(self.rows_scaled, k + 1)
        for t in range(NTILE):
            if t % (NTILE // self.CHUNKS) == 0:
                pe.wait_ge(self.place_known, self.CHUNKS * k + t * self.CHUNKS // NTILE + 1)
            ins = nc.tensor.matmul(bank, self.low[:, k, t, :], self.high[:, k, t, :, :].rearrange("p c h -> p (c h)"),
                                   start=(t == 0), stop=(t == NTILE - 1))
        ins.then_inc(self.listed, 1)

    def indices(self, nc, g, dve, k, bank):
        V, f = nc.vector, self.found
        dve.wait_ge(self.listed, k + 1)
        V.tensor_copy(f[:, k].rearrange("p c h -> p (c h)"), bank).then_inc(self.step, 1)
        dve.wait_ge(self.step, 3 * k + 1)
        V.scalar_tensor_tensor(f[:, k, 1], f[:, k, 1], float(P), f[:, k, 2], ALU.mult, ALU.add).then_inc(self.step, 1)
        dve.wait_ge(self.step, 3 * k + 2)
        V.scalar_tensor_tensor(f[:, k, 0], f[:, k, 0], -float(EMPTY), f[:, k, 1], ALU.mult, ALU.add).then_inc(self.step, 1)
        dve.wait_ge(self.step, 3 * k + 3)
        V.tensor_scalar(g.take[:, k * NBLK:(k + 1) * NBLK], f[:, k, 0], float(EMPTY), None, ALU.add)
        V.tensor_scalar(g.put[:, k * NBLK:(k + 1) * NBLK], f[:, k, 0], float(EMPTY + k * T), None,
                        ALU.add).then_inc(self.indices_known, 1)
        dve.wait_ge(self.indices_known, k + 1)


def route_phase(nc, g, name, L):
    with ExitStack() as ctx:
        def sb(n, shape, dt=F32):
            return ctx.enter_context(nc.sbuf_tensor(f"{name}_{n}", shape, dt))

        def ps(n, shape):
            return ctx.enter_context(nc.psum_tensor(f"{name}_{n}", shape, F32))

        def sem(n):
            return ctx.enter_context(nc.semaphore(f"{name}_{n}"))

        scores = sb("scores", [P, NTILE, E])
        work = sb("work", [P, NTILE, E])
        row = sb("row", [P, NTILE])
        best = sb("best", [P, RANKS, NTILE])
        choice = sb("choice", [P, RANKS, NTILE, E])
        choice_bf = sb("choice_bf", [P, RANKS, NTILE, E], BF16)
        before = sb("before", [P, RANKS, E, NTILE])
        place = sb("place", [P, RANKS, NTILE, E])
        pos = sb("pos", [P, RANKS, NTILE])
        hi, lo = L.hi, L.lo
        ps_rank = ps("ps_rank", [P, RANKS, NTILE, E])
        ps_total = ps("ps_total", [P, RANKS, NTILE, E])
        ps_found = ps("ps_found", [P, 3 * NBLK])

        step = sem("vector_step")
        shifted = sem("logits_shifted")
        raised = sem("exponentials_ready")
        chosen = sem("choices_ready")
        counted = sem("counts_ready")
        block = ctx.enter_context(nc.Block(no_gpsimd_drain=True))

        def over_experts(a):
            return a.broadcast_to([P, NTILE, E]) if a.shape[1] == NTILE else a

        @block.vector
        def _(dve):
            V = nc.vector
            link = Chain(dve, step)
            each = [P, NTILE, E]

            def wide(a):
                return a.rearrange("p (t o) -> p t o", o=1).broadcast_to(each)

            def ramp(n):
                return g.c(n).rearrange("p (o e) -> p o e", o=1).broadcast_to(each)
            link(V.tensor_reduce(row[:, :], g.logits[:, :, :], AX, ALU.max))
            V.tensor_tensor(scores[:, :, :], g.logits[:, :, :], wide(row[:, :]), ALU.subtract).then_inc(shifted, 1)
            dve.wait_ge(raised, 1)
            link(V.tensor_reduce(row[:, :], work[:, :, :], AX, ALU.add))
            link(V.reciprocal(row[:, :], row[:, :]))
            link(V.tensor_tensor(scores[:, :, :], work[:, :, :], wide(row[:, :]), ALU.mult))
            for k in range(RANKS):
                link(V.tensor_reduce(best[:, k, :], scores[:, :, :], AX, ALU.max))
                link(V.tensor_tensor(work[:, :, :], scores[:, :, :], wide(best[:, k, :]), ALU.is_equal))
                link(V.tensor_tensor(work[:, :, :], work[:, :, :], ramp("tieorder"), ALU.mult))
                link(V.tensor_reduce(row[:, :], work[:, :, :], AX, ALU.max))
                link(V.tensor_tensor(choice[:, k], work[:, :, :], wide(row[:, :]), ALU.is_equal))
                if k == 0:
                    link(V.scalar_tensor_tensor(scores[:, :, :], choice[:, k], -4.0, scores[:, :, :], ALU.mult, ALU.add))
            V.tensor_copy(choice_bf[:, :, :, :], choice[:, :, :, :]).then_inc(chosen, 1)
            V.memset(before[:, :, :, 0:1], 0.0)
            dve.wait_ge(counted, 1)
            for k in range(RANKS):
                ins = V.tensor_copy(before[:, k, :, 1:NTILE], ps_total[:, k, 0:NTILE - 1, :].rearrange("p t e -> p e t"))
            link(ins)
            flat = before[:, :, :, :].rearrange("p k e t -> p (k e t)")
            link(V.tensor_tensor_scan(flat, g.c("segment"), flat, 0.0, ALU.mult, ALU.add))
            for k in range(RANKS):
                ins = V.tensor_tensor(place[:, k], ps_rank[:, k], before[:, k].rearrange("p e t -> p t e"), ALU.add)
            link(ins)
            link(V.tensor_tensor(place[:, :, :, :], place[:, :, :, :], choice[:, :, :, :], ALU.mult))
            link(V.tensor_reduce(pos[:, :, :], place[:, :, :, :], AX, ALU.add))
            for k in range(RANKS):
                ins = V.tensor_tensor(place[:, k], choice[:, k], ramp("expert"), ALU.mult)
            link(ins)
            link(V.tensor_reduce(hi[:, :, :], place[:, :, :, :], AX, ALU.add))
            link(V.tensor_scalar(lo[:, :, :], pos[:, :, :], float(CAP), 0.5, ALU.is_lt, ALU.mult))
            link(V.tensor_tensor(g.weight[:, :, :], best[:, :, :], lo[:, :, :], ALU.mult))
            link(V.tensor_scalar(lo[:, :, :], pos[:, :, :], float(P), None, ALU.is_ge))
            for m in range(2, NJ):
                link(V.scalar_tensor_tensor(lo[:, :, :], pos[:, :, :], float(m * P), lo[:, :, :], ALU.is_ge, ALU.add))
            link(V.scalar_tensor_tensor(hi[:, :, :], hi[:, :, :], float(NJ), lo[:, :, :], ALU.mult, ALU.add))
            link(V.scalar_tensor_tensor(lo[:, :, :], lo[:, :, :], -float(P), pos[:, :, :], ALU.mult, ALU.add))
            L.onehots(nc, g, dve, 0)
            L.indices(nc, g, dve, 0, ps_found[:, :])

        @block.scalar
        def _(act):
            act.wait_ge(shifted, 1)
            nc.scalar.activation(work[:, :, :], scores[:, :, :], ACT.Exp).then_inc(raised, 1)
            L.row_numbers(nc, g, act, 0)

        @block.tensor
        def _(pe):
            pe.wait_ge(chosen, 1)
            c = choice_bf[:, :, :, :].rearrange("p k t e -> p (k t e)")
            nc.tensor.matmul(ps_rank[:, :, :, :].rearrange("p k t e -> p (k t e)"), g.tri[:, :], c, start=True, stop=True)
            nc.tensor.matmul(ps_total[:, :, :, :].rearrange("p k t e -> p (k t e)"), g.ones[:, :], c,
                             start=True, stop=True).then_inc(counted, 1)
            L.products(nc, pe, 0, ps_found[:, :])


class Run:

    def __init__(self, base, m):
        self.base, self.m = base, m

    def exists(self):
        return self.m is not None or 0 <= self.base < NRUN

    def at(self, offset=0, scale=1):
        v = scale * (self.base + offset)
        return v if self.m is None else self.m * (4 * scale) + v

    def uses(self, buffers, scale=1):
        v = scale * (self.base // buffers)
        return v if self.m is None else self.m * (4 // buffers * scale) + v


def expert_phase(nc, g, name, w1, w2, L, out=None):
    with ExitStack() as ctx:
        def sb(n, shape, dt=F32):
            return ctx.enter_context(nc.sbuf_tensor(f"{name}_{n}", shape, dt))

        def ps(n, shape):
            return ctx.enter_context(nc.psum_tensor(f"{name}_{n}", shape, F32))

        def sem(n):
            return ctx.enter_context(nc.semaphore(f"{name}_{n}"))

        w1s = sb("w1", [P, 4, FF])
        w2s = sb("w2", [P, 4, NF, D])
        xT = sb("xT", [P, 2, CAP])
        hT = sb("hT", [P, 2, NF, CAP])
        y = sb("y", [P, 2, NJ, D])
        take = sb("take_now", [P, 4, NJ], U32)
        put = sb("put_now", [P, 2, NJ], U32)
        rows = sb("combined_rows", [P, NTILE, D])
        ps_in = [ps(f"ps_in{u}", [P, CAP]) for u in range(2)]
        ps_h = [ps(f"ps_h{f}", [P, CAP]) for f in range(NF)]
        ps_y = [ps(f"ps_y{u}", [P, NJ, D]) for u in range(2)]

        w_loaded = [sem(f"weights_loaded{u}") for u in range(4)]
        gathered = [sem(f"rows_gathered{u}") for u in range(4)]
        scattered = [sem(f"rows_scattered{u}") for u in range(2)]
        indexed = sem("indices_ready")
        in_done = sem("rows_transposed")
        xT_ready = sem("xT_ready")
        up_done = sem("up_done")
        h_ready = sem("h_ready")
        down_done = sem("down_done")
        y_ready = sem("y_ready")
        biased = sem("bias_added")
        returned = [sem(f"rank_rows_loaded{q}") for q in range(4)]
        added = sem("rank0_added")
        summed = sem("group_summed")
        stored = sem("group_stored")
        block = ctx.enter_context(nc.Block())
        QT = NTILE // 4
        ps_found = ps_y[1][:, 0, 0:3 * NBLK]

        def wait(eng, s, value):
            if not (isinstance(value, int) and value <= 0):
                eng.wait_ge(s, value)

        def steps(eng, emit):
            def at(i, m=None):
                return lambda ahead: Run(i + ahead, m)
            for i in range(-2, 3):
                emit(i, at(i))
            with eng.Fori(0, 2) as m:
                for i in range(3, 7):
                    emit(None, at(i, m))
            for i in range(11, NRUN + 1):
                emit(i, at(i))

        @block.sync
        def _(sp):
            def load(r, u, first):
                e = r % E if isinstance(r, int) else r & (E - 1)
                if not first:
                    sp.wait_ge(down_done, r - 3)
                    sp.sem_inc(g.passed, 1)
                sp.dma_start(w1s[:, u, :], w1[bass.ds(e, 1), :, :].rearrange("o c f -> c (o f)")).then_inc(w_loaded[u], 16)
                sp.dma_start(w2s[:, u, :, :], w2[bass.ds(e, 1), :, :].rearrange("o (b f) c -> f (o b) c", b=NF)).then_inc(w_loaded[u], 16)

            def rank_rows(k):
                for q in range(4):
                    sp.dma_start(rows[:, QT * q:QT * (q + 1), :],
                                 g.y_dram[k * T + QT * q * P:k * T + QT * (q + 1) * P, :].rearrange("(n p) d -> p n d", p=P)
                                 ).then_inc(returned[q], 16)
            for r in range(4):
                load(r, r, True)
            with sp.Fori(1, 3) as m:
                for u in range(4):
                    load(4 * m + u, u, False)
            for r in range(12, 14):
                load(r, r % 4, False)
            for u in range(2):
                sp.wait_ge(scattered[u], E // 2 * NJ * 16)
            rank_rows(0)
            for r in range(14, NRUN):
                load(r, r % 4, False)
            sp.wait_ge(added, 4)
            for u in range(2):
                sp.wait_ge(scattered[u], NRUN // 2 * NJ * 16)
            rank_rows(1)
            if out is not None:
                for q in range(4):
                    sp.wait_ge(summed, q + 1)
                    sp.dma_start(out[QT * q:QT * (q + 1), :, :].rearrange("n p d -> p n d"),
                                 g.x[:, QT * q:QT * (q + 1), :]).then_inc(stored, 16)
                sp.wait_ge(stored, 16 * 4)

        AHEAD = 5

        @block.gpsimd
        def _(pool):
            def gather(r):
                u = r.base % 4
                wait(pool, in_done, r.at(-3))
                nc.gpsimd.tensor_copy(take[:, u, :], g.take[:, bass.ds(r.at(0, NJ), NJ)]).then_inc(indexed, 1)
                pool.wait_ge(indexed, r.at(1) + max(r.at(-6), 0) if r.m is None else r.at(1) + r.at(-6))
                pool.sem_inc(g.passed, 1)
                for j in range(NJ):
                    nc.gpsimd.indirect_dma_start(out=g.xe[:, u, j, :], out_offset=None, in_=g.xn_rows,
                                                 in_offset=bass.IndirectOffsetOnAxis(ap=take[:, u, j:j + 1], axis=0),
                                                 bounds_check=T - 1, oob_is_err=False).then_inc(gathered[u], 16)

            def scatter(r):
                u = r.base % 2
                wait(pool, scattered[u], r.uses(2, NJ * 16))
                nc.gpsimd.tensor_copy(put[:, u, :], g.put[:, bass.ds(r.at(0, NJ), NJ)]).then_inc(indexed, 1)
                pool.wait_ge(indexed, r.at(1) + min(r.at(7), NRUN) if r.m is None else r.at(1) + r.at(7))
                pool.wait_ge(y_ready, r.at(1))
                pool.sem_inc(g.passed, 1)
                for j in range(NJ):
                    nc.gpsimd.indirect_dma_start(out=g.y_dram, out_offset=bass.IndirectOffsetOnAxis(ap=put[:, u, j:j + 1], axis=0),
                                                 in_=y[:, u, j, :], in_offset=None,
                                                 bounds_check=RANKS * T - 1, oob_is_err=False).then_inc(scattered[u], 16)

            def emit(i, run):
                if i == E - AHEAD:
                    pool.wait_ge(L.indices_known, 2)
                if run(AHEAD).exists():
                    gather(run(AHEAD))
                if run(-1).exists():
                    scatter(run(-1))
            pool.wait_ge(g.cleared, 8 * 16)
            for r in range(AHEAD - 2):
                gather(Run(r, None))
            steps(pool, emit)
            for u in range(2):
                pool.wait_ge(scattered[u], NRUN // 2 * NJ * 16)

        @block.tensor
        def _(pe):
            def transpose_in(r):
                u = r.base % 2
                pe.wait_ge(gathered[r.base % 4], r.uses(4, NJ * 16) + NJ * 16)
                wait(pe, xT_ready, r.at(-1))
                for j in range(NJ):
                    ins = nc.tensor.transpose(ps_in[u][:, j * P:(j + 1) * P], g.xe[:, r.base % 4, j, :], g.c("ident"))
                ins.then_inc(in_done, 1)

            def up(r):
                u = r.base % 2
                pe.wait_ge(w_loaded[r.base % 4], r.uses(4, 32) + 32)
                pe.wait_ge(xT_ready, r.at(1))
                for f in range(NF):
                    if r.m is not None or r.base > 0:
                        pe.wait_ge(h_ready, r.at(-1, NF) + f + 1)
                    nc.tensor.matmul(ps_h[f][:, :], w1s[:, r.base % 4, f * P:(f + 1) * P], xT[:, u, :],
                                     start=True, stop=True).then_inc(up_done, 1)

            def down(r):
                u = r.base % 2
                wait(pe, y_ready, r.at(-1))
                pe.wait_ge(h_ready, r.at(1, NF))
                for j in range(NJ):
                    for f in range(NF):
                        ins = nc.tensor.matmul(ps_y[u][:, j, :], hT[:, u, f, j * P:(j + 1) * P], w2s[:, r.base % 4, f, :],
                                               start=(f == 0), stop=(f == NF - 1))
                ins.then_inc(down_done, 1)

            def emit(i, run):
                if run(2).exists():
                    transpose_in(run(2))
                if run(1).exists():
                    up(run(1))
                if run(0).exists():
                    down(run(0))
            L.products(nc, pe, 1, ps_found)
            steps(pe, emit)

        @block.scalar
        def _(act):
            def emit(i, run):
                r = run(1)
                if not r.exists():
                    return
                for f in range(NF):
                    act.wait_ge(up_done, r.at(0, NF) + f + 1)
                    if f == 0:
                        wait(act, down_done, r.at(-1))
                    nc.scalar.activation(hT[:, r.base % 2, f, :], ps_h[f][:, :], ACT.Gelu_apprx_tanh).then_inc(h_ready, 1)
            L.row_numbers(nc, g, act, 1)
            steps(act, emit)

        @block.vector
        def _(dve):
            def weighted(k, q):
                dve.wait_ge(returned[q], 16 * (k + 1))
                if k == 1:
                    dve.wait_ge(added, q + 1)
                for t in range(QT * q, QT * (q + 1)):
                    ins = nc.vector.scalar_tensor_tensor(g.x[:, t, :], rows[:, t, :], g.weight[:, k, t:t + 1],
                                                         g.x[:, t, :], ALU.mult, ALU.add)
                ins.then_inc(added if k == 0 else summed, 1)

            def emit(i, run):
                if run(2).exists():
                    r = run(2)
                    dve.wait_ge(in_done, r.at(1))
                    wait(dve, up_done, r.at(-1, NF))
                    nc.vector.tensor_copy(xT[:, r.base % 2, :], ps_in[r.base % 2][:, :]).then_inc(xT_ready, 1)
                if run(0).exists():
                    r = run(0)
                    u = r.base % 2
                    dve.wait_ge(down_done, r.at(1))
                    wait(dve, scattered[u], r.uses(2, NJ * 16))
                    nc.vector.tensor_copy(y[:, u, :, :], ps_y[u][:, :, :]).then_inc(y_ready, 1)
                if i == 0:
                    nc.vector.tensor_tensor(g.x[:, :, :], g.x[:, :, :],
                                            g.bias[:, :].rearrange("p (o d) -> p o d", o=1).broadcast_to([P, NTILE, D]),
                                            ALU.add).then_inc(biased, 1)
                if i is not None and 13 <= i <= 16:
                    dve.wait_ge(biased, 1)
                    weighted(0, i - 13)
            L.onehots(nc, g, dve, 1)
            L.indices(nc, g, dve, 1, ps_found)
            steps(dve, emit)
            for q in range(4):
                weighted(1, q)
            dve.wait_ge(summed, 4)


def ffn(nc, g, name, w1, w2, out=None, load=None):
    with ExitStack() as ctx:
        g.xe = ctx.enter_context(nc.sbuf_tensor(f"{name}_expert_rows", [P, 4, NJ, D], F32))
        L = SlotList(nc, ctx, f"{name}_list")
        with ExitStack() as inner:
            g.logits = inner.enter_context(nc.psum_tensor(f"{name}_logits", [P, NTILE, E], F32))
            norm_phase(nc, g, f"{name}_norm", True, load)
            route_phase(nc, g, f"{name}_route", L)
        expert_phase(nc, g, f"{name}_experts", w1, w2, L, out)


C = 4
BT = 64
NBK = NT // BT
NCH = BT // C
GR = NB * NCH
PASSES = 12


def attention_core(nc, g, W):
    with ExitStack() as ctx:
        def sb(n, shape, dt=F32):
            return ctx.enter_context(nc.sbuf_tensor(f"att_{n}", shape, dt))

        def ps(n, shape):
            return ctx.enter_context(nc.psum_tensor(f"att_{n}", shape, F32))

        def sem(n):
            return ctx.enter_context(nc.semaphore(f"att_{n}"))

        blk, two = [P, GR, C], [P, 2, GR, C]
        z16 = sb("low_rank", [16, 2, NB * BT])
        sig, sg, kraw, k2 = (sb(n, blk) for n in ("sig_k_or_q", "sig_gamma", "k_raw", "k_square_or_norm"))
        kinv = k2
        k, f, q, a = (sb(n, two) for n in ("k", "forget", "q", "a"))
        kds = [None] + [sb(f"k_decayed{d}", [P, GR, C - d]) for d in range(1, C)]
        pa = [None] + [sb(f"a_k{d}", [P, GR, C - d]) for d in range(1, C)]
        pb = [sb(f"q_k{d}", [P, GR, C - d]) for d in range(C)]
        A = sb("A", [P, GR, C * C])
        B = sb("B", [P, GR, C * C])
        tmp = sb("solve_term", [P, 2, GR, C - 1])
        tmp2 = sb("output_term", [P, 2, GR, C - 1])
        XY = sb("XY", [P, 2, 2, GR, C])
        ZO = sb("ZO", [P, 2, 2, GR, C])
        Xm = sb("X_masked", [P, 2, HD, NB * BT])
        Kbar = sb("K_bar", two)
        decay = sb("decay", two)
        gate = sb("out_gate", two)
        hist = sb("states", [P, 2, NCH, HD, NB])
        Es = sb("Y_S", [P, 2, HD, NB, C])
        R = sb("K_u", [P, HD, NB, C + 1])
        E2 = sb("Z_S", [P, 2, HD, NB, 4 * C])
        p1 = [ps(f"ps_stage1_{n}", [P, NB * BT]) for n in range(2)]
        p2 = [ps(f"ps_stage2_{n}", [P, NB * BT]) for n in range(2)]
        pc = [ps(f"ps_u{n}", [P, HD, NB, 2 * C]) for n in range(2)]
        po = ps("ps_o", [P, NB, BT])

        pass1 = sem("stage1_passes")
        act1 = sem("stage1_read_by_scalar")
        sig_done = sem("sigmoids_of_k_and_q")
        dve1 = sem("stage1_read_by_vector")
        k2_ready = sem("k_square_ready")
        norm_step = sem("norm_step")
        k_ready = sem("k_and_a_ready")
        pass2 = sem("stage2_passes")
        act2 = sem("stage2_read_by_scalar")
        pool_step = sem("pool_step")
        pa_ready = sem("a_k_products_ready")
        pb_ready = sem("q_k_products_ready")
        Y_ready = sem("Y_start_ready")
        A_ready = sem("A_ready")
        Kbar_ready = sem("K_bar_ready")
        solve_step = sem("solve_step")
        solved = sem("X_Y_solved")
        masked = sem("X_masked_ready")
        ZO_ready = sem("Z_O_ready")
        spread = sem("X_in_bank")
        E_ready = sem("Y_S_ready")
        u_ready = sem("u_ready")
        R_ready = sem("K_u_ready")
        state = sem("states_ready")
        E2_ready = sem("Z_S_ready")
        o_done = sem("o_collected")
        o_read = sem("o_read")
        o_ready = sem("o_gated")
        zero = sem("state_zeroed")
        block = ctx.enter_context(nc.Block(no_gpsimd_drain=True))

        def flat(t):
            return t.rearrange("p a b -> p (a b)")

        def wait(eng, s, value):
            if not (isinstance(value, int) and value <= 0):
                eng.wait_ge(s, value)

        def bodies(eng, emit):
            emit(-2, 0, False, False, True)
            emit(-1, 1, False, True, True)
            emit(0, 0, True, True, True)
            with eng.Fori(0, 2) as m:
                emit(2 * m + 1, 1, True, True, True)
                emit(2 * m + 2, 0, True, True, True)
            emit(5, 1, True, True, True)
            emit(6, 0, True, True, False)
            emit(7, 1, True, False, False)

        @block.tensor
        def _(pe):
            hs = g.c("headsum")

            def mm(out, w, x, start=True):
                return nc.tensor.matmul(out, w, x, start=start, stop=True, skip_group_check=not start)

            def cols(j):
                return g.xnT[:, :, bass.ds(BT * j, BT)]

            def stage1(j, u, n):
                if n in (0, 3):
                    wait(pe, dve1, 2 * j + (0 if n == 0 else 1))
                else:
                    wait(pe, act1, 4 * j + {1: 0, 2: 1, 4: 2, 5: 3}[n])
                bank = p1[n % 2]
                if n == 2:
                    wait(pe, act1, 4 * j + 1)
                    ins = mm(bank[:, :], W.f2, z16[:, u, :])
                elif n == 5:
                    pe.wait_ge(k2_ready, j + 1)
                    ins = mm(bank[:, :], hs, flat(k2[:, :, :]))
                else:
                    w, m = {0: (W.low, 16), 1: (W.k, P), 3: (W.gamma, P), 4: (W.q, P)}[n]
                    ins = mm(bank[0:m, :].rearrange("p (b t) -> p b t", b=NB), w, cols(j))
                ins.then_inc(pass1, 1)

            def stage2(j, u, n):
                wait(pe, act2, 6 * j + n - 1)
                bank = p2[n % 2]
                if n == 0:
                    ins = mm(bank[:, :].rearrange("p (b t) -> p b t", b=NB), W.v, cols(j))
                elif n == 1:
                    pe.wait_ge(pa_ready, j + 1)
                    mm(bank[:, 0:3 * GR], hs, flat(pa[1][:, :, :]))
                    ins = mm(bank[:, 3 * GR:4 * GR], hs, flat(pa[3][:, :, :]))
                elif n == 2:
                    mm(bank[:, 0:2 * GR], hs, flat(pa[2][:, :, :]))
                    pe.wait_ge(pb_ready, j + 1)
                    ins = mm(bank[:, 2 * GR:4 * GR], hs, flat(pb[2][:, :, :]))
                elif n == 3:
                    ins = mm(bank[:, :], hs, flat(pb[0][:, :, :]))
                elif n == 4:
                    mm(bank[:, 0:3 * GR], hs, flat(pb[1][:, :, :]))
                    ins = mm(bank[:, 3 * GR:4 * GR], hs, flat(pb[3][:, :, :]))
                else:
                    ins = mm(bank[:, :], W.og2, z16[:, u, :])
                ins.then_inc(pass2, 1)

            def put_X(i, u, n):
                wait(pe, R_ready, NCH * i + 2 * n - 2)
                if n == 0:
                    pe.wait_ge(masked, i + 1)
                x = Xm[:, u, :, :].rearrange("p v (b t) -> p (v b) t", b=NB)[:, :, 2 * C * n:2 * C * (n + 1)]
                mm(pc[n % 2][:, :, :, :].rearrange("p v b t -> p (v b) t"), hs, x).then_inc(spread, 1)

            def add_YS(i, c):
                pe.wait_ge(E_ready, NCH * i + c + 1)
                h = c % 2
                out = pc[(c // 2) % 2][:, :, :, C * h:C * h + C].rearrange("p v b t -> p (v b) t")
                mm(out, hs, Es[:, c % 2].rearrange("p v b t -> p (v b) t"), start=False).then_inc(u_ready, 1)

            def collect(i, s):
                pe.wait_ge(E2_ready, 4 * i + s + 1)
                if s == 0:
                    wait(pe, o_read, i)
                for v in range(HD):
                    lo = COL["collect"][0] + v * P
                    ins = mm(po[:, :, 4 * C * s:4 * C * (s + 1)], g.const[:, lo:lo + P], E2[:, s % 2, v], start=(v == 0))
                ins.then_inc(o_done, 1)

            AT2 = {0: (0,), 3: (1,), 4: (2,), 6: (3,), 7: (4,), 11: (5,)}
            AT1 = {1: (0,), 3: (1,), 7: (2,), 8: (3,), 10: (4,), 12: (5,)}

            def emit(i, u, chain, s2, s1):
                if chain:
                    put_X(i, u, 0)
                for c in range(NCH):
                    if chain:
                        add_YS(i, c)
                        if c % 2 == 0 and c < NCH - 2:
                            put_X(i, u, c // 2 + 1)
                        if c in (2, 5) and not (isinstance(i, int) and i == 0):
                            collect(i - 1, 2 + c // 5)
                        if c in (9, 13):
                            collect(i, c // 13)
                    if s1:
                        for n in AT1.get(c, ()):
                            stage1(i + 2, u, n)
                    if s2:
                        for n in AT2.get(c, ()):
                            stage2(i + 1, 1 - u, n)
            bodies(pe, emit)
            collect(NBK - 1, 2)
            collect(NBK - 1, 3)

        @block.scalar
        def _(act):
            S = nc.scalar

            def sigmoid(out, j, n, inc):
                act.wait_ge(pass1, 6 * j + n + 1)
                S.activation(out, p1[n % 2][:, :], ACT.Sigmoid).then_inc(inc, 1)

            def spread_out(dst, bank, lo, d):
                n = C - d
                src = bank[:, lo:lo + n * GR].rearrange("p (g t) -> p g t", g=GR)
                last = d + (n - 1) * (C + 1) + 1
                return S.activation(dst[:, :, d:last:C + 1], src, ACT.Copy)

            def emit(i, u, chain, s2, s1):
                j, v = i + 1, 1 - u
                b = i + 2
                if s2:
                    act.wait_ge(pass2, 6 * j + 1)
                    wait(act, ZO_ready, j - 1)
                    S.activation(flat(XY[:, v, 1]), p2[0][:, :], ACT.Copy).then_inc(act2, 1)
                if s1:
                    act.wait_ge(pass1, 6 * b + 1)
                    S.activation(z16[:, u, :], p1[0][0:16, :], ACT.Copy).then_inc(act1, 1)
                    wait(act, dve1, 2 * b)
                    sigmoid(flat(sig[:, :, :]), b, 1, sig_done)
                if s2:
                    act.wait_ge(pass2, 6 * j + 2)
                    wait(act, solved, j)
                    spread_out(A, p2[1], 0, 1)
                    spread_out(A, p2[1], 3 * GR, 3).then_inc(act2, 1)
                    act.wait_ge(pass2, 6 * j + 3)
                    spread_out(A, p2[0], 0, 2).then_inc(A_ready, 1)
                    wait(act, ZO_ready, j)
                    spread_out(B, p2[0], 2 * GR, 2).then_inc(act2, 1)
                if s1:
                    wait(act, pass1, 6 * b)
                    act.wait_ge(dve1, 2 * b + 1)
                    S.activation(flat(k2[:, :, :]), flat(kraw[:, :, :]), ACT.Square).then_inc(k2_ready, 1)
                if s2:
                    act.wait_ge(pass2, 6 * j + 4)
                    spread_out(B, p2[1], 0, 0).then_inc(act2, 1)
                    act.wait_ge(pass2, 6 * j + 5)
                    spread_out(B, p2[0], 0, 1)
                    spread_out(B, p2[0], 3 * GR, 3).then_inc(act2, 1)
                if s1:
                    wait(act, pb_ready, b - 1)
                    sigmoid(flat(f[:, u]), b, 2, act1)
                    wait(act, k_ready, b)
                    sigmoid(flat(sg[:, :, :]), b, 3, act1)
                if s2:
                    wait(act, state, NCH * (j - 1))
                    act.wait_ge(pa_ready, j + 1)
                    for s in range(C):
                        kd = k[:, v] if s == C - 1 else kds[C - 1 - s]
                        last = S.activation(Kbar[:, v, :, s:s + 1], kd[:, :, s:s + 1], ACT.Copy)
                    last.then_inc(Kbar_ready, 1)
                if s1:
                    act.wait_ge(dve1, 2 * b + 1)
                    sigmoid(flat(sig[:, :, :]), b, 4, sig_done)
                if s2:
                    act.wait_ge(solved, j + 1)
                    wait(act, spread, (j - 1) * (NCH // 2))
                    for n in range(HD):
                        last = S.activation(Xm[:, v, n, :], flat(XY[:, v, 1]), ACT.Copy, scale=g.c("delta")[:, n:n + 1])
                    last.then_inc(masked, 1)
                    act.wait_ge(pass2, 6 * j + 6)
                    wait(act, o_ready, j - 1)
                    S.activation(flat(gate[:, v]), p2[1][:, :], ACT.Sigmoid).then_inc(act2, 1)
                if s1:
                    act.wait_ge(pass1, 6 * b + 6)
                    S.activation(flat(kinv[:, :, :]), p1[1][:, :], ACT.Sqrt).then_inc(act1, 1)
            bodies(act, emit)

        @block.gpsimd
        def _(pool):
            G = nc.gpsimd
            link = Chain(pool, pool_step)
            STEPS = 14

            def products_a(j, u):
                link.begin(STEPS * j)
                pool.wait_ge(k_ready, j + 1)
                wait(pool, pass2, 6 * j - 1)
                wait(pool, Kbar_ready, j)
                kd = [k[:, u]] + [t[:, :, :] for t in kds[1:]]
                for d in range(1, C):
                    link(G.tensor_tensor(kd[d], kd[d - 1][:, :, 0:C - d], f[:, u, :, d:C], ALU.mult))
                for d in range(1, C):
                    last = G.tensor_tensor(pa[d][:, :, :], a[:, u, :, d:C], kd[d], ALU.mult)
                last.then_inc(pa_ready, 1)
                wait(pool, state, NCH * (j - 1))
                pool.sem_inc(g.passed, 1)
                link(G.tensor_copy(decay[:, u, :, 0:1], f[:, u, :, 0:1]))
                for t in range(1, C):
                    link(G.tensor_tensor(decay[:, u, :, t:t + 1], decay[:, u, :, t - 1:t], f[:, u, :, t:t + 1], ALU.mult))
                G.tensor_tensor(XY[:, u, 0], a[:, u], decay[:, u], ALU.mult).then_inc(Y_ready, 1)

            def products_b(j, u):
                kd = [k[:, u]] + [t[:, :, :] for t in kds[1:]]
                pool.wait_ge(dve1, 2 * j + 2)
                for d in range(C):
                    last = G.tensor_tensor(pb[d][:, :, :], q[:, u, :, d:C], kd[d], ALU.mult)
                last.then_inc(pb_ready, 1)

            def outputs(j, u):
                pool.wait_ge(solved, j + 1)
                pool.wait_ge(act2, 6 * j + 5)
                wait(pool, o_read, j - 1)
                link(G.tensor_tensor(q[:, u], q[:, u], decay[:, u], ALU.mult))
                for s in range(C):
                    n = C - s
                    b4 = B[:, :, :].rearrange("p g (s t) -> p g s t", s=C)[:, :, s, s:C]
                    for h in range(2):
                        x = XY[:, u, h, :, s:s + 1].broadcast_to([P, GR, n])
                        last = G.tensor_tensor((ZO[:, u, h] if s == 0 else tmp2[:, h, :, 0:n]), x, b4, ALU.mult)
                    if s:
                        link(last)
                        last = G.tensor_tensor(ZO[:, u, :, :, s:C], ZO[:, u, :, :, s:C], tmp2[:, :, :, 0:n], ALU.add)
                    if s < C - 1 and s:
                        link(last)
                link(last)
                G.tensor_tensor(ZO[:, u, 0], ZO[:, u, 0], q[:, u], ALU.add).then_inc(ZO_ready, 1)

            def z_state(i, u, s):
                if s == 0:
                    pool.wait_ge(ZO_ready, i + 1)
                wait(pool, o_done, 4 * i + s - 1)
                for c in range(4 * s, 4 * s + 4):
                    wait(pool, state, NCH * i + c)
                    z = ZO[:, u, 0].rearrange("p (b n) t -> p b n t", b=NB)[:, :, c, :]
                    z = z.rearrange("p (o b) t -> p o b t", o=1).broadcast_to([P, HD, NB, C])
                    st = hist[:, u, c].rearrange("p v (b o) -> p v b o", o=1).broadcast_to([P, HD, NB, C])
                    last = G.tensor_tensor(E2[:, s % 2, :, :, C * (c % 4):C * (c % 4 + 1)], z, st, ALU.mult)
                last.then_inc(E2_ready, 1)

            def emit(i, u, chain, s2, s1):
                if s2:
                    products_a(i + 1, 1 - u)
                if chain and not (isinstance(i, int) and i == 0):
                    z_state(i - 1, 1 - u, 3)
                if s2:
                    products_b(i + 1, 1 - u)
                if chain:
                    z_state(i, u, 0)
                    z_state(i, u, 1)
                if s2:
                    outputs(i + 1, 1 - u)
                if chain:
                    z_state(i, u, 2)
            pool.wait_ge(zero, 1)
            bodies(pool, emit)
            z_state(NBK - 1, 1, 3)

        @block.vector
        def _(dve):
            V = nc.vector
            norm_link = Chain(dve, norm_step)
            solve_link = Chain(dve, solve_step)

            def as3(bank):
                return bank[:, :].rearrange("p (g t) -> p g t", t=C)

            def k_product(j):
                dve.wait_ge(sig_done, 2 * j + 1)
                wait(dve, k_ready, j)
                wait(dve, k2_ready, j)
                V.tensor_tensor(kraw[:, :, :], as3(p1[1]), sig[:, :, :], ALU.mult).then_inc(dve1, 1)

            def q_product(j, u):
                dve.wait_ge(sig_done, 2 * j + 2)
                wait(dve, ZO_ready, j - 1)
                V.tensor_tensor(q[:, u], as3(p1[0]), sig[:, :, :], ALU.mult).then_inc(dve1, 1)

            def k_norm(j, u):
                norm_link.begin(4 * j)
                dve.wait_ge(act1, 4 * j + 4)
                wait(dve, pb_ready, j - 1)
                wait(dve, Kbar_ready, j - 1)
                norm_link(V.tensor_scalar(kinv[:, :, :], kinv[:, :, :], 1e-12, None, ALU.max))
                norm_link(V.reciprocal(kinv[:, :, :], kinv[:, :, :]))
                norm_link(V.tensor_tensor(k[:, u], kraw[:, :, :], kinv[:, :, :], ALU.mult))
                norm_link(V.scalar_tensor_tensor(a[:, u], k[:, u], -1.0, sg[:, :, :], ALU.mult, ALU.mult))
                V.tensor_tensor(a[:, u], a[:, u], f[:, u], ALU.mult).then_inc(k_ready, 1)

            def solve(j, u):
                solve_link.begin(5 * j)
                dve.wait_ge(A_ready, j + 1)
                dve.wait_ge(Y_ready, j + 1)
                for s in range(C - 1):
                    n = C - 1 - s
                    a4 = A[:, :, :].rearrange("p g (s t) -> p g s t", s=C)[:, :, s, s + 1:C]
                    for h in range(2):
                        x = XY[:, u, h, :, s:s + 1].broadcast_to([P, GR, n])
                        ins = V.tensor_tensor(tmp[:, h, :, 0:n], x, a4, ALU.mult)
                    solve_link(ins)
                    ins = V.tensor_tensor(XY[:, u, :, :, s + 1:C], XY[:, u, :, :, s + 1:C], tmp[:, :, :, 0:n], ALU.add)
                    if s < C - 2:
                        solve_link(ins)
                ins.then_inc(solved, 1)

            def chunk(i, u, c):
                each = [P, HD, NB, C]
                S4 = hist[:, u, c].rearrange("p v (b o) -> p v b o", o=1)

                def part(t):
                    t = t.rearrange("p (b n) t -> p b n t", b=NB)[:, :, c, :]
                    return t.rearrange("p (o b) t -> p o b t", o=1)
                if c == 0:
                    dve.wait_ge(solved, i + 1)
                    dve.wait_ge(Kbar_ready, i + 1)
                wait(dve, state, NCH * i + c)
                V.tensor_tensor(Es[:, c % 2], part(XY[:, u, 0]).broadcast_to(each), S4.broadcast_to(each), ALU.mult).then_inc(E_ready, 1)
                V.tensor_tensor(R[:, :, :, C:C + 1], part(decay[:, u])[:, :, :, C - 1:C].broadcast_to([P, HD, NB, 1]), S4, ALU.mult)
                dve.wait_ge(u_ready, NCH * i + c + 1)
                V.tensor_tensor(R[:, :, :, 0:C], pc[(c // 2) % 2][:, :, :, C * (c % 2):C * (c % 2) + C],
                                part(Kbar[:, u]).broadcast_to(each), ALU.mult).then_inc(R_ready, 1)
                dve.wait_ge(R_ready, NCH * i + c + 1)
                if c < NCH - 1:
                    dst = hist[:, u, c + 1]
                else:
                    dst = hist[:, 1 - u, 0]
                    wait(dve, E2_ready, 4 * i)
                V.tensor_reduce(dst, R[:, :, :, :], AX, ALU.add).then_inc(state, 1)

            def finish(i, u):
                dve.wait_ge(o_done, 4 * i + 4)
                out = g.oT[:, :, bass.ds(BT * i, BT)]
                V.tensor_tensor(out, po[:, :, :], ZO[:, u, 1].rearrange("p (b n) t -> p b (n t)", b=NB), ALU.add).then_inc(o_read, 1)
                dve.wait_ge(o_read, i + 1)
                dve.wait_ge(act2, 6 * i + 6)
                V.tensor_tensor(out, out, gate[:, u].rearrange("p (b n) t -> p b (n t)", b=NB), ALU.mult).then_inc(o_ready, 1)

            def emit(i, u, chain, s2, s1):
                for c in range(NCH):
                    if chain:
                        chunk(i, u, c)
                        if c == 8 and not (isinstance(i, int) and i == 0):
                            finish(i - 1, 1 - u)
                    if s1 and c == 5:
                        k_product(i + 2)
                    if s2 and c == 9:
                        solve(i + 1, 1 - u)
                    if s1 and c == 12:
                        q_product(i + 2, u)
                    if s1 and c == 15:
                        k_norm(i + 2, u)

            V.memset(hist[:, 0, 0], 0.0).then_inc(zero, 1)
            dve.wait_ge(zero, 1)
            bodies(dve, emit)
            finish(NBK - 1, 1)
            dve.wait_ge(o_ready, NBK)


def rsqrt_of_stats(nc, dve, link, stats, w, var_ready, root_ready):
    V = nc.vector
    mean, dmean, m2, var, root, quot, scale = (w[:, i, :] for i in range(7))
    a = [stats[:, :, k] for k in range(6)]
    V.tensor_tensor(mean, a[1], a[4], ALU.add)
    V.tensor_tensor(dmean, a[1], a[4], ALU.subtract)
    link(V.tensor_tensor(m2, a[2], a[5], ALU.add))
    link(V.tensor_tensor(dmean, dmean, dmean, ALU.mult))
    link(V.tensor_scalar(dmean, dmean, 0.25, 1e-5, ALU.mult, ALU.add))
    V.tensor_scalar(mean, mean, 0.5, None, ALU.mult)
    V.scalar_tensor_tensor(var, m2, 1.0 / D, dmean, ALU.mult, ALU.add).then_inc(var_ready, 1)
    dve.wait_ge(root_ready, 1)
    link(V.reciprocal(quot, root))
    link(V.tensor_tensor(quot, quot, var, ALU.mult))
    link(V.tensor_tensor(root, root, quot, ALU.add))
    link(V.reciprocal(scale, root))
    link(V.tensor_scalar(scale, scale, 2.0, None, ALU.mult))


def attention_weights(nc, g, W, Wq, Wk, Wv, Wgamma, Wf1, Wf2, Wog1, Wog2, norm_w, Wo):
    with ExitStack() as ctx:
        ps_mean = ctx.enter_context(nc.psum_tensor("ps_column_sums", [P, D], F32))
        cleared = ctx.enter_context(nc.semaphore("padding_zeroed"))
        loaded = ctx.enter_context(nc.semaphore("weights_loaded"))
        padded = ctx.enter_context(nc.semaphore("padded_weights_loaded"))
        weighted = ctx.enter_context(nc.semaphore("norm_weighted"))
        summed = ctx.enter_context(nc.semaphore("columns_summed"))
        made = ctx.enter_context(nc.semaphore("attention_weights_made"))
        gsmall = ctx.enter_context(nc.sbuf_tensor("gamma_small", [P, H], F32))
        nw = ctx.enter_context(nc.sbuf_tensor("norm_weight", [P, 1], F32))
        wo = ctx.enter_context(nc.sbuf_tensor("Wo_weighted", [P, D], F32))
        block = ctx.enter_context(nc.Block(no_gpsimd_drain=True))

        @block.sync
        def _(sp):
            for dst, src in ((W.q, Wq), (W.k, Wk), (W.v, Wv), (gsmall[:, :], Wgamma), (W.low[:, 0:HD], Wf1),
                             (W.low[:, HD:2 * HD], Wog1), (wo[:, :], Wo), (nw[:, :], norm_w.rearrange("(p o) -> p o", o=1))):
                sp.dma_start(dst, src[:, :]).then_inc(loaded, 16)
            sp.wait_ge(cleared, 2)
            sp.dma_start(W.f2[0:HD, :], Wf2[:, :]).then_inc(padded, 16)
            sp.dma_start(W.og2[HD:2 * HD, :], Wog2[:, :]).then_inc(padded, 16)
            sp.wait_ge(padded, 32)

        @block.vector
        def _(dve):
            V = nc.vector
            V.memset(W.f2, 0.0).then_inc(cleared, 1)
            V.memset(W.og2, 0.0).then_inc(cleared, 1)
            dve.wait_ge(loaded, 8 * 16)
            V.tensor_copy(W.gamma.rearrange("p (h c) -> p h c", h=H),
                          gsmall[:, :].rearrange("p (h o) -> p h o", o=1).broadcast_to([P, H, HD])).then_inc(made, 1)
            V.tensor_scalar(wo[:, :], wo[:, :], nw[:, :], None, ALU.mult).then_inc(weighted, 1)
            V.tensor_copy(W.out[:, D:2 * D], g.c("ident")).then_inc(made, 1)
            dve.wait_ge(weighted, 1)
            dve.wait_ge(summed, 1)
            V.scalar_tensor_tensor(W.out[:, 0:D], ps_mean[:, :], -1.0 / D, wo[:, :], ALU.mult, ALU.add).then_inc(made, 1)
            dve.wait_ge(made, 3)

        @block.tensor
        def _(pe):
            pe.wait_ge(weighted, 1)
            nc.tensor.matmul(ps_mean[:, :], g.c("ones"), wo[:, :], start=True, stop=True).then_inc(summed, 1)


def attention_output(nc, g, W, out=None):
    with ExitStack() as ctx:
        def sb(n, shape, dt=F32):
            return ctx.enter_context(nc.sbuf_tensor(f"attout_{n}", shape, dt))

        def sem(n):
            return ctx.enter_context(nc.semaphore(f"attout_{n}"))
        stage = sb("stage", [P, 2, 4 * P])
        proj = sb("projected", [P, NTILE, D])
        stats = sb("stats", [P, NTILE, 6])
        w = sb("stat_work", [P, 8, NTILE])
        ps = [ctx.enter_context(nc.psum_tensor(f"attout_ps{n}", [P, 4, 2 * D], F32)) for n in range(2)]
        staged = sem("staged")
        multiplied = sem("projected")
        kept = sem("projection_kept")
        measured = sem("statistics_taken")
        step = sem("vector_step")
        var_ready = sem("variance_ready")
        root_ready = sem("root_ready")
        summed = sem("group_summed")
        stored = sem("group_stored")
        block = ctx.enter_context(nc.Block(no_gpsimd_drain=True))

        def pairs(eng, emit):
            for u in range(2):
                emit(0, u, True)
            with eng.Fori(1, NG // 2) as i:
                for u in range(2):
                    emit(i, u, False)

        @block.scalar
        def _(act):
            def emit(i, u, first):
                if not first:
                    act.wait_ge(multiplied, 2 * i + u - 1)
                nc.scalar.activation(stage[:, u, :], g.oT[:, bass.ds(2 * i + u, 1), :], ACT.Copy).then_inc(staged, 1)
                act.wait_ge(measured, 2 * i + u + 1)
                nc.scalar.activation(proj[:, bass.ds(8 * i + 4 * u, 4), :], ps[u][:, :, 0:D], ACT.Copy).then_inc(kept, 1)
            pairs(act, emit)
            act.wait_ge(var_ready, 1)
            nc.scalar.activation(w[:, 4, :], w[:, 3, :], ACT.Sqrt).then_inc(root_ready, 1)

        @block.tensor
        def _(pe):
            def emit(i, u, first):
                pe.wait_ge(staged, 2 * i + u + 1)
                if not first:
                    pe.wait_ge(kept, 2 * i + u - 1)
                for j in range(4):
                    ins = nc.tensor.matmul(ps[u][:, j, :], stage[:, u, j * P:(j + 1) * P], W.out, start=True, stop=True)
                ins.then_inc(multiplied, 1)
            pairs(pe, emit)

        @block.vector
        def _(dve):
            link = Chain(dve, step)

            def emit(i, u, first):
                dve.wait_ge(multiplied, 2 * i + u + 1)
                for j in range(4):
                    ins = nc.vector.bn_stats(stats[:, bass.ds(8 * i + 4 * u + j, 1), :], ps[u][:, j:j + 1, D:2 * D])
                ins.then_inc(measured, 1)
            pairs(dve, emit)
            dve.wait_ge(measured, NG)
            rsqrt_of_stats(nc, dve, link, stats, w, var_ready, root_ready)
            dve.wait_ge(kept, NG)
            with dve.Fori(0, NG) as i:
                for j in range(4):
                    t = 4 * i + j
                    xt = g.x[:, bass.ds(t, 1), :]
                    ins = nc.vector.scalar_tensor_tensor(xt, proj[:, bass.ds(t, 1), :], w[:, 6, bass.ds(t, 1)], xt, ALU.mult, ALU.add)
                ins.then_inc(summed, 1)
            dve.wait_ge(summed, NG)

        if out is not None:
            @block.sync
            def _(sp):
                with sp.Fori(0, NG) as i:
                    sp.wait_ge(summed, i + 1)
                    sp.dma_start(out[bass.ds(4 * i, 4), :, :].rearrange("n p d -> p n d"), g.x[:, bass.ds(4 * i, 4), :]).then_inc(stored, 16)
                sp.wait_ge(stored, 16 * NG)


def attention(nc, g, Wq, Wk, Wv, Wgamma, Wf1, Wf2, Wog1, Wog2, norm_w, Wo, out=None):
    W = Shared()
    with ExitStack() as ctx:
        def sb(n, shape):
            return ctx.enter_context(nc.sbuf_tensor(f"weight_{n}", shape, F32))
        W.out = sb("out", [P, 2 * D])[:, :]
        g.oT = sb("oT", [P, NB, NT])
        with ExitStack() as inner:
            def sbi(n, shape):
                return inner.enter_context(nc.sbuf_tensor(f"weight_{n}", shape, F32))[:, :]
            W.q, W.k, W.v, W.gamma = (sbi(n, [P, D]) for n in ("q", "k", "v", "gamma"))
            W.low = sbi("low", [P, 2 * HD])
            W.f2, W.og2 = sbi("f2", [2 * HD, D]), sbi("og2", [2 * HD, D])
            g.xnT = inner.enter_context(nc.sbuf_tensor("attention_xnT", [P, NB, NT], F32))
            attention_weights(nc, g, W, Wq, Wk, Wv, Wgamma, Wf1, Wf2, Wog1, Wog2, norm_w, Wo)
            norm_phase(nc, g, "att_norm", False)
            attention_core(nc, g, W)
        attention_output(nc, g, W, out)


def macaron_kernel(nc, x, Wq, Wk, Wv, Wgamma, Wf1, Wf2, Wog1, Wog2, norm_w, Wo, router_w, w1, w2, bias, consts, out):
    g = Shared()
    with ExitStack() as ctx:
        def sb(n, shape, dt=F32):
            return ctx.enter_context(nc.sbuf_tensor(n, shape, dt))
        g.x = sb("x_tokens", [P, NTILE, D])
        g.const = sb("constants", [P, NCONST])
        g.c = lambda n: g.const[:, COL[n][0]:COL[n][1]]
        g.tri = sb("tri_bf", [P, P], BF16)
        g.ones = sb("ones_bf", [P, P], BF16)
        g.router = sb("router", [P, E])
        g.bias = sb("half_bias", [P, D])
        g.weight = sb("rank_weight", [P, RANKS, NTILE])
        g.take = sb("take_rows", [P, RANKS * NBLK], U32)
        g.put = sb("put_rows", [P, RANKS * NBLK], U32)
        g.router_in, g.bias_in = router_w, bias
        xn = nc.dram_tensor("normalised_rows", [NTILE, P, D], F32, kind="Internal").ap()
        g.xn_dram = xn
        g.xn_rows = xn.rearrange("n p d -> (n p) d")
        g.y_dram = nc.dram_tensor("expert_outputs", [RANKS * T, D], F32, kind="Internal").ap()
        out_tiles = out.rearrange("b (n p) d -> (b n) p d", p=P)

        def sem(n):
            return ctx.enter_context(nc.semaphore(n))
        g.x_loaded = [sem(f"x_loaded{q}") for q in range(4)]
        g.consts_loaded = sem("constants_loaded")
        g.copied = sem("small_constants_made")
        g.passed = sem("waits_passed")
        g.zeroed = sem("zero_tile_made")
        g.cleared = sem("expert_rows_cleared")

        ffn(nc, g, "first", w1, w2, load=(x.rearrange("b t d -> (b t) d"), consts))
        attention(nc, g, Wq, Wk, Wv, Wgamma, Wf1, Wf2, Wog1, Wog2, norm_w, Wo)
        ffn(nc, g, "second", w1, w2, out_tiles)


_INS = ["L0_attn_x", "L0_attn_Wq", "L0_attn_Wk", "L0_attn_Wv", "L0_attn_Wgamma", "L0_attn_Wf1", "L0_attn_Wf2",
        "L0_attn_Wog1", "L0_attn_Wog2", "L0_attn_norm_w", "L0_attn_Wo", "L0_ffn_router_w", "L0_ffn_w1", "L0_ffn_w2",
        "L0_ffn_bias"]


def kernel(**inputs):
    import concourse.bacc as _bacc
    from concourse.bass_utils import run_bass_kernel_spmd as _run

    nc = _bacc.Bacc("TRN2", target_bir_lowering=False, num_devices=1)
    arrays, args = {}, []
    for name in _INS:
        a = np.ascontiguousarray(inputs[name])
        arrays[f"in_{name}"] = a
        args.append(nc.dram_tensor(f"in_{name}", a.shape, mybir.dt.from_np(a.dtype), kind="ExternalInput").ap())
    arrays["in_constants"] = constant_table()
    args.append(nc.dram_tensor("in_constants", (P, NCONST), F32, kind="ExternalInput").ap())
    args.append(nc.dram_tensor("out_tokens", (NB, NT, D), F32, kind="ExternalOutput").ap())
    macaron_kernel(nc, *args)
    r = _run(nc, [arrays], core_ids=[0])
    return r.results[0]["out_tokens"]
```

```python
from contextlib import ExitStack

import numpy as np
import concourse.bass as bass
from concourse import mybir
from concourse.alu_op_type import AluOpType as ALU

F32 = mybir.dt.float32
BF16 = mybir.dt.bfloat16
U32 = mybir.dt.uint32
ACT = mybir.ActivationFunctionType
AX = mybir.AxisListType.X

P = 128
D = 128
NB = 8
NT = 512
H, HD = 16, 8
T = NB * NT
NTILE = T // P
NG = NTILE // 4
E = 8
FF = 512
NF = FF // P
CAP = T // E
NJ = CAP // P
RANKS = 2
NBLK = E * NJ
NRUN = RANKS * E
EMPTY = 1 << 20

_off = 0
COL = {}
for _name, _n in (("ident", 128), ("headsum", 128), ("tri", 128), ("ones", 128), ("iota", 128),
                  ("tile", 32), ("tieorder", 8), ("expert", 8), ("segment", 512), ("part", 1), ("delta", 8),
                  ("collect", 1024)):
    COL[_name] = (_off, _off + _n)
    _off += _n
NCONST = _off


def constant_table():
    t = np.zeros((P, NCONST), np.float32)

    def put(name, a):
        lo, hi = COL[name]
        t[:, lo:hi] = np.broadcast_to(a, (P, hi - lo))
    p = np.arange(P)
    put("ident", np.eye(P))
    put("headsum", p[:, None] // HD == p[None, :] // HD)
    put("tri", p[:, None] < p[None, :])
    put("ones", 1.0)
    put("iota", p[None, :])
    put("tile", np.arange(32)[None, :])
    put("tieorder", 8.0 - np.arange(8)[None, :])
    put("expert", np.arange(8)[None, :])
    put("segment", (np.arange(512) % 32 != 0)[None, :])
    put("part", p[:, None])
    put("delta", p[:, None] % HD == np.arange(HD)[None, :])
    same = p[:, None] // HD == p[None, :] // HD
    put("collect", np.concatenate([same & (p[None, :] % HD == v) for v in range(HD)], 1))
    return t


class Chain:

    def __init__(self, eng, sem):
        self.eng, self.sem, self.base, self.n = eng, sem, 0, 0

    def begin(self, base):
        self.base, self.n = base, 0

    def __call__(self, ins):
        self.n += 1
        ins.then_inc(self.sem, 1)
        self.eng.wait_ge(self.sem, self.base + self.n)



class Shared:
    pass


def load_inputs(nc, g, sp, x_in, consts):
    def quarter(n):
        q = NTILE // 4
        sp.dma_start(g.x[:, q * n:q * (n + 1), :],
                     x_in[q * n * P:q * (n + 1) * P, :].rearrange("(n p) d -> p n d", p=P)).then_inc(g.x_loaded[n], 16)
    late = COL["collect"][0]
    quarter(0)
    quarter(1)
    sp.dma_start(g.const[:, 0:late], consts[:, 0:late]).then_inc(g.consts_loaded, 16)
    sp.dma_start(g.router[:, :], g.router_in[:, :]).then_inc(g.consts_loaded, 16)
    quarter(2)
    quarter(3)
    sp.dma_start(g.const[:, late:], consts[:, late:]).then_inc(g.late_consts_loaded, 16)
    sp.dma_start(g.bias[:, :], g.bias_in.rearrange("a b d -> (a b) d").broadcast_to([P, D])).then_inc(g.late_consts_loaded, 16)


def clear_expert_rows(g, act):
    act.wait_ge(g.zeroed, 1)
    rows = RANKS * T // 8
    for q in range(8):
        act.dma_start(g.y_dram[q * rows:(q + 1) * rows, :].rearrange("(p n) d -> p (n d)", p=P),
                      g.xe[:, 0:2, :, :].rearrange("p a j d -> p (a j d)")).then_inc(g.cleared, 16)


def norm_phase(nc, g, name, route, load=None, attended=False):
    with ExitStack() as ctx:
        def sb(n, shape, dt=F32):
            return ctx.enter_context(nc.sbuf_tensor(f"{name}_{n}", shape, dt))

        def sem(n):
            return ctx.enter_context(nc.semaphore(f"{name}_{n}"))

        stats = g.stats
        w = sb("stat_work", [P, 8, NTILE])
        PARTS = 2 if load is not None or attended else 1
        rows = sb("rows", [P, 4, 4, D])
        cols = sb("cols", [P, 2, 4 * P]) if route else None
        psT = [ctx.enter_context(nc.psum_tensor(f"{name}_psT{u}", [P, 4, P], F32)) for u in range(2)]
        ps_mean = None if route else ctx.enter_context(nc.psum_tensor("ps_column_sums", [P, D], F32))

        step = sem("vector_step")
        var_ready = sem("variance_ready")
        root_ready = sem("root_ready")
        rows_ready = sem("rows_normalised")
        transposed = sem("rows_transposed")
        cols_ready = sem("columns_copied")
        scored = sem("logits_done") if route else None
        stored = [sem(f"rows_stored{u}") for u in range(4)] if route else None
        block = ctx.enter_context(nc.Block(no_gpsimd_drain=True))

        @block.vector
        def _(dve):
            link = Chain(dve, step)
            if not route:
                dve.wait_ge(g.columns_summed, 1)
                nc.vector.scalar_tensor_tensor(g.W.out[:, 0:D], ps_mean[:, :], -1.0 / D, g.W.wo, ALU.mult, ALU.add).then_inc(g.weights_made, 1)

            def normalise(n):
                if n >= 4:
                    dve.wait_ge(transposed, n - 3)
                    if route:
                        dve.wait_ge(stored[n % 4], 16 * (n // 4))
                for j in range(4):
                    t = 4 * n + j
                    ins = nc.vector.tensor_scalar(rows[:, n % 4, j, :], g.x[:, t, :], w[:, 0, t:t + 1], w[:, 6, t:t + 1],
                                                  ALU.subtract, ALU.mult)
                ins.then_inc(rows_ready, 1)

            for part in range(PARTS):
                lo, hi = NTILE // PARTS * part, NTILE // PARTS * (part + 1)
                if attended and part == 0:
                    for t in range(lo, hi):
                        ins = nc.vector.scalar_tensor_tensor(g.x[:, t, :], g.projected[:, t, :], g.out_scale[:, 6, t:t + 1],
                                                             g.x[:, t, :], ALU.mult, ALU.add)
                    ins.then_inc(g.attended[0], 1)
                    dve.wait_ge(g.attended[0], 1)
                if attended and part == 1:
                    dve.wait_ge(g.attended[1], 2)
                if load is not None or attended:
                    for t in range(lo, hi):
                        if load is not None and t % (NTILE // 4) == 0:
                            dve.wait_ge(g.x_loaded[t // (NTILE // 4)], 16)
                        ins = nc.vector.bn_stats(stats[:, t, :], g.x[:, t, :])
                    ins.then_inc(g.measured, 1)
                    dve.wait_ge(g.measured, part + (7 if attended else 1))
                rsqrt_of_stats(nc, dve, link, stats[:, lo:hi, :], w[:, :, lo:hi], var_ready, root_ready, part + 1)
                for n in range(NG // PARTS * part, NG // PARTS * (part + 1)):
                    normalise(n)
            if load is not None:
                dve.wait_ge(g.consts_loaded, 2 * 16)
                dve.wait_ge(g.late_consts_loaded, 2 * 16)
                for src, dst in (("tri", g.tri), ("ones", g.ones)):
                    nc.vector.tensor_copy(dst[:, :], g.c(src)).then_inc(g.copied, 1)
                nc.vector.tensor_scalar(g.bias[:, :], g.bias[:, :], 0.5, None, ALU.mult).then_inc(g.copied, 1)
                dve.wait_ge(g.copied, 3)

        @block.tensor
        def _(pe):
            def transposes(n):
                pe.wait_ge(rows_ready, n + 1)
                if n >= 2:
                    pe.wait_ge(cols_ready, n - 1)
                for j in range(4):
                    ins = nc.tensor.transpose(psT[n % 2][:, j, :], rows[:, n % 4, j, :], g.c("ident"))
                ins.then_inc(transposed, 1)

            def logits(n):
                pe.wait_ge(cols_ready, n + 1)
                for j in range(4):
                    ins = nc.tensor.matmul(g.logits[:, 4 * n + j, :],
                                           cols[:, n % 2, j * P:(j + 1) * P], g.router[:, :], start=True, stop=True)
                ins.then_inc(scored, 1)

            if load is not None:
                pe.wait_ge(g.consts_loaded, 2 * 16)
            if not route:
                nc.tensor.matmul(ps_mean[:, :], g.c("ones"), g.W.wo, start=True, stop=True).then_inc(g.columns_summed, 1)
            for n in range(NG):
                transposes(n)
                if route and n >= 1:
                    logits(n - 1)
            if route:
                logits(NG - 1)

        if route:
            @block.gpsimd
            def _(pool):
                if attended:
                    half = slice(NTILE // 2, NTILE)
                    p = g.projected[:, half, :]
                    scale = g.out_scale[:, 6, half].rearrange("p (t o) -> p t o", o=1).broadcast_to([P, NTILE // 2, D])
                    nc.gpsimd.tensor_tensor(p, p, scale, ALU.mult).then_inc(g.attended[1], 1)
                    pool.wait_ge(g.attended[1], 1)
                    nc.gpsimd.tensor_tensor(g.x[:, half, :], g.x[:, half, :], p, ALU.add).then_inc(g.attended[1], 1)
                nc.gpsimd.memset(g.xe[:, :, :, :], 0.0).then_inc(g.zeroed, 1)

        @block.scalar
        def _(act):
            def roots(part):
                lo, hi = NTILE // PARTS * part, NTILE // PARTS * (part + 1)
                act.wait_ge(var_ready, part + 1)
                nc.scalar.activation(w[:, 4, lo:hi], w[:, 3, lo:hi], ACT.Sqrt).then_inc(root_ready, 1)
            roots(0)
            if load is not None:
                clear_expert_rows(g, act)
            for n in range(NG):
                if PARTS == 2 and n == (4 if attended else 2):
                    roots(1)
                act.wait_ge(transposed, n + 1)
                if route:
                    if n >= 2:
                        act.wait_ge(scored, n - 1)
                    dst = cols[:, n % 2, :]
                else:
                    dst = g.xnT[:, n, :]
                nc.scalar.activation(dst, psT[n % 2][:, :, :].rearrange("p j q -> p (j q)"), ACT.Copy).then_inc(cols_ready, 1)

        if route:
            @block.sync
            def _(sp):
                if load is not None:
                    load_inputs(nc, g, sp, *load)
                with sp.Fori(0, NG // 4) as i:
                    for u in range(4):
                        sp.wait_ge(rows_ready, 4 * i + u + 1)
                        sp.dma_start(g.xn_dram[bass.ds((4 * i + u) * 4, 4), :, :].rearrange("n p d -> p n d"),
                                     rows[:, u, :, :]).then_inc(stored[u], 16)
                for u in range(4):
                    sp.wait_ge(stored[u], 16 * (NG // 4))


class SlotList:
    CHUNKS = 4

    def __init__(self, nc, ctx, name):
        def sb(n, shape, dt=F32):
            return ctx.enter_context(nc.sbuf_tensor(f"{name}_{n}", shape, dt))
        self.hi = sb("hi", [P, RANKS, NTILE])
        self.lo = sb("lo", [P, RANKS, NTILE])
        self.low = sb("low_onehot", [P, RANKS, NTILE, P], BF16)
        self.high = sb("high_onehot", [P, RANKS, NTILE, 3, NBLK], BF16)
        self.found = sb("found", [P, RANKS, 3, NBLK])
        self.block_known = ctx.enter_context(nc.semaphore(f"{name}_block_onehots"))
        self.place_known = ctx.enter_context(nc.semaphore(f"{name}_place_onehots"))
        self.rows_scaled = ctx.enter_context(nc.semaphore(f"{name}_row_numbers"))
        self.listed = ctx.enter_context(nc.semaphore(f"{name}_slot_tokens"))
        self.step = ctx.enter_context(nc.semaphore(f"{name}_step"))
        self.indices_known = ctx.enter_context(nc.semaphore(f"{name}_indices"))

    def onehots(self, nc, g, dve, k):
        shape = [P, NTILE, NBLK]
        nc.vector.tensor_tensor(self.high[:, k, :, 0, :], g.c("tile").rearrange("p (o q) -> p o q", o=1).broadcast_to(shape),
                                self.hi[:, k].rearrange("p (t o) -> p t o", o=1).broadcast_to(shape),
                                ALU.is_equal).then_inc(self.block_known, 1)
        dve.wait_ge(self.block_known, k + 1)
        nc.vector.tensor_tensor(self.high[:, k, :, 1, :], self.high[:, k, :, 0, :],
                                g.c("tile").rearrange("p (t o) -> p t o", o=1).broadcast_to(shape), ALU.mult)
        n = NTILE // self.CHUNKS
        shape = [P, n, P]
        for c in range(self.CHUNKS):
            nc.vector.tensor_tensor(self.low[:, k, n * c:n * (c + 1)], g.c("iota").rearrange("p (o q) -> p o q", o=1).broadcast_to(shape),
                                    self.lo[:, k, n * c:n * (c + 1)].rearrange("p (t o) -> p t o", o=1).broadcast_to(shape),
                                    ALU.is_equal).then_inc(self.place_known, 1)

    def row_numbers(self, nc, g, act, k):
        act.wait_ge(self.block_known, k + 1)
        nc.scalar.activation(self.high[:, k, :, 2, :], self.high[:, k, :, 0, :], ACT.Copy, scale=g.c("part")).then_inc(self.rows_scaled, 1)

    def products(self, nc, pe, k, bank):
        pe.wait_ge(self.rows_scaled, k + 1)
        for t in range(NTILE):
            if t % (NTILE // self.CHUNKS) == 0:
                pe.wait_ge(self.place_known, self.CHUNKS * k + t * self.CHUNKS // NTILE + 1)
            ins = nc.tensor.matmul(bank, self.low[:, k, t, :], self.high[:, k, t, :, :].rearrange("p c h -> p (c h)"),
                                   start=(t == 0), stop=(t == NTILE - 1))
        ins.then_inc(self.listed, 1)

    def indices(self, nc, g, dve, k, bank):
        V, f = nc.vector, self.found
        dve.wait_ge(self.listed, k + 1)
        V.tensor_copy(f[:, k].rearrange("p c h -> p (c h)"), bank).then_inc(self.step, 1)
        dve.wait_ge(self.step, 3 * k + 1)
        V.scalar_tensor_tensor(f[:, k, 1], f[:, k, 1], float(P), f[:, k, 2], ALU.mult, ALU.add).then_inc(self.step, 1)
        dve.wait_ge(self.step, 3 * k + 2)
        V.scalar_tensor_tensor(f[:, k, 0], f[:, k, 0], -float(EMPTY), f[:, k, 1], ALU.mult, ALU.add).then_inc(self.step, 1)
        dve.wait_ge(self.step, 3 * k + 3)
        V.tensor_scalar(g.take[:, k * NBLK:(k + 1) * NBLK], f[:, k, 0], float(EMPTY), None, ALU.add)
        V.tensor_scalar(g.put[:, k * NBLK:(k + 1) * NBLK], f[:, k, 0], float(EMPTY + k * T), None,
                        ALU.add).then_inc(self.indices_known, 1)
        dve.wait_ge(self.indices_known, k + 1)


def route_phase(nc, g, name, L):
    with ExitStack() as ctx:
        def sb(n, shape, dt=F32):
            return ctx.enter_context(nc.sbuf_tensor(f"{name}_{n}", shape, dt))

        def ps(n, shape):
            return ctx.enter_context(nc.psum_tensor(f"{name}_{n}", shape, F32))

        def sem(n):
            return ctx.enter_context(nc.semaphore(f"{name}_{n}"))

        scores = sb("scores", [P, NTILE, E])
        work = sb("work", [P, NTILE, E])
        row = sb("row", [P, NTILE])
        best = sb("best", [P, RANKS, NTILE])
        choice = sb("choice", [P, RANKS, NTILE, E])
        choice_bf = sb("choice_bf", [P, RANKS, NTILE, E], BF16)
        before = sb("before", [P, RANKS, E, NTILE])
        place = sb("place", [P, RANKS, NTILE, E])
        pos = sb("pos", [P, RANKS, NTILE])
        hi, lo = L.hi, L.lo
        ps_rank = ps("ps_rank", [P, RANKS, NTILE, E])
        ps_total = ps("ps_total", [P, RANKS, NTILE, E])
        ps_found = ps("ps_found", [P, 3 * NBLK])

        step = sem("vector_step")
        shifted = sem("logits_shifted")
        raised = sem("exponentials_ready")
        chosen = sem("choices_ready")
        counted = sem("counts_ready")
        block = ctx.enter_context(nc.Block(no_gpsimd_drain=True))

        @block.vector
        def _(dve):
            V = nc.vector
            link = Chain(dve, step)
            each = [P, NTILE, E]

            def wide(a):
                return a.rearrange("p (t o) -> p t o", o=1).broadcast_to(each)

            def ramp(n):
                return g.c(n).rearrange("p (o e) -> p o e", o=1).broadcast_to(each)
            link(V.tensor_reduce(row[:, :], g.logits[:, :, :], AX, ALU.max))
            V.tensor_tensor(scores[:, :, :], g.logits[:, :, :], wide(row[:, :]), ALU.subtract).then_inc(shifted, 1)
            dve.wait_ge(raised, 1)
            link(V.tensor_reduce(row[:, :], work[:, :, :], AX, ALU.add))
            link(V.reciprocal(row[:, :], row[:, :]))
            link(V.tensor_tensor(scores[:, :, :], work[:, :, :], wide(row[:, :]), ALU.mult))
            for k in range(RANKS):
                link(V.tensor_reduce(best[:, k, :], scores[:, :, :], AX, ALU.max))
                link(V.tensor_tensor(work[:, :, :], scores[:, :, :], wide(best[:, k, :]), ALU.is_equal))
                link(V.tensor_tensor(work[:, :, :], work[:, :, :], ramp("tieorder"), ALU.mult))
                link(V.tensor_reduce(row[:, :], work[:, :, :], AX, ALU.max))
                link(V.tensor_tensor(choice[:, k], work[:, :, :], wide(row[:, :]), ALU.is_equal))
                if k == 0:
                    link(V.scalar_tensor_tensor(scores[:, :, :], choice[:, k], -4.0, scores[:, :, :], ALU.mult, ALU.add))
            V.tensor_copy(choice_bf[:, :, :, :], choice[:, :, :, :]).then_inc(chosen, 1)
            V.memset(before[:, :, :, 0:1], 0.0)
            dve.wait_ge(counted, 1)
            for k in range(RANKS):
                ins = V.tensor_copy(before[:, k, :, 1:NTILE], ps_total[:, k, 0:NTILE - 1, :].rearrange("p t e -> p e t"))
            link(ins)
            flat = before[:, :, :, :].rearrange("p k e t -> p (k e t)")
            link(V.tensor_tensor_scan(flat, g.c("segment"), flat, 0.0, ALU.mult, ALU.add))
            for k in range(RANKS):
                ins = V.tensor_tensor(place[:, k], ps_rank[:, k], before[:, k].rearrange("p e t -> p t e"), ALU.add)
            link(ins)
            link(V.tensor_tensor(place[:, :, :, :], place[:, :, :, :], choice[:, :, :, :], ALU.mult))
            link(V.tensor_reduce(pos[:, :, :], place[:, :, :, :], AX, ALU.add))
            for k in range(RANKS):
                ins = V.tensor_tensor(place[:, k], choice[:, k], ramp("expert"), ALU.mult)
            link(ins)
            link(V.tensor_reduce(hi[:, :, :], place[:, :, :, :], AX, ALU.add))
            link(V.tensor_scalar(lo[:, :, :], pos[:, :, :], float(CAP), 0.5, ALU.is_lt, ALU.mult))
            link(V.tensor_tensor(g.weight[:, :, :], best[:, :, :], lo[:, :, :], ALU.mult))
            link(V.tensor_scalar(lo[:, :, :], pos[:, :, :], float(P), None, ALU.is_ge))
            for m in range(2, NJ):
                link(V.scalar_tensor_tensor(lo[:, :, :], pos[:, :, :], float(m * P), lo[:, :, :], ALU.is_ge, ALU.add))
            link(V.scalar_tensor_tensor(hi[:, :, :], hi[:, :, :], float(NJ), lo[:, :, :], ALU.mult, ALU.add))
            link(V.scalar_tensor_tensor(lo[:, :, :], lo[:, :, :], -float(P), pos[:, :, :], ALU.mult, ALU.add))
            L.onehots(nc, g, dve, 0)
            L.indices(nc, g, dve, 0, ps_found[:, :])

        @block.scalar
        def _(act):
            act.wait_ge(shifted, 1)
            nc.scalar.activation(work[:, :, :], scores[:, :, :], ACT.Exp).then_inc(raised, 1)
            L.row_numbers(nc, g, act, 0)

        @block.tensor
        def _(pe):
            pe.wait_ge(chosen, 1)
            c = choice_bf[:, :, :, :].rearrange("p k t e -> p (k t e)")
            nc.tensor.matmul(ps_rank[:, :, :, :].rearrange("p k t e -> p (k t e)"), g.tri[:, :], c, start=True, stop=True)
            nc.tensor.matmul(ps_total[:, :, :, :].rearrange("p k t e -> p (k t e)"), g.ones[:, :], c,
                             start=True, stop=True).then_inc(counted, 1)
            L.products(nc, pe, 0, ps_found[:, :])


class Run:

    def __init__(self, base, m):
        self.base, self.m = base, m

    def exists(self):
        return self.m is not None or 0 <= self.base < NRUN

    def at(self, offset=0, scale=1):
        v = scale * (self.base + offset)
        return v if self.m is None else self.m * (4 * scale) + v

    def uses(self, buffers, scale=1):
        v = scale * (self.base // buffers)
        return v if self.m is None else self.m * (4 // buffers * scale) + v


def expert_phase(nc, g, name, w1, w2, L, out=None, weights=None):
    with ExitStack() as ctx:
        def sb(n, shape, dt=F32):
            return ctx.enter_context(nc.sbuf_tensor(f"{name}_{n}", shape, dt))

        def ps(n, shape):
            return ctx.enter_context(nc.psum_tensor(f"{name}_{n}", shape, F32))

        def sem(n):
            return ctx.enter_context(nc.semaphore(f"{name}_{n}"))

        w1s = sb("w1", [P, 4, FF])
        w2s = sb("w2", [P, 4, NF, D])
        xT = sb("xT", [P, 2, CAP])
        hT = sb("hT", [P, 2, NF, CAP])
        y = sb("y", [P, 2, NJ, D])
        take = sb("take_now", [P, 4, NJ], U32)
        put = sb("put_now", [P, 2, NJ], U32)
        rows = sb("combined_rows", [P, NTILE, D])
        ps_in = [ps(f"ps_in{u}", [P, CAP]) for u in range(2)]
        ps_h = [ps(f"ps_h{f}", [P, CAP]) for f in range(NF)]
        ps_y = [ps(f"ps_y{u}", [P, NJ, D]) for u in range(2)]

        w_loaded = [sem(f"weights_loaded{u}") for u in range(4)]
        gathered = [sem(f"rows_gathered{u}") for u in range(4)]
        scattered = [sem(f"rows_scattered{u}") for u in range(2)]
        take_ready = sem("gather_indices_ready")
        put_ready = sem("scatter_indices_ready")
        in_done = sem("rows_transposed")
        xT_ready = sem("xT_ready")
        up_done = sem("up_done")
        h_ready = sem("h_ready")
        down_done = sem("down_done")
        y_ready = sem("y_ready")
        returned = [sem(f"rank_rows_loaded{q}") for q in range(4)]
        added = sem("bias_and_rank0_added")
        summed = sem("group_summed")
        pool_scaled = sem("pool_tiles_scaled")
        pool_summed = sem("pool_tiles_summed")
        stored = sem("group_stored")
        block = ctx.enter_context(nc.Block())
        QT = NTILE // 4
        POOL_TILES = 2
        ps_found = ps_y[1][:, 0, 0:3 * NBLK]

        def wait(eng, s, value):
            if not (isinstance(value, int) and value <= 0):
                eng.wait_ge(s, value)

        def steps(eng, emit):
            def at(i, m=None):
                return lambda ahead: Run(i + ahead, m)
            for i in range(-2, 3):
                emit(i, at(i))
            with eng.Fori(0, 2) as m:
                for i in range(3, 7):
                    emit(None, at(i, m))
            for i in range(11, NRUN + 1):
                emit(i, at(i))

        def rank_rows(eng, k, q):
            eng.dma_start(rows[:, QT * q:QT * (q + 1), :],
                          g.y_dram[k * T + QT * q * P:k * T + QT * (q + 1) * P, :].rearrange("(n p) d -> p n d", p=P)
                          ).then_inc(returned[q], 16)

        @block.sync
        def _(sp):
            def load(r, u, first):
                e = r % E if isinstance(r, int) else r & (E - 1)
                if not first:
                    sp.wait_ge(down_done, r - 3)
                    sp.sem_inc(g.passed, 1)
                sp.dma_start(w1s[:, u, :], w1[bass.ds(e, 1), :, :].rearrange("o c f -> c (o f)")).then_inc(w_loaded[u], 16)
                sp.dma_start(w2s[:, u, :, :], w2[bass.ds(e, 1), :, :].rearrange("o (b f) c -> f (o b) c", b=NF)).then_inc(w_loaded[u], 16)

            for r in range(4):
                load(r, r, True)
            if weights is not None:
                load_attention_weights(g, sp, *weights)
            with sp.Fori(1, 3) as m:
                for u in range(4):
                    load(4 * m + u, u, False)
            for r in range(12, NRUN):
                load(r, r % 4, False)
            sp.wait_ge(added, 8)
            for u in range(2):
                sp.wait_ge(scattered[u], NRUN // 2 * NJ * 16)
            for q in range(4):
                rank_rows(sp, 1, q)
            if out is not None:
                for q in range(4):
                    sp.wait_ge(summed, q + 1)
                    sp.wait_ge(pool_summed, q + 1)
                    sp.dma_start(out[QT * q:QT * (q + 1), :, :].rearrange("n p d -> p n d"),
                                 g.x[:, QT * q:QT * (q + 1), :]).then_inc(stored, 16)
                sp.wait_ge(stored, 16 * 4)

        AHEAD = 5

        @block.gpsimd
        def _(pool):
            def gather(r):
                u = r.base % 4
                pool.wait_ge(take_ready, r.at(1))
                pool.sem_inc(g.passed, 1)
                for j in range(NJ):
                    nc.gpsimd.indirect_dma_start(out=g.xe[:, u, j, :], out_offset=None, in_=g.xn_rows,
                                                 in_offset=bass.IndirectOffsetOnAxis(ap=take[:, u, j:j + 1], axis=0),
                                                 bounds_check=T - 1, oob_is_err=False).then_inc(gathered[u], 16)

            def scatter(r):
                u = r.base % 2
                pool.wait_ge(put_ready, r.at(1))
                pool.wait_ge(y_ready, r.at(1))
                pool.sem_inc(g.passed, 1)
                for j in range(NJ):
                    nc.gpsimd.indirect_dma_start(out=g.y_dram, out_offset=bass.IndirectOffsetOnAxis(ap=put[:, u, j:j + 1], axis=0),
                                                 in_=y[:, u, j, :], in_offset=None,
                                                 bounds_check=RANKS * T - 1, oob_is_err=False).then_inc(scattered[u], 16)

            def emit(i, run):
                if run(AHEAD).exists():
                    gather(run(AHEAD))
                if run(-1).exists():
                    scatter(run(-1))
            pool.wait_ge(g.cleared, 8 * 16)
            pool.wait_ge(g.zeroed, 1 if weights is not None else 2)
            for r in range(AHEAD - 2):
                gather(Run(r, None))
            steps(pool, emit)
            for u in range(2):
                pool.wait_ge(scattered[u], NRUN // 2 * NJ * 16)
            for q in range(4):
                pool.wait_ge(returned[q], 32)
                pool.wait_ge(added, q + 5)
                some = slice(QT * (q + 1) - POOL_TILES, QT * (q + 1))
                scale = g.weight[:, 1, some].rearrange("p (t o) -> p t o", o=1).broadcast_to([P, POOL_TILES, D])
                nc.gpsimd.tensor_tensor(rows[:, some, :], rows[:, some, :], scale, ALU.mult).then_inc(pool_scaled, 1)
                pool.wait_ge(pool_scaled, q + 1)
                nc.gpsimd.tensor_tensor(g.x[:, some, :], g.x[:, some, :], rows[:, some, :], ALU.add).then_inc(pool_summed, 1)

        @block.tensor
        def _(pe):
            def transpose_in(r):
                u = r.base % 2
                pe.wait_ge(gathered[r.base % 4], r.uses(4, NJ * 16) + NJ * 16)
                wait(pe, xT_ready, r.at(-1))
                for j in range(NJ):
                    ins = nc.tensor.transpose(ps_in[u][:, j * P:(j + 1) * P], g.xe[:, r.base % 4, j, :], g.c("ident"))
                ins.then_inc(in_done, 1)

            def up(r):
                u = r.base % 2
                pe.wait_ge(w_loaded[r.base % 4], r.uses(4, 32) + 32)
                pe.wait_ge(xT_ready, r.at(1))
                for f in range(NF):
                    if r.m is not None or r.base > 0:
                        pe.wait_ge(h_ready, r.at(-1, NF) + f + 1)
                    nc.tensor.matmul(ps_h[f][:, :], w1s[:, r.base % 4, f * P:(f + 1) * P], xT[:, u, :],
                                     start=True, stop=True).then_inc(up_done, 1)

            def down(r):
                u = r.base % 2
                wait(pe, y_ready, r.at(-1))
                pe.wait_ge(h_ready, r.at(1, NF))
                for j in range(NJ):
                    for f in range(NF):
                        ins = nc.tensor.matmul(ps_y[u][:, j, :], hT[:, u, f, j * P:(j + 1) * P], w2s[:, r.base % 4, f, :],
                                               start=(f == 0), stop=(f == NF - 1))
                ins.then_inc(down_done, 1)

            def emit(i, run):
                if run(2).exists():
                    transpose_in(run(2))
                if run(1).exists():
                    up(run(1))
                if run(0).exists():
                    down(run(0))
            L.products(nc, pe, 1, ps_found)
            steps(pe, emit)

        @block.scalar
        def _(act):
            def emit(i, run):
                if i == 11:
                    for u in range(2):
                        act.wait_ge(scattered[u], E // 2 * NJ * 16)
                if i is not None and 11 <= i <= 14:
                    rank_rows(act, 0, i - 11)
                r = run(1)
                if not r.exists():
                    return
                for f in range(NF):
                    act.wait_ge(up_done, r.at(0, NF) + f + 1)
                    if f == 0:
                        wait(act, down_done, r.at(-1))
                    nc.scalar.activation(hT[:, r.base % 2, f, :], ps_h[f][:, :], ACT.Gelu_apprx_tanh).then_inc(h_ready, 1)
            L.row_numbers(nc, g, act, 1)
            steps(act, emit)

        @block.vector
        def _(dve):
            def weighted(k, q):
                dve.wait_ge(returned[q], 16 * (k + 1))
                if k == 1:
                    dve.wait_ge(added, q + 5)
                for t in range(QT * q, QT * (q + 1) - (POOL_TILES if k else 0)):
                    ins = nc.vector.scalar_tensor_tensor(g.x[:, t, :], rows[:, t, :], g.weight[:, k, t:t + 1],
                                                         g.x[:, t, :], ALU.mult, ALU.add)
                ins.then_inc(added if k == 0 else summed, 1)

            def statistics(q):
                dve.wait_ge(summed, q + 1)
                for t in range(QT * q, QT * (q + 1)):
                    if t == QT * (q + 1) - POOL_TILES:
                        dve.wait_ge(pool_summed, q + 1)
                    ins = nc.vector.bn_stats(g.stats[:, t, :], g.x[:, t, :])
                ins.then_inc(g.measured, 1)

            def take_indices(r):
                wait(dve, in_done, r.at(-3))
                nc.vector.tensor_copy(take[:, r.base % 4, :], g.take[:, bass.ds(r.at(0, NJ), NJ)]).then_inc(take_ready, 1)

            def emit(i, run):
                if run(AHEAD).exists():
                    take_indices(run(AHEAD))
                if run(2).exists():
                    r = run(2)
                    dve.wait_ge(in_done, r.at(1))
                    wait(dve, up_done, r.at(-1, NF))
                    nc.vector.tensor_copy(xT[:, r.base % 2, :], ps_in[r.base % 2][:, :]).then_inc(xT_ready, 1)
                if run(0).exists():
                    r = run(0)
                    u = r.base % 2
                    dve.wait_ge(down_done, r.at(1))
                    wait(dve, scattered[u], r.uses(2, NJ * 16))
                    nc.vector.tensor_copy(put[:, u, :], g.put[:, bass.ds(r.at(0, NJ), NJ)]).then_inc(put_ready, 1)
                    nc.vector.tensor_copy(y[:, u, :, :], ps_y[u][:, :, :]).then_inc(y_ready, 1)
                if i is not None and i <= 1:
                    xq = g.x[:, QT * (i + 2):QT * (i + 3), :]
                    nc.vector.tensor_tensor(xq, xq, g.bias[:, :].rearrange("p (o d) -> p o d", o=1).broadcast_to([P, QT, D]),
                                            ALU.add).then_inc(added, 1)
                if i == 2 and weights is not None:
                    spread_attention_weights(nc, g, dve)
                if i is not None and 13 <= i <= 16:
                    dve.wait_ge(added, 4)
                    weighted(0, i - 13)
            for r in range(AHEAD - 2):
                take_indices(Run(r, None))
            if weights is not None:
                nc.vector.memset(g.W.f2, 0.0).then_inc(g.padding_zeroed, 1)
                nc.vector.memset(g.W.og2, 0.0).then_inc(g.padding_zeroed, 1)
            L.onehots(nc, g, dve, 1)
            L.indices(nc, g, dve, 1, ps_found)
            steps(dve, emit)
            for q in range(4):
                weighted(1, q)
                if q and weights is not None:
                    statistics(q - 1)
            dve.wait_ge(summed, 4)
            if weights is not None:
                statistics(3)
                dve.wait_ge(g.measured, 6)


def ffn(nc, g, name, w1, w2, out=None, load=None, weights=None, attended=False):
    with ExitStack() as ctx:
        g.xe = ctx.enter_context(nc.sbuf_tensor(f"{name}_expert_rows", [P, 4, NJ, D], F32))
        L = SlotList(nc, ctx, f"{name}_list")
        with ExitStack() as inner:
            g.logits = inner.enter_context(nc.psum_tensor(f"{name}_logits", [P, NTILE, E], F32))
            norm_phase(nc, g, f"{name}_norm", True, load, attended)
            route_phase(nc, g, f"{name}_route", L)
        expert_phase(nc, g, f"{name}_experts", w1, w2, L, out, weights)


C = 4
BT = 64
NBK = NT // BT
NCH = BT // C
GR = NB * NCH


def attention_core(nc, g, W):
    with ExitStack() as ctx:
        def sb(n, shape, dt=F32):
            return ctx.enter_context(nc.sbuf_tensor(f"att_{n}", shape, dt))

        def ps(n, shape):
            return ctx.enter_context(nc.psum_tensor(f"att_{n}", shape, F32))

        def sem(n):
            return ctx.enter_context(nc.semaphore(f"att_{n}"))

        blk, two = [P, GR, C], [P, 2, GR, C]
        z16 = sb("low_rank", [16, 2, NB * BT])
        sg, kraw, k2 = (sb(n, blk) for n in ("sig_gamma", "k_raw", "k_square_or_norm"))
        kinv = k2
        k, f, q, a = (sb(n, two) for n in ("k", "forget", "q", "a"))
        kds = [None] + [sb(f"k_decayed{d}", [P, GR, C - d]) for d in range(1, C)]
        pa = [None] + [sb(f"a_k{d}", [P, GR, C - d]) for d in range(1, C)]
        pb = [sb(f"q_k{d}", [P, GR, C - d]) for d in range(C)]
        A = sb("A", [P, GR, C * C])
        B = sb("B", [P, GR, C * C])
        tmp = sb("solve_term", [P, 2, GR, C - 1])
        tmp2 = sb("output_term", [P, 2, GR, C - 1])
        XY = sb("XY", [P, 2, 2, GR, C])
        ZO = sb("ZO", [P, 2, 2, GR, C])
        Xm = sb("X_masked", [P, 2, HD, NB * BT])
        Kbar = sb("K_bar", two)
        decay = sb("decay", two)
        gate = sb("out_gate", two)
        hist = sb("states", [P, 2, NCH, HD, NB])
        Es = sb("Y_S", [P, 2, HD, NB, C])
        R = sb("K_u", [P, HD, NB, C + 1])
        E2 = sb("Z_S", [P, 2, HD, NB, 4 * C])
        p1 = [ps(f"ps_stage1_{n}", [P, NB * BT]) for n in range(2)]
        p2 = [ps(f"ps_stage2_{n}", [P, NB * BT]) for n in range(2)]
        pc = [ps(f"ps_u{n}", [P, HD, NB, 2 * C]) for n in range(2)]
        po = ps("ps_o", [P, NB, BT])

        pass1 = sem("stage1_passes")
        act1 = sem("stage1_read_by_scalar")
        sig_done = sem("sigmoids_of_k_and_q")
        dve1 = sem("stage1_read_by_vector")
        k2_ready = sem("k_square_ready")
        norm_step = sem("norm_step")
        k_ready = sem("k_and_a_ready")
        pass2 = sem("stage2_passes")
        act2 = sem("stage2_read_by_scalar")
        pool_step = sem("pool_step")
        pa_ready = sem("a_k_products_ready")
        pb_ready = sem("q_k_products_ready")
        decay_begun = sem("decay_begun")
        Y_ready = sem("Y_start_ready")
        Kbar_ready = sem("K_bar_ready")
        solve_step = sem("solve_step")
        solved = sem("X_Y_solved")
        masked = sem("X_masked_ready")
        ZO_ready = sem("Z_O_ready")
        spread = sem("X_in_bank")
        E_ready = sem("Y_S_ready")
        u_ready = sem("u_ready")
        R_ready = sem("K_u_ready")
        state = sem("states_ready")
        E2_ready = sem("Z_S_ready")
        o_done = sem("o_collected")
        o_read = sem("o_read")
        o_ready = sem("o_gated")
        zero = sem("state_zeroed")
        block = ctx.enter_context(nc.Block(no_gpsimd_drain=True))

        def flat(t):
            return t.rearrange("p a b -> p (a b)")

        def wait(eng, s, value):
            if not (isinstance(value, int) and value <= 0):
                eng.wait_ge(s, value)

        def bodies(eng, emit):
            emit(-2, 0, False, False, True)
            emit(-1, 1, False, True, True)
            emit(0, 0, True, True, True)
            with eng.Fori(0, 2) as m:
                emit(2 * m + 1, 1, True, True, True)
                emit(2 * m + 2, 0, True, True, True)
            emit(5, 1, True, True, True)
            emit(6, 0, True, True, False)
            emit(7, 1, True, False, False)

        @block.tensor
        def _(pe):
            hs = g.c("headsum")

            def mm(out, w, x, start=True):
                return nc.tensor.matmul(out, w, x, start=start, stop=True, skip_group_check=not start)

            def cols(j):
                return g.xnT[:, :, bass.ds(BT * j, BT)]

            def stage1(j, u, n):
                if n in (1, 2):
                    wait(pe, dve1, 2 * j + n - 1)
                else:
                    wait(pe, act1, 4 * j + {0: 0, 3: 1, 4: 2, 5: 3}[n])
                if n == 3:
                    pe.sem_inc(g.passed, 1)
                bank = p1[1 if n == 1 else 0]
                if n == 5:
                    ins = mm(bank[:, :], W.f2, z16[:, u, :])
                elif n == 2:
                    pe.wait_ge(k2_ready, j + 1)
                    ins = mm(bank[:, :], hs, flat(k2[:, :, :]))
                else:
                    w, m = {0: (W.k, P), 1: (W.q, P), 3: (W.low, 16), 4: (W.gamma, P)}[n]
                    ins = mm(bank[0:m, :].rearrange("p (b t) -> p b t", b=NB), w, cols(j))
                ins.then_inc(pass1, 1)

            def stage2(j, u, n):
                wait(pe, act2, 7 * j + {0: -2, 1: 0, 6: 6}.get(n, n - 1))
                bank = p2[1 if n == 6 else n % 2]
                if n == 0:
                    ins = mm(bank[:, :].rearrange("p (b t) -> p b t", b=NB), W.v, cols(j))
                elif n == 1:
                    pe.wait_ge(pa_ready, j + 1)
                    mm(bank[:, 0:3 * GR], hs, flat(pa[1][:, :, :]))
                    ins = mm(bank[:, 3 * GR:4 * GR], hs, flat(pa[3][:, :, :]))
                elif n == 2:
                    ins = mm(bank[:, 0:2 * GR], hs, flat(pa[2][:, :, :]))
                elif n == 3:
                    pe.wait_ge(pb_ready, j + 1)
                    ins = mm(bank[:, 0:2 * GR], hs, flat(pb[2][:, :, :]))
                elif n == 4:
                    ins = mm(bank[:, :], hs, flat(pb[0][:, :, :]))
                elif n == 5:
                    mm(bank[:, 0:3 * GR], hs, flat(pb[1][:, :, :]))
                    ins = mm(bank[:, 3 * GR:4 * GR], hs, flat(pb[3][:, :, :]))
                else:
                    ins = mm(bank[:, :], W.og2, z16[:, u, :])
                ins.then_inc(pass2, 1)

            def put_X(i, u, n):
                wait(pe, R_ready, NCH * i + 2 * n - 2)
                if n == 0:
                    pe.wait_ge(masked, i + 1)
                x = Xm[:, u, :, :].rearrange("p v (b t) -> p (v b) t", b=NB)[:, :, 2 * C * n:2 * C * (n + 1)]
                mm(pc[n % 2][:, :, :, :].rearrange("p v b t -> p (v b) t"), hs, x).then_inc(spread, 1)

            def add_YS(i, c):
                pe.wait_ge(E_ready, NCH * i + c + 1)
                h = c % 2
                out = pc[(c // 2) % 2][:, :, :, C * h:C * h + C].rearrange("p v b t -> p (v b) t")
                mm(out, hs, Es[:, c % 2].rearrange("p v b t -> p (v b) t"), start=False).then_inc(u_ready, 1)

            def collect(i, s):
                pe.wait_ge(E2_ready, 4 * i + s + 1)
                if s == 0:
                    wait(pe, o_read, i)
                for v in range(HD):
                    lo = COL["collect"][0] + v * P
                    ins = mm(po[:, :, 4 * C * s:4 * C * (s + 1)], g.const[:, lo:lo + P], E2[:, s % 2, v], start=(v == 0))
                ins.then_inc(o_done, 1)

            STAGE1 = {1: (0,), 4: (1,), 5: (2,), 8: (3,), 11: (4,), 13: (5,)}
            STAGE2 = {3: (1, 2), 6: (3, 4), 7: (5,), 14: (6,)}
            NEXT_X = {1: 1, 3: 2, 5: 3, 7: 4, 9: 5, 11: 6, 13: 7}

            def emit(i, u, chain, s2, s1):
                if chain:
                    put_X(i, u, 0)
                for c in range(NCH):
                    if chain:
                        add_YS(i, c)
                        if c in (0, 2) and not (isinstance(i, int) and i == 0):
                            collect(i - 1, 2 + c // 2)
                        if c in (10, 12):
                            collect(i, (c - 10) // 2)
                    if s1:
                        for n in STAGE1.get(c, ()):
                            stage1(i + 2, u, n)
                    if s2:
                        for n in STAGE2.get(c, ()):
                            stage2(i + 1, 1 - u, n)
                    if chain and c in NEXT_X:
                        put_X(i, u, NEXT_X[c])
                    if s1 and c == NCH - 1:
                        stage2(i + 2, u, 0)
            bodies(pe, emit)
            collect(NBK - 1, 2)
            collect(NBK - 1, 3)

        @block.scalar
        def _(act):
            S = nc.scalar

            def sigmoid(out, j, n, inc):
                act.wait_ge(pass1, 6 * j + n + 1)
                S.activation(out, p1[1 if n == 1 else 0][:, :], ACT.Sigmoid).then_inc(inc, 1)

            def spread_out(dst, bank, lo, d):
                n = C - d
                src = bank[:, lo:lo + n * GR].rearrange("p (g t) -> p g t", g=GR)
                last = d + (n - 1) * (C + 1) + 1
                return S.activation(dst[:, :, d:last:C + 1], src, ACT.Copy)

            def emit(i, u, chain, s2, s1):
                j, v = i + 1, 1 - u
                b = i + 2
                if s2:
                    act.wait_ge(pass2, 7 * j + 1)
                    wait(act, ZO_ready, j - 1)
                    S.activation(flat(XY[:, v, 1]), p2[0][:, :], ACT.Copy).then_inc(act2, 1)
                    wait(act, state, NCH * (j - 1))
                    act.wait_ge(act1, 4 * j + 4)
                    S.activation(decay[:, v, :, 0:1], f[:, v, :, 0:1], ACT.Copy).then_inc(decay_begun, 1)
                if s1:
                    wait(act, k_ready, b)
                    sigmoid(flat(kraw[:, :, :]), b, 0, sig_done)
                    act.wait_ge(dve1, 2 * b + 1)
                    S.activation(flat(k2[:, :, :]), flat(kraw[:, :, :]), ACT.Square).then_inc(k2_ready, 1)
                if s2:
                    act.wait_ge(pass2, 7 * j + 2)
                    wait(act, solved, j)
                    spread_out(A, p2[1], 0, 1)
                    spread_out(A, p2[1], 3 * GR, 3).then_inc(act2, 1)
                    act.wait_ge(pass2, 7 * j + 3)
                    spread_out(A, p2[0], 0, 2).then_inc(act2, 1)
                    for s in range(C):
                        kd = k[:, v] if s == C - 1 else kds[C - 1 - s]
                        last = S.activation(Kbar[:, v, :, s:s + 1], kd[:, :, s:s + 1], ACT.Copy)
                    last.then_inc(Kbar_ready, 1)
                if s1:
                    wait(act, ZO_ready, b - 1)
                    sigmoid(flat(q[:, u]), b, 1, sig_done)
                    act.wait_ge(pass1, 6 * b + 3)
                    S.activation(flat(kinv[:, :, :]), p1[0][:, :], ACT.Sqrt).then_inc(act1, 1)
                if s2:
                    act.wait_ge(pass2, 7 * j + 4)
                    wait(act, ZO_ready, j)
                    spread_out(B, p2[1], 0, 2).then_inc(act2, 1)
                    act.wait_ge(pass2, 7 * j + 5)
                    spread_out(B, p2[0], 0, 0).then_inc(act2, 1)
                    act.wait_ge(pass2, 7 * j + 6)
                    spread_out(B, p2[1], 0, 1)
                    spread_out(B, p2[1], 3 * GR, 3).then_inc(act2, 1)
                if s1:
                    act.wait_ge(pass1, 6 * b + 4)
                    S.activation(z16[:, u, :], p1[0][0:16, :], ACT.Copy).then_inc(act1, 1)
                def gamma_and_f():
                    sigmoid(flat(sg[:, :, :]), b, 4, act1)
                    wait(act, Y_ready, b - 1)
                    sigmoid(flat(f[:, u]), b, 5, act1)
                if s1 and not chain:
                    gamma_and_f()
                if s2:
                    act.wait_ge(solved, j + 1)
                    wait(act, spread, (j - 1) * (NCH // 2))
                    for n in range(HD):
                        last = S.activation(Xm[:, v, n, :], flat(XY[:, v, 1]), ACT.Copy, scale=g.c("delta")[:, n:n + 1])
                    last.then_inc(masked, 1)
                if s1 and chain:
                    gamma_and_f()
                if s2:
                    act.wait_ge(pass2, 7 * j + 7)
                    wait(act, o_ready, j - 1)
                    S.activation(flat(gate[:, v]), p2[1][:, :], ACT.Sigmoid).then_inc(act2, 1)
            bodies(act, emit)

        @block.gpsimd
        def _(pool):
            G = nc.gpsimd
            link = Chain(pool, pool_step)
            STEPS = 13

            def products_a(j, u):
                link.begin(STEPS * j)
                pool.wait_ge(k_ready, j + 1)
                wait(pool, pass2, 7 * j - 1)
                wait(pool, Kbar_ready, j)
                kd = [k[:, u]] + [t[:, :, :] for t in kds[1:]]
                for d in range(1, C):
                    link(G.tensor_tensor(kd[d], kd[d - 1][:, :, 0:C - d], f[:, u, :, d:C], ALU.mult))
                for d in range(1, C):
                    last = G.tensor_tensor(pa[d][:, :, :], a[:, u, :, d:C], kd[d], ALU.mult)
                last.then_inc(pa_ready, 1)
                pool.wait_ge(decay_begun, j + 1)
                for t in range(1, C):
                    link(G.tensor_tensor(decay[:, u, :, t:t + 1], decay[:, u, :, t - 1:t], f[:, u, :, t:t + 1], ALU.mult))
                G.tensor_tensor(XY[:, u, 0], a[:, u], decay[:, u], ALU.mult).then_inc(Y_ready, 1)

            def products_b(j, u):
                kd = [k[:, u]] + [t[:, :, :] for t in kds[1:]]
                pool.wait_ge(dve1, 2 * j + 2)
                for d in range(C):
                    last = G.tensor_tensor(pb[d][:, :, :], q[:, u, :, d:C], kd[d], ALU.mult)
                last.then_inc(pb_ready, 1)

            def outputs(j, u):
                pool.wait_ge(pb_ready, j + 1)
                pool.wait_ge(Y_ready, j + 1)
                link(G.tensor_tensor(q[:, u], q[:, u], decay[:, u], ALU.mult))
                pool.wait_ge(solved, j + 1)
                pool.wait_ge(act2, 7 * j + 6)
                wait(pool, o_read, j - 1)
                for s in range(C):
                    n = C - s
                    b4 = B[:, :, :].rearrange("p g (s t) -> p g s t", s=C)[:, :, s, s:C]
                    for h in range(2):
                        x = XY[:, u, h, :, s:s + 1].broadcast_to([P, GR, n])
                        last = G.tensor_tensor((ZO[:, u, h] if s == 0 else tmp2[:, h, :, 0:n]), x, b4, ALU.mult)
                    if s:
                        link(last)
                        last = G.tensor_tensor(ZO[:, u, :, :, s:C], ZO[:, u, :, :, s:C], tmp2[:, :, :, 0:n], ALU.add)
                    if s < C - 1 and s:
                        link(last)
                link(last)
                G.tensor_tensor(ZO[:, u, 0], ZO[:, u, 0], q[:, u], ALU.add).then_inc(ZO_ready, 1)

            def z_state(i, u, s):
                if s == 0:
                    pool.wait_ge(ZO_ready, i + 1)
                wait(pool, o_done, 4 * i + s - 1)
                for c in range(4 * s, 4 * s + 4):
                    wait(pool, state, NCH * i + c)
                    z = ZO[:, u, 0].rearrange("p (b n) t -> p b n t", b=NB)[:, :, c, :]
                    z = z.rearrange("p (o b) t -> p o b t", o=1).broadcast_to([P, HD, NB, C])
                    st = hist[:, u, c].rearrange("p v (b o) -> p v b o", o=1).broadcast_to([P, HD, NB, C])
                    last = G.tensor_tensor(E2[:, s % 2, :, :, C * (c % 4):C * (c % 4 + 1)], z, st, ALU.mult)
                last.then_inc(E2_ready, 1)

            def emit(i, u, chain, s2, s1):
                if chain and not (isinstance(i, int) and i == 0):
                    z_state(i - 1, 1 - u, 3)
                if s2:
                    products_a(i + 1, 1 - u)
                    products_b(i + 1, 1 - u)
                if chain:
                    z_state(i, u, 0)
                    z_state(i, u, 1)
                if s2:
                    outputs(i + 1, 1 - u)
                if chain:
                    z_state(i, u, 2)
            pool.wait_ge(zero, 1)
            bodies(pool, emit)
            z_state(NBK - 1, 1, 3)

        @block.vector
        def _(dve):
            V = nc.vector

            def as3(bank):
                return bank[:, :].rearrange("p (g t) -> p g t", t=C)

            def k_product(j):
                dve.wait_ge(sig_done, 2 * j + 1)
                V.tensor_tensor(kraw[:, :, :], as3(p1[0]), kraw[:, :, :], ALU.mult).then_inc(dve1, 1)

            def q_product(j, u):
                dve.wait_ge(sig_done, 2 * j + 2)
                V.tensor_tensor(q[:, u], as3(p1[1]), q[:, u], ALU.mult).then_inc(dve1, 1)

            def k_norm(j, u, part):
                if part == 0:
                    dve.wait_ge(act1, 4 * j + 1)
                    V.tensor_scalar(kinv[:, :, :], kinv[:, :, :], 1e-12, None, ALU.max).then_inc(norm_step, 1)
                elif part <= 4:
                    dve.wait_ge(norm_step, 7 * j + 1)
                    n = GR // 4
                    x = kinv[:, n * (part - 1):n * part, :]
                    V.reciprocal(x, x).then_inc(norm_step, 1)
                else:
                    wait(dve, pb_ready, j - 1)
                    wait(dve, Kbar_ready, j - 1)
                    dve.wait_ge(norm_step, 7 * j + 5)
                    V.tensor_tensor(k[:, u], kraw[:, :, :], kinv[:, :, :], ALU.mult).then_inc(norm_step, 1)

            def make_a(j, u, part):
                if part == 0:
                    dve.wait_ge(norm_step, 7 * j + 6)
                    dve.wait_ge(act1, 4 * j + 4)
                    V.scalar_tensor_tensor(a[:, u], k[:, u], -1.0, sg[:, :, :], ALU.mult, ALU.mult).then_inc(norm_step, 1)
                else:
                    dve.wait_ge(norm_step, 7 * j + 7)
                    V.tensor_tensor(a[:, u], a[:, u], f[:, u], ALU.mult).then_inc(k_ready, 1)

            def solve(j, u, s, part):
                n = C - 1 - s
                if part == 0:
                    if s == 0:
                        dve.wait_ge(act2, 7 * j + 3)
                        dve.wait_ge(Y_ready, j + 1)
                    else:
                        dve.wait_ge(solve_step, 5 * j + 2 * s)
                    a4 = A[:, :, :].rearrange("p g (s t) -> p g s t", s=C)[:, :, s, s + 1:C]
                    for h in range(2):
                        x = XY[:, u, h, :, s:s + 1].broadcast_to([P, GR, n])
                        ins = V.tensor_tensor(tmp[:, h, :, 0:n], x, a4, ALU.mult)
                    ins.then_inc(solve_step, 1)
                else:
                    dve.wait_ge(solve_step, 5 * j + 2 * s + 1)
                    ins = V.tensor_tensor(XY[:, u, :, :, s + 1:C], XY[:, u, :, :, s + 1:C], tmp[:, :, :, 0:n], ALU.add)
                    ins.then_inc(solve_step if s < C - 2 else solved, 1)

            def chunk_parts(i, u, c):
                S4 = hist[:, u, c].rearrange("p v (b o) -> p v b o", o=1)

                def part(t):
                    t = t.rearrange("p (b n) t -> p b n t", b=NB)[:, :, c, :]
                    return t.rearrange("p (o b) t -> p o b t", o=1)
                return [P, HD, NB, C], S4, part

            def chunk_start(i, u, c):
                each, S4, part = chunk_parts(i, u, c)
                if c == 0:
                    dve.wait_ge(solved, i + 1)
                    dve.wait_ge(Kbar_ready, i + 1)
                wait(dve, state, NCH * i + c)
                V.tensor_tensor(Es[:, c % 2], part(XY[:, u, 0]).broadcast_to(each), S4.broadcast_to(each), ALU.mult).then_inc(E_ready, 1)
                V.tensor_tensor(R[:, :, :, C:C + 1], part(decay[:, u])[:, :, :, C - 1:C].broadcast_to([P, HD, NB, 1]), S4, ALU.mult)

            def chunk_end(i, u, c):
                each, S4, part = chunk_parts(i, u, c)
                dve.wait_ge(u_ready, NCH * i + c + 1)
                V.tensor_tensor(R[:, :, :, 0:C], pc[(c // 2) % 2][:, :, :, C * (c % 2):C * (c % 2) + C],
                                part(Kbar[:, u]).broadcast_to(each), ALU.mult).then_inc(R_ready, 1)
                dve.wait_ge(R_ready, NCH * i + c + 1)
                if c < NCH - 1:
                    dst = hist[:, u, c + 1]
                else:
                    dst = hist[:, 1 - u, 0]
                    wait(dve, E2_ready, 4 * i)
                V.tensor_reduce(dst, R[:, :, :, :], AX, ALU.add).then_inc(state, 1)

            def add_O(i, u):
                dve.wait_ge(o_done, 4 * i + 4)
                V.tensor_tensor(g.oT[:, :, bass.ds(BT * i, BT)], po[:, :, :],
                                ZO[:, u, 1].rearrange("p (b n) t -> p b (n t)", b=NB), ALU.add).then_inc(o_read, 1)

            def gate_o(i, u):
                dve.wait_ge(o_read, i + 1)
                dve.wait_ge(act2, 7 * i + 7)
                out = g.oT[:, :, bass.ds(BT * i, BT)]
                V.tensor_tensor(out, out, gate[:, u].rearrange("p (b n) t -> p b (n t)", b=NB), ALU.mult).then_inc(o_ready, 1)

            def emit(i, u, chain, s2, s1):
                for c in range(NCH):
                    if chain:
                        chunk_start(i, u, c)
                    if s2 and c == 0:
                        make_a(i + 1, 1 - u, 1)
                    if s2 and c == 1:
                        q_product(i + 1, 1 - u)
                    if s1 and c == 2:
                        k_product(i + 2)
                    if chain and c == 3 and not (isinstance(i, int) and i == 0):
                        add_O(i - 1, 1 - u)
                    if s2 and 4 <= c <= 7:
                        solve(i + 1, 1 - u, (c - 4) // 2, (c - 4) % 2)
                    if s2 and c == 8:
                        solve(i + 1, 1 - u, 2, 0)
                        solve(i + 1, 1 - u, 2, 1)
                    if chain and c == 9 and not (isinstance(i, int) and i == 0):
                        gate_o(i - 1, 1 - u)
                    if s1 and 9 <= c <= 14:
                        k_norm(i + 2, u, c - 9)
                    if s1 and c == 15:
                        make_a(i + 2, u, 0)
                    if chain:
                        chunk_end(i, u, c)

            V.memset(hist[:, 0, 0], 0.0).then_inc(zero, 1)
            dve.wait_ge(zero, 1)
            bodies(dve, emit)
            add_O(NBK - 1, 1)
            gate_o(NBK - 1, 1)
            dve.wait_ge(o_ready, NBK)


def rsqrt_of_stats(nc, dve, link, stats, w, var_ready, root_ready, times=1):
    V = nc.vector
    mean, dmean, m2, var, root, quot, scale = (w[:, i, :] for i in range(7))
    a = [stats[:, :, k] for k in range(6)]
    V.tensor_tensor(mean, a[1], a[4], ALU.add)
    V.tensor_tensor(dmean, a[1], a[4], ALU.subtract)
    link(V.tensor_tensor(m2, a[2], a[5], ALU.add))
    link(V.tensor_tensor(dmean, dmean, dmean, ALU.mult))
    link(V.tensor_scalar(dmean, dmean, 0.25, 1e-5, ALU.mult, ALU.add))
    V.tensor_scalar(mean, mean, 0.5, None, ALU.mult)
    V.scalar_tensor_tensor(var, m2, 1.0 / D, dmean, ALU.mult, ALU.add).then_inc(var_ready, 1)
    dve.wait_ge(root_ready, times)
    link(V.reciprocal(quot, root))
    link(V.tensor_tensor(quot, quot, var, ALU.mult))
    link(V.tensor_tensor(root, root, quot, ALU.add))
    link(V.reciprocal(scale, root))
    link(V.tensor_scalar(scale, scale, 2.0, None, ALU.mult))


def load_attention_weights(g, sp, Wq, Wk, Wv, Wgamma, Wf1, Wf2, Wog1, Wog2, norm_w, Wo):
    W = g.W
    for dst, src in ((W.q, Wq), (W.k, Wk), (W.v, Wv), (W.gamma_small, Wgamma), (W.low[:, 0:HD], Wf1),
                     (W.low[:, HD:2 * HD], Wog1), (W.wo, Wo), (W.norm, norm_w.rearrange("(p o) -> p o", o=1))):
        sp.dma_start(dst, src[:, :]).then_inc(g.weights_loaded, 16)
    sp.wait_ge(g.padding_zeroed, 2)
    sp.dma_start(W.f2[0:HD, :], Wf2[:, :]).then_inc(g.weights_loaded, 16)
    sp.dma_start(W.og2[HD:2 * HD, :], Wog2[:, :]).then_inc(g.weights_loaded, 16)


def spread_attention_weights(nc, g, dve):
    W, V = g.W, nc.vector
    dve.wait_ge(g.weights_loaded, 10 * 16)
    V.tensor_copy(W.gamma.rearrange("p (h c) -> p h c", h=H),
                  W.gamma_small.rearrange("p (h o) -> p h o", o=1).broadcast_to([P, H, HD])).then_inc(g.weights_made, 1)
    V.tensor_scalar(W.wo, W.wo, W.norm, None, ALU.mult).then_inc(g.weights_made, 1)
    V.tensor_copy(W.out[:, D:2 * D], g.c("ident")).then_inc(g.weights_made, 1)
    dve.wait_ge(g.weights_made, 3)


def attention_output(nc, g, W):
    with ExitStack() as ctx:
        def sb(n, shape, dt=F32):
            return ctx.enter_context(nc.sbuf_tensor(f"attout_{n}", shape, dt))

        def sem(n):
            return ctx.enter_context(nc.semaphore(f"attout_{n}"))
        stage = sb("stage", [P, 4, 4 * P])
        proj = g.projected
        stats = sb("stats", [P, NTILE, 6])
        w = g.out_scale
        ps = [ctx.enter_context(nc.psum_tensor(f"attout_ps{n}", [P, 4, 2 * D], F32)) for n in range(4)]
        staged = sem("staged")
        multiplied = sem("projected")
        kept = sem("projection_kept")
        measured = sem("statistics_taken")
        step = sem("vector_step")
        var_ready = sem("variance_ready")
        root_ready = sem("root_ready")
        block = ctx.enter_context(nc.Block(no_gpsimd_drain=True))

        @block.scalar
        def _(act):
            def stage_in(n):
                if n >= 4:
                    act.wait_ge(multiplied, n - 3)
                nc.scalar.activation(stage[:, n % 4, :], g.oT[:, n, :], ACT.Copy).then_inc(staged, 1)
            for n in range(4):
                stage_in(n)
            for n in range(NG):
                act.wait_ge(measured, n + 1)
                act.wait_ge(staged, n + 1)
                nc.scalar.activation(proj[:, 4 * n:4 * n + 4, :], ps[n % 4][:, :, 0:D], ACT.Copy).then_inc(kept, 1)
                if n + 4 < NG:
                    stage_in(n + 4)
            act.wait_ge(var_ready, 1)
            nc.scalar.activation(w[:, 4, :], w[:, 3, :], ACT.Sqrt).then_inc(root_ready, 1)

        @block.tensor
        def _(pe):
            for n in range(NG):
                pe.wait_ge(staged, n + 1)
                if n >= 4:
                    pe.wait_ge(kept, n - 3)
                for j in range(4):
                    ins = nc.tensor.matmul(ps[n % 4][:, j, :], stage[:, n % 4, j * P:(j + 1) * P], W.out, start=True, stop=True)
                ins.then_inc(multiplied, 1)

        @block.vector
        def _(dve):
            link = Chain(dve, step)
            for n in range(NG):
                dve.wait_ge(multiplied, n + 1)
                for j in range(4):
                    ins = nc.vector.bn_stats(stats[:, 4 * n + j, :], ps[n % 4][:, j, D:2 * D])
                ins.then_inc(measured, 1)
            dve.wait_ge(measured, NG)
            rsqrt_of_stats(nc, dve, link, stats, w, var_ready, root_ready)


def attention(nc, g):
    with ExitStack() as ctx:
        g.xnT = ctx.enter_context(nc.sbuf_tensor("attention_xnT", [P, NB, NT], F32))
        norm_phase(nc, g, "att_norm", False)
        attention_core(nc, g, g.W)
    attention_output(nc, g, g.W)


def macaron_kernel(nc, x, Wq, Wk, Wv, Wgamma, Wf1, Wf2, Wog1, Wog2, norm_w, Wo, router_w, w1, w2, bias, consts, out):
    g = Shared()
    with ExitStack() as ctx:
        def sb(n, shape, dt=F32):
            return ctx.enter_context(nc.sbuf_tensor(n, shape, dt))
        g.x = sb("x_tokens", [P, NTILE, D])
        g.const = sb("constants", [P, NCONST])
        g.c = lambda n: g.const[:, COL[n][0]:COL[n][1]]
        g.tri = sb("tri_bf", [P, P], BF16)
        g.ones = sb("ones_bf", [P, P], BF16)
        g.router = sb("router", [P, E])
        g.bias = sb("half_bias", [P, D])
        g.stats = sb("statistics", [P, NTILE, 6])
        g.oT = sb("gated_outputs", [P, NB, NT])
        g.projected = g.oT[:, :, :].rearrange("p n (j d) -> p (n j) d", d=D)
        g.out_scale = sb("output_statistics", [P, 8, NTILE])
        W = g.W = Shared()
        W.q, W.k, W.v, W.gamma, W.wo = (sb(f"weight_{n}", [P, D])[:, :] for n in ("q", "k", "v", "gamma", "out_weighted"))
        W.gamma_small, W.norm = sb("weight_gamma_small", [P, H])[:, :], sb("weight_norm", [P, 1])[:, :]
        W.low = sb("weight_low", [P, 2 * HD])[:, :]
        W.f2, W.og2 = (sb(f"weight_{n}", [2 * HD, D])[:, :] for n in ("f2", "og2"))
        W.out = sb("weight_out", [P, 2 * D])[:, :]
        g.weight = sb("rank_weight", [P, RANKS, NTILE])
        g.take = sb("take_rows", [P, RANKS * NBLK], U32)
        g.put = sb("put_rows", [P, RANKS * NBLK], U32)
        g.router_in, g.bias_in = router_w, bias
        xn = nc.dram_tensor("normalised_rows", [NTILE, P, D], F32, kind="Internal").ap()
        g.xn_dram = xn
        g.xn_rows = xn.rearrange("n p d -> (n p) d")
        g.y_dram = nc.dram_tensor("expert_outputs", [RANKS * T, D], F32, kind="Internal").ap()
        out_tiles = out.rearrange("b (n p) d -> (b n) p d", p=P)

        def sem(n):
            return ctx.enter_context(nc.semaphore(n))
        g.x_loaded = [sem(f"x_loaded{q}") for q in range(4)]
        g.consts_loaded = sem("constants_loaded")
        g.late_consts_loaded = sem("late_constants_loaded")
        g.copied = sem("small_constants_made")
        g.measured = sem("x_measured")
        g.attended = [sem(f"attention_added{h}") for h in range(2)]
        g.padding_zeroed = sem("padding_zeroed")
        g.weights_loaded = sem("attention_weights_loaded")
        g.weights_made = sem("attention_weights_made")
        g.columns_summed = sem("output_weight_columns_summed")
        weights = (Wq, Wk, Wv, Wgamma, Wf1, Wf2, Wog1, Wog2, norm_w, Wo)
        g.passed = sem("waits_passed")
        g.zeroed = sem("zero_tile_made")
        g.cleared = sem("expert_rows_cleared")

        ffn(nc, g, "first", w1, w2, load=(x.rearrange("b t d -> (b t) d"), consts), weights=weights)
        attention(nc, g)
        ffn(nc, g, "second", w1, w2, out_tiles, attended=True)


_INS = ["L0_attn_x", "L0_attn_Wq", "L0_attn_Wk", "L0_attn_Wv", "L0_attn_Wgamma", "L0_attn_Wf1", "L0_attn_Wf2",
        "L0_attn_Wog1", "L0_attn_Wog2", "L0_attn_norm_w", "L0_attn_Wo", "L0_ffn_router_w", "L0_ffn_w1", "L0_ffn_w2",
        "L0_ffn_bias"]


def kernel(**inputs):
    import concourse.bacc as _bacc
    from concourse.bass_utils import run_bass_kernel_spmd as _run

    nc = _bacc.Bacc("TRN2", target_bir_lowering=False, num_devices=1)
    arrays, args = {}, []
    for name in _INS:
        a = np.ascontiguousarray(inputs[name])
        arrays[f"in_{name}"] = a
        args.append(nc.dram_tensor(f"in_{name}", a.shape, mybir.dt.from_np(a.dtype), kind="ExternalInput").ap())
    arrays["in_constants"] = constant_table()
    args.append(nc.dram_tensor("in_constants", (P, NCONST), F32, kind="ExternalInput").ap())
    args.append(nc.dram_tensor("out_tokens", (NB, NT, D), F32, kind="ExternalOutput").ap())
    macaron_kernel(nc, *args)
    r = _run(nc, [arrays], core_ids=[0])
    return r.results[0]["out_tokens"]
```
